# Optimizing a Trainium2 kernel written in Bass

```python
import numpy as np
import jax
import jax.numpy as jnp

def _softmax(x, axis=-1):
    return jax.nn.softmax(x, axis=axis)

def _gelu(x):
    return jax.nn.gelu(x, approximate=True)

def _silu(x):
    return jax.nn.silu(x)

def _sigmoid(x):
    return jax.nn.sigmoid(x)

def _layernorm(x, axis=-1, eps=1e-05):
    m = jnp.mean(x, axis=axis, keepdims=True)
    v = jnp.var(x, axis=axis, keepdims=True)
    return (x - m) / jnp.sqrt(v + eps)

def _scatter_add(tgt, idx, src, axis=0):
    return tgt.at[idx].add(src)

def _segment_sum(src, seg, n):
    return jax.ops.segment_sum(src, seg, n)
kernel_name = 'mk_gnn_preln_d2_gnn_r64_ae661d'

def setup_inputs(seed: int=0):
    np.random.seed(seed)
    _w = jnp.asarray

    def _rec_inputs():
        import jax
        import jax.numpy as jnp
        _gk = jax.random.key(seed)
        x = -0.000202 + 1 * jax.random.normal(jax.random.fold_in(_gk, 1), (100000, 128), jnp.float32)
        src = jax.random.randint(jax.random.fold_in(_gk, 2), (25000,), 0, 100000, jnp.int32)
        dst = jax.random.randint(jax.random.fold_in(_gk, 3), (25000,), 0, 100000, jnp.int32)
        _o = jnp.argsort(dst, stable=True)
        src = src[_o]
        dst = dst[_o]
        edge_attr_128 = -8.513e-05 + 0.999844 * jax.random.normal(jax.random.fold_in(_gk, 12), (25000, 128), jnp.float32)
        return (x, src, dst, edge_attr_128)
    x, src, dst, edge_attr_128 = _rec_inputs()

    def _L0_gnn_setup():
        import jax, jax.numpy as jnp
        import numpy as np
        N_NODES = 50000
        N_EDGES = 12500
        IN_DIM = 128
        OUT_DIM = 128
        HEADS = 4
        HEAD_DIM = OUT_DIM // HEADS
        NEG_SLOPE = 0.2
        LN_EPS = 1e-05
        key = jax.random.key(seed)
        ks = jax.random.split(key, 8)
        x = jax.random.normal(ks[0], (N_NODES, IN_DIM), dtype=jnp.float32)
        edge_index = jax.random.randint(ks[1], (2, N_EDGES), 0, N_NODES, dtype=jnp.int64)
        W = jax.random.normal(ks[2], (IN_DIM, HEADS * HEAD_DIM), dtype=jnp.float32) / np.sqrt(IN_DIM)
        att_src = jax.random.normal(ks[3], (HEADS, HEAD_DIM), dtype=jnp.float32) / np.sqrt(HEAD_DIM)
        att_dst = jax.random.normal(ks[4], (HEADS, HEAD_DIM), dtype=jnp.float32) / np.sqrt(HEAD_DIM)
        bias = jnp.zeros((OUT_DIM,), dtype=jnp.float32)
        gamma = jnp.ones((OUT_DIM,), dtype=jnp.float32)
        beta = jnp.zeros((OUT_DIM,), dtype=jnp.float32)
        return {'x': x, 'edge_index': edge_index, 'W': W, 'att_src': att_src, 'att_dst': att_dst, 'bias': bias, 'gamma': gamma, 'beta': beta}
    _L0_gnn_all = _L0_gnn_setup()
    _L0_gnn_in = {k: v for k, v in _L0_gnn_all.items() if k in ('W', 'att_src', 'att_dst', 'bias', 'gamma', 'beta')}
    del _L0_gnn_all

    def _L1_gnn_setup():
        import jax, jax.numpy as jnp
        import numpy as np
        N_NODES, N_EDGES, HIDDEN, HOPS = (20000, 10000, 128, 3)
        LEAKY_ALPHA = 0.2

        def _segment_softmax(scores, seg, num_segments):
            m = jax.ops.segment_max(scores, seg, num_segments)
            ex = jnp.exp(scores - m[seg])
            denom = jax.ops.segment_sum(ex, seg, num_segments)
            return ex / denom[seg]
        key = jax.random.key(seed)
        ks = jax.random.split(key, 9)
        s = 1.0 / np.sqrt(HIDDEN)
        return {'node_feat': jax.random.normal(ks[0], (N_NODES, HIDDEN), jnp.float32), 'edge_feat': jax.random.normal(ks[1], (N_EDGES, HIDDEN), jnp.float32), 'senders': jax.random.randint(ks[2], (N_EDGES,), 0, N_NODES), 'receivers': jax.random.randint(ks[3], (N_EDGES,), 0, N_NODES), 'Wq': jax.random.normal(ks[4], (HOPS, HIDDEN, HIDDEN), jnp.float32) * s, 'bq': jnp.zeros((HOPS, HIDDEN), jnp.float32), 'Wn': jax.random.normal(ks[5], (HOPS, HIDDEN, HIDDEN), jnp.float32) * s, 'bn': jnp.zeros((HOPS, HIDDEN), jnp.float32), 'We': jax.random.normal(ks[6], (HOPS, HIDDEN, HIDDEN), jnp.float32) * s, 'be': jnp.zeros((HOPS, HIDDEN), jnp.float32), 'attn': jax.random.normal(ks[7], (HOPS, HIDDEN), jnp.float32) * s}
    _L1_gnn_all = _L1_gnn_setup()
    _L1_gnn_in = {k: v for k, v in _L1_gnn_all.items() if k in ('Wq', 'bq', 'Wn', 'bn', 'We', 'be', 'attn')}
    del _L1_gnn_all
    return {'x': x, 'src': src, 'dst': dst, 'edge_attr_128': edge_attr_128, 'L0_gnn_W': _L0_gnn_in['W'], 'L0_gnn_att_src': _L0_gnn_in['att_src'], 'L0_gnn_att_dst': _L0_gnn_in['att_dst'], 'L0_gnn_bias': _L0_gnn_in['bias'], 'L0_gnn_gamma': _L0_gnn_in['gamma'], 'L0_gnn_beta': _L0_gnn_in['beta'], 'L1_gnn_Wq': _L1_gnn_in['Wq'], 'L1_gnn_bq': _L1_gnn_in['bq'], 'L1_gnn_Wn': _L1_gnn_in['Wn'], 'L1_gnn_bn': _L1_gnn_in['bn'], 'L1_gnn_We': _L1_gnn_in['We'], 'L1_gnn_be': _L1_gnn_in['be'], 'L1_gnn_attn': _L1_gnn_in['attn']}

def reference(x, src, dst, edge_attr_128, L0_gnn_W, L0_gnn_att_src, L0_gnn_att_dst, L0_gnn_bias, L0_gnn_gamma, L0_gnn_beta, L1_gnn_Wq, L1_gnn_bq, L1_gnn_Wn, L1_gnn_bn, L1_gnn_We, L1_gnn_be, L1_gnn_attn):
    import jax
    import jax.numpy as jnp

    def _L0_gnn_ref(x, edge_index, W, att_src, att_dst, bias, gamma, beta):
        import jax, jax.numpy as jnp
        import numpy as np
        N_NODES = 50000
        N_EDGES = 12500
        IN_DIM = 128
        OUT_DIM = 128
        HEADS = 4
        HEAD_DIM = OUT_DIM // HEADS
        NEG_SLOPE = 0.2
        LN_EPS = 1e-05
        N = x.shape[0]
        loop = jnp.arange(N, dtype=edge_index.dtype)
        src = jnp.concatenate([edge_index[0], loop])
        dst = jnp.concatenate([edge_index[1], loop])
        h = (x @ W).reshape(N, HEADS, HEAD_DIM)
        a_s = jnp.einsum('nhd,hd->nh', h, att_src)
        a_d = jnp.einsum('nhd,hd->nh', h, att_dst)
        e = jax.nn.leaky_relu(a_s[src] + a_d[dst], NEG_SLOPE)
        e_max = jax.ops.segment_max(e, dst, num_segments=N)
        e_exp = jnp.exp(e - e_max[dst])
        denom = jax.ops.segment_sum(e_exp, dst, num_segments=N)
        alpha = e_exp / (denom[dst] + 1e-16)
        msg = h[src] * alpha[..., None]
        out = jax.ops.segment_sum(msg, dst, num_segments=N)
        out = out.reshape(N, HEADS * HEAD_DIM) + bias
        mu = out.mean(-1, keepdims=True)
        var = ((out - mu) ** 2).mean(-1, keepdims=True)
        out = (out - mu) * jax.lax.rsqrt(var + LN_EPS) * gamma + beta
        return jax.nn.gelu(out, approximate=False)

    def _L1_gnn_ref(node_feat, edge_feat, senders, receivers, Wq, bq, Wn, bn, We, be, attn):
        import jax, jax.numpy as jnp
        import numpy as np
        N_NODES, N_EDGES, HIDDEN, HOPS = (20000, 10000, 128, 3)
        LEAKY_ALPHA = 0.2

        def _segment_softmax(scores, seg, num_segments):
            m = jax.ops.segment_max(scores, seg, num_segments)
            ex = jnp.exp(scores - m[seg])
            denom = jax.ops.segment_sum(ex, seg, num_segments)
            return ex / denom[seg]
        n = node_feat.shape[0]
        h = node_feat
        for i in range(Wq.shape[0]):
            q = h @ Wq[i] + bq[i]
            v = (h @ Wn[i] + bn[i])[senders] + (edge_feat @ We[i] + be[i])
            feats = jax.nn.leaky_relu(q[receivers] + v, LEAKY_ALPHA)
            score = feats @ attn[i]
            alpha = _segment_softmax(score, receivers, n)
            pooled = jax.ops.segment_sum(alpha[:, None] * v, receivers, n)
            h = jax.nn.relu(pooled)
        return h
    edge_index = jnp.stack([src, dst])
    h = jnp.maximum(_layernorm(x, axis=-1), 0.0)
    x = x + _L0_gnn_ref(h, edge_index, L0_gnn_W, L0_gnn_att_src, L0_gnn_att_dst, L0_gnn_bias, L0_gnn_gamma, L0_gnn_beta)
    h = jnp.maximum(_layernorm(x, axis=-1), 0.0)
    x = x + _L1_gnn_ref(h, edge_attr_128, src, dst, L1_gnn_Wq, L1_gnn_bq, L1_gnn_Wn, L1_gnn_bn, L1_gnn_We, L1_gnn_be, L1_gnn_attn)
    return x

_drawn_inputs = setup_inputs


def setup_inputs(seed=0):
    import zlib

    import numpy as np

    out = dict(_drawn_inputs(seed))
    spreads = {'L0_gnn_bias': (0.0, 0.1),
     'L0_gnn_gamma': (1.0, 0.2),
     'L0_gnn_beta': (0.0, 0.1),
     'L1_gnn_bq': (0.0, 0.8),
     'L1_gnn_bn': (0.0, 0.282),
     'L1_gnn_be': (0.0, 0.288)}
    factors = {'L0_gnn_att_dst': 4.305, 'L1_gnn_Wq': 7.626}
    for name, (base, spread) in spreads.items():
        noise = np.random.default_rng([zlib.crc32(name.encode()), seed]).standard_normal(out[name].shape)
        drawn = base * np.exp(spread * noise) if base else spread * noise
        out[name] = jnp.asarray(drawn.astype(out[name].dtype))
    for name, factor in factors.items():
        out[name] = (out[name] * factor).astype(out[name].dtype)
    return out
```

```python
from contextlib import ExitStack

import numpy as np
import concourse.bass as bass
from concourse import mybir

P = 128
D = 128
N = 100000
E = 25000
HEADS = 4
HOPS = 3
TILE_GROUP = 4
CHUNK = TILE_GROUP * P
CHUNKS = 2 * -(-E // (2 * CHUNK))
E_PAD = CHUNKS * CHUNK
TILES = E_PAD // P
HALVES = 2
LINES = TILES // HALVES
ROWS = 4
BLOCK = P * ROWS
BLOCKS = -(-N // BLOCK)
LAST_BLOCK_PARTS = (N - (BLOCKS - 1) * BLOCK) // ROWS
NODE_RING = 4
EPS = 1e-5
NONE = -1e30
SKIP = 1 << 20
SLOPE = 0.2
RSQRT_SEED = float(0x5F3759DF)
assert (N - (BLOCKS - 1) * BLOCK) % ROWS == 0 and BLOCKS % NODE_RING == 0


def visits(eng, first, total, ring, visit):
    turns = (total - first) // ring
    with eng.Fori(0, turns) as j:
        for u in range(first, first + ring):
            visit(j * ring + u, u % ring, j + u // ring)
    for n in range(first + turns * ring, total):
        visit(n, n % ring, n // ring)


def build(nc, x, src_tiles, dst_tiles, next_tiles, edge_ids, dst_lines, prev_lines, next_lines, edge_attr,
          W, att, bias, gamma, beta, Wq, Wn, We, bq, bn, be, attn, ident_in, sel_in, out):
    f32 = mybir.dt.float32
    i32 = mybir.dt.int32
    ALU = mybir.AluOpType
    ACT = mybir.ActivationFunctionType
    AX = mybir.AxisListType
    ctx = ExitStack()
    with ctx:
        def sb(name, shape, dt=f32):
            return ctx.enter_context(nc.sbuf_tensor(name, shape, dt))

        def sem(name):
            return ctx.enter_context(nc.semaphore(name))

        def sems(name, n):
            return [sem(f"{name}{i}") for i in range(n)]

        pos_table = nc.dram_tensor("pos_table", (N, 1), i32).ap()
        xd_rows = nc.dram_tensor("xd_rows", (E_PAD, D), f32).ap()
        hd_feat = nc.dram_tensor("hd_feat", (P, E_PAD), f32).ap()
        x1_rows = nc.dram_tensor("x1_rows", (E_PAD, D), f32).ap()
        h_tables = [nc.dram_tensor("h1_table", (2 * E_PAD, D), f32).ap(),
                    nc.dram_tensor("h2_table", (E_PAD + P, D), f32).ap(),
                    nc.dram_tensor("h3_table", (E_PAD + P, D), f32).ap()]

        def chunked(rows):
            return rows.rearrange("(c t p) d -> c p t d", t=TILE_GROUP, p=P)

        xd_chunks, x1_chunks = chunked(xd_rows), chunked(x1_rows)
        h_chunks = [chunked(h_tables[0][0:E_PAD, :])] + [chunked(t[0:E_PAD, :]) for t in h_tables[1:]]
        own_chunks = chunked(h_tables[0][E_PAD:2 * E_PAD, :])
        hd_chunks = hd_feat.rearrange("f (c e) -> c f e", e=CHUNK)

        ident = sb("ident", [P, P])
        sel = sb("sel", [4 * HEADS, 4, P])
        w_sb = sb("w_sb", [P, D])
        wT = sb("wT", [P, D])
        att_sb = sb("att_sb", [P, 2 * HEADS])
        w_att = sb("w_att", [P, 4 * HEADS])
        wq_sb = sb("wq_sb", [P, HOPS, D])
        wn_sb = sb("wn_sb", [P, HOPS, D])
        we_sb = sb("we_sb", [P, HOPS, D])
        bq_sb = sb("bq_sb", [P, HOPS])
        bn_sb = sb("bn_sb", [P, HOPS])
        be_sb = sb("be_sb", [P, HOPS])
        v_bias = sb("v_bias", [P, HOPS])
        attn_sb = sb("attn_sb", [P, HOPS])
        bias_bc = sb("bias_bc", [P, D])
        gamma_bc = sb("gamma_bc", [P, D])
        beta_bc = sb("beta_bc", [P, D])
        src_i = sb("src_i", [P, TILES], i32)
        dst_i = sb("dst_i", [P, TILES], i32)
        next_i = sb("next_i", [P, TILES], i32)
        edge_i = sb("edge_i", [P, TILES], i32)
        recv_i = sb("recv_i", [P, TILES], i32)
        put_i = sb("put_i", [P, TILES], i32)
        pos_i = sb("pos_i", [P, TILES], i32)
        hop1_i = next_i
        last_t = sb("last_t", [P, TILES])
        inner_t = sb("inner_t", [P, TILES])
        dst_l = sb("dst_l", [LINES, HALVES, P], i32)
        prev_l = sb("prev_l", [LINES, HALVES, P], i32)
        next_l = sb("next_l", [LINES, HALVES, P], i32)
        same_l = sb("same_l", [LINES, HALVES, P])
        pen_l = sb("pen_l", [LINES, HALVES, P])
        last_l = sb("last_l", [LINES, HALVES, P])
        whole_l = sb("whole_l", [LINES, HALVES])
        V = sb("V", [P, E_PAD])
        scores = sb("scores", [P, TILES, 2 * HEADS])
        coef = sb("coef", [P, TILES, 4 * HEADS])
        ring_a = [sb(f"ring_a{r}", [P, TILE_GROUP, D]) for r in range(2)]
        ring_b = [sb(f"ring_b{r}", [P, TILE_GROUP, D]) for r in range(2)]
        idx_a = [sb(f"idx_a{r}", [P, TILE_GROUP], i32) for r in range(2)]
        idx_b = [sb(f"idx_b{r}", [P, TILE_GROUP], i32) for r in range(2)]
        pos_in = [sb(f"pos_in{r}", [P, TILE_GROUP], i32) for r in range(2)]
        xn = sb("xn", [P, 2 * TILE_GROUP, D])
        aT = sb("aT", [P, CHUNK])
        bT = sb("bT", [P, CHUNK])
        hd_out = [sb(f"hd_out{r}", [P, CHUNK]) for r in range(2)]
        y_sb = sb("y_sb", [P, TILE_GROUP, D])
        x1_sb = [sb(f"x1_sb{r}", [P, TILE_GROUP, D]) for r in range(2)]
        h_sb = [sb(f"h_sb{r}", [P, TILE_GROUP, D]) for r in range(2)]
        hn_sb = sb("hn_sb", [P, TILE_GROUP, D])
        coef_st = [sb(f"coef_st{r}", [P, TILE_GROUP, 4 * HEADS]) for r in range(2)]
        coefT = sb("coefT", [4 * HEADS, CHUNK])
        pv = sb("pv", [P, CHUNK])
        run_pair = sb("run_pair", [P, 2, CHUNK])
        run_sum = [run_pair[:, r, :] for r in range(2)]
        o_pair = sb("o_pair", [P, 2, CHUNK])
        o_sb = [o_pair[:, r, :] for r in range(2)]
        tz_pair = sb("tz_pair", [P, 2, CHUNK])
        t_sb, z_sb = tz_pair[:, 0, :], tz_pair[:, 1, :]
        stats = sb("stats", [P, 2 * TILE_GROUP, 6])
        mv = sb("mv", [P, 2 * TILE_GROUP, 2])
        var_e = sb("var_e", [P, 2 * TILE_GROUP])
        rstd = sb("rstd", [P, 2 * TILE_GROUP])
        nwt = sb("nwt", [P, 2 * TILE_GROUP])
        KH = HEADS * HALVES
        node_all = sb("node_all", [P, NODE_RING, ROWS, D])
        node_out = sb("node_out", [P, 2, ROWS * D])
        SL = node_all[:].rearrange("p r t d -> p (r t) d")[0:LINES]
        def lines_in(pair):
            return pair.rearrange("p a b -> p (a b)")[0:LINES, :].rearrange("l (k e) -> l k e", e=P)
        ML = lines_in(xn[:, :, :])
        AL = lines_in(tz_pair[:, :, :])
        PL = lines_in(o_pair[:, :, :])
        DL = lines_in(node_out[:, :, :])
        C1 = lines_in(run_pair[:, :, :])
        C2 = SL[:, KH:2 * KH, :]
        carry_l = sb("carry_l", [LINES, HALVES * HEADS])
        row_f, row_w = pv[0:HEADS, 0:TILES], pv[0:HEADS, TILES:2 * TILES]
        row_a, row_pen = coefT[0:HEADS, 0:TILES], coefT[0:HEADS, TILES:2 * TILES]
        opened = aT[0:HEADS, 0:TILES + 1]
        node_x = [node_all[:, r] for r in range(NODE_RING)]
        node_y = [node_out[:, r, :].rearrange("p (t d) -> p t d", d=D) for r in range(2)]

        bank = [ctx.enter_context(nc.psum_tensor(f"bank{i}", [P, 512], f32)) for i in range(8)]

        def tile_of(b, t):
            return bank[b][:, t * P:(t + 1) * P]

        def rows_of(b):
            return bank[b][:, :].rearrange("p (t d) -> p t d", t=TILE_GROUP)

        loaded = sem("loaded")
        att_zero, att_loaded = sem("att_zero"), sem("att_loaded")
        wT_done, wT_copied, watt_done = sem("wT_done"), sem("wT_copied"), sem("watt_done")
        weights_ready, index_ready = sem("weights_ready"), sem("index_ready")
        pos_fill, pos_clear = sem("pos_fill"), sem("pos_clear")
        zero_rows, zeroed = sem("zero_rows"), sem("zeroed")
        staged = sem("staged")
        pool_seen, sync_seen, vector_seen = sem("pool_seen"), sem("sync_seen"), sem("vector_seen")
        pos_put, pos_got = sems("pos_put", 2), sems("pos_got", 2)
        pos_copied, pos_ready, hop1_ready = sem("pos_copied"), sem("pos_ready"), sem("hop1_ready")
        step = sem("step")
        nx_in = sems("nx_in", NODE_RING)
        nn_norm, nn_T, nn_relu, nn_h = sem("nn_norm"), sem("nn_T"), sem("nn_relu"), sem("nn_h")
        nn_y, nn_gelu, nn_out = sem("nn_y"), sem("nn_gelu"), sem("nn_out")
        nn_stored = sems("nn_stored", 2)
        xs_in, xd_in = sems("xs_in", 2), sems("xd_in", 2)
        l_norm, l_T, l_relu, l_h = sem("l_norm"), sem("l_T"), sem("l_relu"), sem("l_h")
        l_hd, l_y, l_gelu, l_n, l_own = sem("l_hd"), sem("l_y"), sem("l_gelu"), sem("l_n"), sem("l_own")
        xd_stored, hd_stored, own_stored = sems("xd_stored", 2), sems("hd_stored", 2), sems("own_stored", 2)
        g_in = sems("g_in", 2)
        g_staged, g_cT, g_cTs, g_bc, g_o = sem("g_staged"), sem("g_cT"), sem("g_cTs"), sem("g_bc"), sem("g_o")
        g_u, g_y, g_gelu, g_x1, g_n = sem("g_u"), sem("g_y"), sem("g_gelu"), sem("g_x1"), sem("g_n")
        g_h, g_hT, g_hTs, g_q, g_done = sem("g_h"), sem("g_hT"), sem("g_hTs"), sem("g_q"), sem("g_done")
        x1_stored, h1_stored = sems("x1_stored", 2), sems("h1_stored", 2)
        hs_in, ea_in = sems("hs_in", 2), sems("ea_in", 2)
        h_staged, h_T, h_Ts, h_v, h_q = sem("h_staged"), sem("h_T"), sem("h_Ts"), sem("h_v"), sem("h_q")
        h_vs, h_z, h_sc, h_scs = sem("h_vs"), sem("h_z"), sem("h_sc"), sem("h_scs")
        k_staged, k_bc, k_h, k_T, k_done = sem("k_staged"), sem("k_bc"), sem("k_h"), sem("k_T"), sem("k_done")
        k_stored, x1_in, put_done = sems("k_stored", 2), sems("x1_in", 2), sems("put_done", 2)
        p2 = {n: sem(f"p2_{n}") for n in ("lines", "local", "rows", "opened", "carried", "args", "exp", "den",
                                          "drows", "dopened", "dcarried", "args2", "exp2", "coef", "back", "done")}
        LOADS = 21

        def prev(slot, use):
            return 1 - slot, use - (1 if slot == 0 else 0)

        block = ctx.enter_context(nc.Block())

        @block.sync
        def _(sp):
            for dst, src in ((ident, ident_in), (sel, sel_in), (w_sb, W), (bq_sb, bq), (bn_sb, bn), (be_sb, be),
                             (attn_sb, attn), (src_i, src_tiles), (dst_i, dst_tiles), (next_i, next_tiles),
                             (edge_i, edge_ids), (dst_l, dst_lines), (prev_l, prev_lines), (next_l, next_lines)):
                sp.dma_start(dst[:], src).then_inc(loaded, 16)
            for dst, src in ((bias_bc, bias), (gamma_bc, gamma), (beta_bc, beta)):
                sp.dma_start(dst[:], src.to_broadcast([P, D])).then_inc(loaded, 16)
            for dst, src in ((wq_sb, Wq), (wn_sb, Wn), (we_sb, We)):
                sp.dma_start(dst[:], src.rearrange("i k f -> k i f")).then_inc(loaded, 16)
            sp.wait_ge(att_zero, 1)
            part = D // HEADS
            for s in range(2):
                for h in range(HEADS):
                    sp.dma_start(att_sb[part * h:part * (h + 1), s * HEADS + h:s * HEADS + h + 1],
                                 att[s, h, :].unsqueeze(1)).then_inc(att_loaded, 16)
            sp.wait_ge(pos_fill, 1)
            sp.dma_start(pos_table.rearrange("(p c) o -> p (c o)", p=125),
                         V[0:125, 0:N // 125].bitcast(i32)).then_inc(pos_clear, 16)
            sp.wait_ge(zero_rows, 1)
            for t in h_tables[1:]:
                sp.dma_start(t[E_PAD:E_PAD + P, :], y_sb[:, 0, :]).then_inc(zeroed, 16)
            for s in (*nn_stored, *hd_stored, *own_stored, *x1_stored, *h1_stored):
                sp.sem_inc(s, 16)

            whole = (BLOCKS - 1) * BLOCK
            x_blocks = x[0:whole, :].rearrange("(b p r) d -> b p r d", p=P, r=ROWS)
            out_blocks = out[0:whole, :].rearrange("(b p r) d -> b p r d", p=P, r=ROWS)

            def node_store(n, slot):
                sp.wait_ge(nn_out, n + 1)
                sp.dma_start(out_blocks[n], node_y[slot][:]).then_inc(nn_stored[slot], 16)

            def node_turn(n, slot, use):
                sp.wait_ge(nn_out, n - NODE_RING + 1)
                sp.dma_start(node_x[slot][:], x_blocks[n]).then_inc(nx_in[slot], 16)
                node_store(n - NODE_RING + 1, (slot + 1) % 2)
            for n in range(NODE_RING):
                sp.dma_start(node_x[n][:], x_blocks[n]).then_inc(nx_in[n], 16)
            node_store(0, 0)
            visits(sp, NODE_RING, BLOCKS - 1, NODE_RING, node_turn)
            n = BLOCKS - 1
            sp.wait_ge(nn_out, n - NODE_RING + 1)
            sp.dma_start(node_x[n % NODE_RING][0:LAST_BLOCK_PARTS],
                         x[whole:N, :].rearrange("(p r) d -> p r d", r=ROWS)).then_inc(nx_in[n % NODE_RING], 16)
            for m in range(n - NODE_RING + 1, n):
                node_store(m, m % 2)
            sp.wait_ge(nn_out, n + 1)
            sp.dma_start(out[whole:N, :].rearrange("(p r) d -> p r d", r=ROWS),
                         node_y[n % 2][0:LAST_BLOCK_PARTS]).then_inc(nn_stored[n % 2], 16)

            def store_own(n, slot):
                sp.wait_ge(l_own, n + 1)
                sp.dma_start(own_chunks[n], h_sb[slot][:]).then_inc(own_stored[slot], 16)

            def keep(n, slot, use):
                sp.wait_ge(xd_in[slot], 64 * (use + 1))
                sp.dma_start(xd_chunks[n], ring_b[slot][:]).then_inc(xd_stored[slot], 16)
                sp.wait_ge(l_hd, n + 1)
                sp.dma_start(hd_chunks[n], hd_out[slot][:]).then_inc(hd_stored[slot], 16)

            def keep_turn(n, slot, use):
                keep(n, slot, use)
                store_own(n - 1, 1 - slot)
            keep(0, 0, 0)
            visits(sp, 1, CHUNKS, 2, keep_turn)
            store_own(CHUNKS - 1, 1)

            for r in range(2):
                sp.wait_ge(xd_stored[r], 16 * (CHUNKS // 2))
                sp.wait_ge(hd_stored[r], 16 * (CHUNKS // 2 + 1))
            sp.wait_ge(l_n, CHUNKS)

            def sums_load(n, slot):
                sp.dma_start(ring_b[slot][:], xd_chunks[n]).then_inc(g_in[slot], 16)
                sp.dma_start(hd_out[slot][:], hd_chunks[n]).then_inc(g_in[slot], 16)

            def sums_store(n, slot):
                sp.wait_ge(g_x1, n + 1)
                sp.dma_start(x1_chunks[n], x1_sb[slot][:]).then_inc(x1_stored[slot], 16)
                sp.wait_ge(g_h, n + 1)
                sp.dma_start(h_chunks[0][n], h_sb[slot][:]).then_inc(h1_stored[slot], 16)

            def sums_turn(n, slot, use):
                sp.wait_ge(g_x1, n - 1)
                sums_load(n, slot)
                sums_store(n - 2, slot)
            sums_load(0, 0)
            sums_load(1, 1)
            visits(sp, 2, CHUNKS, 2, sums_turn)
            sums_store(CHUNKS - 2, 0)
            sums_store(CHUNKS - 1, 1)

            chunk_full = E // CHUNK
            at = chunk_full * CHUNK
            tiles_full, rest = (E - at) // P, (E - at) % P
            edge_chunks = edge_attr[0:at, :].rearrange("(c t p) d -> c p t d", t=TILE_GROUP, p=P)
            for hop in range(HOPS):
                base, uses = hop * CHUNKS, hop * CHUNKS // 2
                if hop:
                    sp.wait_ge(h_T, base)
                for n in range(CHUNKS - chunk_full):
                    if CHUNKS - 1 - n > chunk_full:
                        sp.sem_inc(ea_in[n % 2], 32)
                        continue
                    sp.dma_start(ring_b[n % 2][:, 0:tiles_full, :],
                                 edge_attr[at:at + tiles_full * P, :].rearrange("(t p) d -> p t d", p=P)
                                 ).then_inc(ea_in[n % 2], 16)
                    sp.dma_start(ring_b[n % 2][0:rest, tiles_full, :],
                                 edge_attr[at + tiles_full * P:E, :]).then_inc(ea_in[n % 2], 16)

                def edge_load(n, slot, use):
                    sp.wait_ge(h_T, base + n - 1)
                    sp.sem_inc(sync_seen, 1)
                    sp.dma_start(ring_b[slot][:], edge_chunks[CHUNKS - 1 - n]).then_inc(ea_in[slot], 32)
                visits(sp, CHUNKS - chunk_full, CHUNKS, 2, edge_load)

                if hop < HOPS - 1:
                    def store(n, slot, use):
                        sp.wait_ge(k_done, base + n + 1)
                        sp.dma_start(h_chunks[hop + 1][n], h_sb[slot][:]).then_inc(k_stored[slot], 16)
                    visits(sp, 0, CHUNKS, 2, store)
                else:
                    for r in range(2):
                        sp.wait_ge(x1_stored[r], 16 * (CHUNKS // 2 + 1))
                        sp.dma_start(x1_sb[r][:], x1_chunks[r]).then_inc(x1_in[r], 16)

                    def x1_load(n, slot, use):
                        sp.wait_ge(k_done, base + n - 1)
                        sp.dma_start(x1_sb[slot][:], x1_chunks[n]).then_inc(x1_in[slot], 16)
                    visits(sp, 2, CHUNKS, 2, x1_load)
            for r in range(2):
                sp.wait_ge(nn_stored[r], 16 * (BLOCKS // 2 + 1))
                sp.wait_ge(own_stored[r], 16 * (CHUNKS // 2 + 1))
                sp.wait_ge(h1_stored[r], 16 * (CHUNKS // 2 + 1))
                sp.wait_ge(k_stored[r], 16 * (HOPS - 1) * CHUNKS // 2)
                sp.wait_ge(pos_put[r], 64 * (CHUNKS // 2))
                sp.wait_ge(put_done[r], 64 * (CHUNKS // 2))
            sp.wait_ge(pos_clear, 16)
            sp.wait_ge(zeroed, 32)

        @block.gpsimd
        def _(pool):
            def wait_count(s, value):
                pool.wait_ge(s, value)
                pool.sem_inc(pool_seen, 1)

            def stage(dst, cols_of):
                nc.gpsimd.tensor_copy(dst[:], cols_of).then_inc(staged, 1)

            def gather(dst_of_tile, table, index, done):
                for t in range(TILE_GROUP):
                    pool.indirect_dma_start(out=dst_of_tile(t), out_offset=None, in_=table,
                                            in_offset=bass.IndirectOffsetOnAxis(ap=index[:, t:t + 1], axis=0)
                                            ).then_inc(done, 16)

            def scatter(table, index, src_of_tile, done):
                for t in range(TILE_GROUP):
                    pool.indirect_dma_start(out=table, in_=src_of_tile(t), in_offset=None, bounds_check=N - 1,
                                            out_offset=bass.IndirectOffsetOnAxis(ap=index[:, t:t + 1], axis=0),
                                            oob_is_err=False).then_inc(done, 16)

            def cols(array, n):
                return array[:, bass.ts(n, TILE_GROUP)]

            pool.wait_ge(index_ready, 1)
            pool.wait_ge(pos_clear, 16)

            def put_pos(n, slot, use):
                stage(pos_in[slot], cols(edge_i, n))
                stage(idx_a[slot], cols(put_i, n))
                pool.wait_ge(staged, 2)
                scatter(pos_table, idx_a[slot], lambda t: pos_in[slot][:, t:t + 1], pos_put[slot])
                pool.sem_clear(staged)

            def put_pos_again(n, slot, use):
                wait_count(pos_put[slot], 64 * use)
                put_pos(n, slot, use)
            put_pos(0, 0, 0)
            put_pos(1, 1, 0)
            visits(pool, 2, CHUNKS, 2, put_pos_again)
            for r in range(2):
                pool.wait_ge(pos_put[r], 64 * (CHUNKS // 2))

            def get_pos(n, slot, use):
                stage(idx_a[slot], cols(src_i, n))
                pool.wait_ge(staged, 1)
                gather(lambda t: pos_in[slot][:, t:t + 1], pos_table, idx_a[slot], pos_got[slot])
                pool.sem_clear(staged)

            def copy_pos(n, slot, use):
                wait_count(pos_got[slot], 64 * (use + 1))
                nc.gpsimd.tensor_copy(cols(pos_i, n), pos_in[slot][:]).then_inc(pos_copied, 1)
                wait_count(pos_copied, n + 1)

            def pos_turn(n, slot, use):
                get_pos(n, slot, use)
                copy_pos(n - 1, *prev(slot, use))
            get_pos(0, 0, 0)
            visits(pool, 1, CHUNKS, 2, pos_turn)
            copy_pos(CHUNKS - 1, 1, CHUNKS // 2 - 1)
            pool.sem_inc(pos_ready, 1)

            def get_x(n, slot, use):
                stage(idx_a[slot], cols(src_i, n))
                stage(idx_b[slot], cols(recv_i, n))
                pool.wait_ge(staged, 2)
                gather(lambda t: ring_a[slot][:, t, :], x, idx_a[slot], xs_in[slot])
                gather(lambda t: ring_b[slot][:, t, :], x, idx_b[slot], xd_in[slot])
                pool.sem_clear(staged)

            def get_x_again(n, slot, use):
                wait_count(l_n, n - 1)
                wait_count(xd_stored[slot], 16 * use)
                get_x(n, slot, use)
            get_x(0, 0, 0)
            get_x(1, 1, 0)
            visits(pool, 2, CHUNKS, 2, get_x_again)

            pool.wait_ge(p2["done"], 1)

            def stage_coef(n, slot):
                nc.gpsimd.tensor_copy(coef_st[slot][:], coef[:, bass.ts(n, TILE_GROUP), :]).then_inc(g_staged, 1)

            def stage_coef_again(n, slot, use):
                wait_count(g_cT, n - 1)
                stage_coef(n, slot)
            stage_coef(0, 0)
            stage_coef(1, 1)
            visits(pool, 2, CHUNKS, 2, stage_coef_again)

            for hop in range(HOPS):
                base, uses = hop * CHUNKS, hop * CHUNKS // 2
                if hop == 0:
                    pool.wait_ge(hop1_ready, 1)
                    pool.wait_ge(zeroed, 32)
                for r in range(2):
                    if hop == 0:
                        pool.wait_ge(h1_stored[r], 16 * (CHUNKS // 2 + 1))
                        pool.wait_ge(own_stored[r], 16 * (CHUNKS // 2 + 1))
                    else:
                        pool.wait_ge(k_stored[r], 16 * uses)
                index = hop1_i if hop == 0 else pos_i

                def get_h(n, slot, use):
                    c = CHUNKS - 1 - n
                    nc.gpsimd.tensor_copy(coef_st[slot][:, :, 0], cols(inner_t, c)).then_inc(h_staged, 1)
                    stage(idx_a[slot], cols(index, c))
                    pool.wait_ge(staged, 1)
                    gather(lambda t: ring_a[slot][:, t, :], h_tables[hop], idx_a[slot], hs_in[slot])
                    pool.sem_clear(staged)

                def get_h_again(n, slot, use):
                    wait_count(h_T, base + n - 1)
                    get_h(n, slot, use)
                get_h(0, 0, 0)
                get_h(1, 1, 0)
                visits(pool, 2, CHUNKS, 2, get_h_again)

                pool.wait_ge(p2["done"], hop + 2)

                def stage_hop_coef(n, slot):
                    nc.gpsimd.tensor_copy(coef_st[slot][:, :, 0:3],
                                          coef[:, bass.ts(n, TILE_GROUP), 0:3]).then_inc(k_staged, 1)

                def stage_hop_coef_again(n, slot, use):
                    wait_count(k_bc, base + n - 1)
                    stage_hop_coef(n, slot)

                if hop < HOPS - 1:
                    stage_hop_coef(0, 0)
                    stage_hop_coef(1, 1)
                    visits(pool, 2, CHUNKS, 2, stage_hop_coef_again)
                    continue
                for r in range(2):
                    pool.wait_ge(nn_stored[r], 16 * (BLOCKS // 2 + 1))

                def put_out(n, slot):
                    stage(idx_a[slot], cols(put_i, n))
                    pool.wait_ge(staged, 1)
                    wait_count(k_done, base + n + 1)
                    scatter(out, idx_a[slot], lambda t: h_sb[slot][:, t, :], put_done[slot])
                    pool.sem_clear(staged)

                stage_hop_coef(0, 0)
                stage_hop_coef(1, 1)
                put_out(0, 0)
                stage_hop_coef_again(2, 0, 1)
                put_out(1, 1)

                def last_turns(n, slot, use):
                    stage_hop_coef_again(n, slot, use)
                    wait_count(put_done[1 - slot], 64 * (use - (1 if slot == 0 else 0)))
                    put_out(n - 1, 1 - slot)
                visits(pool, 3, CHUNKS, 2, last_turns)
                pool.wait_ge(put_done[1], 64 * (CHUNKS // 2 - 1))
                put_out(CHUNKS - 1, 1)

        @block.scalar
        def _(act):
            def copy(dst, src):
                return nc.scalar.activation(dst, src, ACT.Copy)

            def node_relu(n):
                act.wait_ge(nn_T, n + 1)
                nc.scalar.activation(aT[:], bank[0][:, :], ACT.Relu).then_inc(nn_relu, 1)

            def node_gelu(n):
                act.wait_ge(nn_y, n + 1)
                nc.scalar.activation(y_sb[:], y_sb[:], ACT.Gelu).then_inc(nn_gelu, 1)

            def node_turn(n, slot, use):
                node_gelu(n - 1)
                node_relu(n)
            node_relu(0)
            visits(act, 1, BLOCKS, 2, node_turn)
            node_gelu(BLOCKS - 1)

            act.wait_ge(pos_clear, 16)

            def l_first(n, slot, use):
                act.wait_ge(l_T, n + 1)
                nc.scalar.activation(aT[:], bank[0][:, :], ACT.Relu)
                nc.scalar.activation(bT[:], bank[1][:, :], ACT.Relu).then_inc(l_relu, 1)
                act.wait_ge(l_h, n + 1)
                copy(V[:, bass.ts(n, CHUNK)], bank[2][:, :])
                copy(scores[:, bass.ts(n, TILE_GROUP), :],
                     bank[4][:, 0:TILE_GROUP * 2 * HEADS].rearrange("p (t k) -> p t k", t=TILE_GROUP))
                act.wait_ge(hd_stored[slot], 16 * (use + 1))
                copy(hd_out[slot][:], bank[3][:, :]).then_inc(l_hd, 1)

            def l_gelu_of(n):
                act.wait_ge(l_y, n + 1)
                nc.scalar.activation(y_sb[:], y_sb[:], ACT.Gelu).then_inc(l_gelu, 1)

            def l_relu_of(n, slot, use):
                act.wait_ge(l_n, n + 1)
                act.wait_ge(own_stored[slot], 16 * (use + 1))
                nc.scalar.activation(h_sb[slot][:], hn_sb[:], ACT.Relu).then_inc(l_own, 1)

            def l_turn(n, slot, use):
                l_gelu_of(n - 1)
                l_first(n, slot, use)
                l_relu_of(n - 1, *prev(slot, use))
            l_first(0, 0, 0)
            visits(act, 1, CHUNKS, 2, l_turn)
            l_gelu_of(CHUNKS - 1)
            l_relu_of(CHUNKS - 1, 1, CHUNKS // 2 - 1)

            def softmax_exps(run, heads):
                K = heads * HALVES
                act.wait_ge(p2["args"], run + 1)
                nc.scalar.activation(AL[:, 0:K], AL[:, 0:K], ACT.Exp)
                nc.scalar.activation(row_a[0:heads], row_a[0:heads], ACT.Exp)
                nc.scalar.activation(PL[:, 0:K], PL[:, 0:K], ACT.Exp).then_inc(p2["exp"], 1)
                if run == 0:
                    act.wait_ge(p2["args2"], 1)
                    nc.scalar.activation(C1[:, 0:K], C1[:, 0:K], ACT.Exp)
                    nc.scalar.activation(C2[:, 0:K], C2[:, 0:K], ACT.Exp).then_inc(p2["exp2"], 1)
            softmax_exps(0, HEADS)

            def g_first(n):
                act.wait_ge(g_cT, n + 1)
                copy(coefT[:], bank[0][0:4 * HEADS, :]).then_inc(g_cTs, 1)

            def g_gelu_of(n):
                act.wait_ge(g_y, n + 1)
                nc.scalar.activation(y_sb[:], y_sb[:], ACT.Gelu).then_inc(g_gelu, 1)

            def g_rows(n, slot, use):
                act.wait_ge(g_n, n + 1)
                act.wait_ge(h1_stored[slot], 16 * (use + 1))
                nc.scalar.activation(h_sb[slot][:], hn_sb[:], ACT.Relu).then_inc(g_h, 1)
                act.wait_ge(g_hT, n + 1)
                copy(aT[:], bank[6][:, :]).then_inc(g_hTs, 1)

            def g_query(n):
                act.wait_ge(g_q, n + 1)
                copy(V[:, bass.ts(n, CHUNK)], bank[7][:, ::-1]).then_inc(g_done, 1)

            def g_turn(n, slot, use):
                g_first(n)
                g_rows(n - 1, *prev(slot, use))
                g_gelu_of(n)
                g_query(n - 1)
            g_first(0)
            g_gelu_of(0)
            visits(act, 1, CHUNKS, 2, g_turn)
            g_rows(CHUNKS - 1, 1, CHUNKS // 2 - 1)
            g_query(CHUNKS - 1)

            for hop in range(HOPS):
                base, uses = hop * CHUNKS, hop * CHUNKS // 2

                def h_first(n):
                    act.wait_ge(h_T, base + n + 1)
                    copy(aT[:], bank[0][:, :])
                    copy(bT[:], bank[1][:, :]).then_inc(h_Ts, 1)
                    act.wait_ge(h_v, base + n + 1)
                    act.wait_ge(h_q, base + n + 1)
                    nc.scalar.activation(V[:, bass.ts(CHUNKS - 1 - n, CHUNK)], bank[3][:, :], ACT.Identity,
                                         bias=v_bias[:, hop:hop + 1]).then_inc(h_vs, 1)

                def h_scores(n):
                    act.wait_ge(h_sc, base + n + 1)
                    copy(scores[:, bass.ts(CHUNKS - 1 - n, TILE_GROUP), 0], bank[4][:, 0:TILE_GROUP]).then_inc(h_scs, 1)

                def h_turn(n, slot, use):
                    h_first(n)
                    h_scores(n - 1)
                h_first(0)
                visits(act, 1, CHUNKS, 2, h_turn)
                h_scores(CHUNKS - 1)
                softmax_exps(hop + 1, 1)

                if hop < HOPS - 1:
                    def k_out(n, slot):
                        act.wait_ge(k_T, base + n + 1)
                        copy(h_sb[slot][:], rows_of(3))
                        copy(V[:, bass.ts(n, CHUNK)], bank[4][:, ::-1]).then_inc(k_done, 1)

                    def k_out_again(n, slot, use):
                        act.wait_ge(k_stored[slot], 16 * (uses + use))
                        k_out(n, slot)
                    k_out(0, 0)
                    k_out(1, 1)
                    visits(act, 2, CHUNKS, 2, k_out_again)

        @block.vector
        def _(dve):
            steps = [0]

            def land(ins):
                steps[0] += 1
                ins.then_inc(step, 1)
                dve.wait_ge(step, steps[0])

            def signal(ins, s):
                land(ins)
                dve.sem_inc(s, 1)

            def settle():
                steps[0] = 0
                dve.sem_clear(step)

            v = nc.vector

            def rsqrt(dst, var):
                w = dst.shape[1]
                va, t = var_e[:, 0:w], nwt[:, 0:w]
                land(v.tensor_scalar(va, var, EPS, None, ALU.add))
                land(v.tensor_scalar(dst.bitcast(i32), va.bitcast(i32), 1, None, ALU.arith_shift_right))
                land(v.tensor_scalar(dst.bitcast(i32), dst.bitcast(i32), -1.0, RSQRT_SEED, ALU.mult, ALU.add))
                for _ in range(3):
                    land(v.scalar_tensor_tensor(out=t, in0=dst, scalar=-0.5, in1=dst, op0=ALU.mult, op1=ALU.mult))
                    land(v.tensor_tensor(t, t, va, ALU.mult))
                    land(v.scalar_tensor_tensor(out=dst, in0=t, scalar=1.5, in1=dst, op0=ALU.add, op1=ALU.mult))

            def normalize(tiles, keep=None, done=None):
                n = len(tiles)
                for i, (_, src) in enumerate(tiles):
                    last = v.bn_stats(stats[:, i, :], src)
                land(last)
                for i in range(n):
                    last = v.bn_aggr(mv[:, i, :], stats[:, i, :])
                land(last)
                rsqrt(rstd[:, 0:n], mv[:, 0:n, 1])
                if keep is not None:
                    land(v.tensor_tensor(rstd[:, 0:n], rstd[:, 0:n], keep, ALU.mult))
                for i, (dst, src) in enumerate(tiles):
                    last = v.tensor_scalar(dst, src, mv[:, i, 0:1], rstd[:, i:i + 1], ALU.subtract, ALU.mult)
                signal(last, done) if done is not None else land(last)

            def after_projection(u, ready):
                def wide(a):
                    return a[:, :].unsqueeze(1).to_broadcast([P, TILE_GROUP, D])
                land(v.tensor_tensor(y_sb[:], u, wide(bias_bc), ALU.add))
                normalize([(y_sb[:, t, :], y_sb[:, t, :]) for t in range(TILE_GROUP)])
                land(v.tensor_tensor(y_sb[:], y_sb[:], wide(gamma_bc), ALU.mult))
                signal(v.tensor_tensor(y_sb[:], y_sb[:], wide(beta_bc), ALU.add), ready)

            signal(v.memset(att_sb[:], 0.0), att_zero)
            land(v.memset(w_att[:], 0.0))
            signal(v.memset(V[0:125, 0:N // 125].bitcast(i32), E_PAD), pos_fill)
            signal(v.memset(y_sb[:], 0.0), zero_rows)
            dve.wait_ge(loaded, 16 * LOADS - 16)
            land(v.tensor_tensor(v_bias[:], bn_sb[:], be_sb[:], ALU.add))
            land(v.tensor_tensor(inner_t[:], next_i[:], dst_i[:], ALU.is_equal))
            land(v.tensor_scalar(last_t[:], inner_t[:], -1.0, 1.0, ALU.mult, ALU.add))
            land(v.scalar_tensor_tensor(out=put_i[:], in0=inner_t[:], scalar=float(SKIP), in1=dst_i[:],
                                        op0=ALU.mult, op1=ALU.add))
            signal(v.tensor_scalar(recv_i[:], dst_i[:], float(N - 1), None, ALU.min), index_ready)
            land(v.tensor_tensor(same_l[:], prev_l[:], dst_l[:], ALU.is_equal))
            land(v.tensor_scalar(pen_l[:], same_l[:], -1.0, -NONE, ALU.add, ALU.mult))
            land(v.tensor_tensor(last_l[:], next_l[:], dst_l[:], ALU.not_equal))
            land(v.tensor_reduce(whole_l[:], same_l[:], AX.X, ALU.min))
            dve.wait_ge(wT_done, 1)
            signal(v.tensor_copy(wT[:], tile_of(0, 0)), wT_copied)
            dve.wait_ge(watt_done, 1)
            H = HEADS
            land(v.tensor_copy(w_att[:, 0:H], bank[1][:, 0:H]))
            land(v.tensor_copy(w_att[:, 2 * H:4 * H], bank[1][:, 0:2 * H]))
            land(v.tensor_copy(w_att[:, 2 * H:3 * H], bank[1][:, H:2 * H]))
            land(v.tensor_tensor(w_att[:, 3 * H:4 * H], w_att[:, 0:H], w_att[:, 2 * H:3 * H], ALU.add))
            dve.sem_inc(weights_ready, 1)
            dve.wait_ge(zeroed, 32)
            settle()

            def node_norm(n, slot, use):
                dve.wait_ge(nx_in[slot], 16 * (use + 1))
                normalize([(xn[:, t, :], node_x[slot][:, t, :]) for t in range(ROWS)], done=nn_norm)

            def node_y_of(n):
                dve.wait_ge(nn_h, n + 1)
                after_projection(rows_of(1), nn_y)

            def node_sum(n, slot, use):
                dve.wait_ge(nn_gelu, n + 1)
                dve.wait_ge(nn_stored[slot % 2], 16 * (use + 1))
                signal(v.tensor_tensor(node_y[slot % 2][:], y_sb[:], node_x[slot][:], ALU.add), nn_out)

            def node_turn(n, slot, use):
                node_y_of(n - 1)
                node_norm(n, slot, use)
                back = (slot - 1) % NODE_RING
                used = use - (1 if slot == 0 else 0)
                node_sum(n - 1, back, used * (NODE_RING // 2) + back // 2)
                settle()
            node_norm(0, 0, 0)
            settle()
            visits(dve, 1, BLOCKS, NODE_RING, node_turn)
            node_y_of(BLOCKS - 1)
            node_sum(BLOCKS - 1, NODE_RING - 1, (BLOCKS - 1) // 2)
            settle()

            def l_norm_of(n, slot, use):
                dve.wait_ge(xs_in[slot], 64 * (use + 1))
                dve.wait_ge(xd_in[slot], 64 * (use + 1))
                normalize([(xn[:, g * TILE_GROUP + t, :], ring[slot][:, t, :])
                           for g, ring in enumerate((ring_a, ring_b)) for t in range(TILE_GROUP)], done=l_norm)

            def l_y_of(n):
                dve.wait_ge(l_h, n + 1)
                after_projection(rows_of(5), l_y)

            def l_own_of(n, slot):
                dve.wait_ge(l_gelu, n + 1)
                land(v.tensor_tensor(x1_sb[slot][:], y_sb[:], ring_a[slot][:], ALU.add))
                normalize([(hn_sb[:, t, :], x1_sb[slot][:, t, :]) for t in range(TILE_GROUP)], done=l_n)

            def l_turn(n, slot, use):
                l_y_of(n - 1)
                l_norm_of(n, slot, use)
                l_own_of(n - 1, 1 - slot)
                settle()
            l_norm_of(0, 0, 0)
            settle()
            visits(dve, 1, CHUNKS, 2, l_turn)
            l_y_of(CHUNKS - 1)
            l_own_of(CHUNKS - 1, 1)
            settle()

            dve.wait_ge(pos_ready, 1)
            none = coef[:, :, 0]
            land(v.tensor_scalar(none, pos_i[:], float(E_PAD), None, ALU.is_ge))
            land(v.tensor_tensor(none, none, edge_i[:], ALU.mult))
            land(v.tensor_tensor(hop1_i[:], none, pos_i[:], ALU.add))
            dve.sem_inc(hop1_ready, 1)

            def softmax(run, heads):
                K = heads * HALVES
                SK = 2 * K if run == 0 else K

                def lines_bc(a):
                    return a[:].unsqueeze(1).to_broadcast([LINES, heads, HALVES, P])

                def by_head(a):
                    return a[:, 0:K].rearrange("l (h f) e -> l h f e", f=HALVES)

                dve.wait_ge(p2["lines"], run + 1)
                for b in range(-(-SK // 4)):
                    w = min(4, SK - 4 * b)
                    land(v.tensor_copy(SL[:, 4 * b:4 * b + w, :],
                                       bank[b][0:LINES, 0:w * P].rearrange("l (k e) -> l k e", e=P)))
                if run == 0:
                    land(v.scalar_tensor_tensor(out=SL[:], in0=SL[:], scalar=SLOPE, in1=SL[:],
                                                op0=ALU.mult, op1=ALU.max))
                for k in range(K):
                    last = v.tensor_tensor_scan(ML[:, k, :], pen_l[:, k % 2, :], SL[:, k, :], NONE, ALU.add, ALU.max)
                signal(last, p2["local"])
                dve.wait_ge(p2["rows"], run + 1)
                land(v.tensor_copy(row_f[0:heads], bank[4][0:heads, 0:TILES]))
                land(v.tensor_copy(row_w[0:heads], bank[4][0:heads, TILES:2 * TILES]))
                land(v.tensor_scalar(row_pen[0:heads], row_w[0:heads], -1.0, -NONE, ALU.add, ALU.mult))
                land(v.memset(opened[0:heads, 0:1], NONE))
                land(v.tensor_tensor_scan(opened[0:heads, 1:TILES + 1], row_pen[0:heads], row_f[0:heads], NONE,
                                          ALU.add, ALU.max))
                land(v.tensor_tensor(row_a[0:heads], opened[0:heads, 0:TILES], opened[0:heads, 1:TILES + 1],
                                     ALU.subtract))
                land(v.tensor_scalar(row_a[0:heads], row_a[0:heads], 0.0, None, ALU.min))
                dve.sem_inc(p2["opened"], 1)
                dve.wait_ge(p2["carried"], run + 1)
                land(v.tensor_copy(carry_l[:, 0:K], bank[5][0:LINES, 0:K]))
                for k in range(K):
                    h, f = k // 2, k % 2
                    last = v.tensor_tensor_scan(ML[:, k, :], pen_l[:, f, :], SL[:, k, :],
                                                carry_l[:, f * heads + h:f * heads + h + 1], ALU.add, ALU.max)
                land(last)
                for k in range(K):
                    h, f = k // 2, k % 2
                    last = v.tensor_copy(AL[:, k, 0:1], carry_l[:, f * heads + h:f * heads + h + 1])
                land(last)
                land(v.tensor_copy(AL[:, 0:K, 1:P], ML[:, 0:K, 0:P - 1]))
                land(v.tensor_tensor(AL[:, 0:K], AL[:, 0:K], ML[:, 0:K], ALU.subtract))
                land(v.tensor_scalar(AL[:, 0:K], AL[:, 0:K], 0.0, None, ALU.min))
                signal(v.tensor_tensor(PL[:, 0:K], SL[:, 0:K], ML[:, 0:K], ALU.subtract), p2["args"])
                dve.wait_ge(p2["exp"], run + 1)
                land(v.tensor_tensor(by_head(AL), by_head(AL), lines_bc(same_l), ALU.mult))
                land(v.tensor_tensor(row_a[0:heads], row_a[0:heads], row_w[0:heads], ALU.mult))
                for k in range(K):
                    last = v.tensor_tensor_scan(DL[:, k, :], AL[:, k, :], PL[:, k, :], 0.0, ALU.mult, ALU.add)
                signal(last, p2["den"])
                dve.wait_ge(p2["drows"], run + 1)
                land(v.tensor_copy(row_f[0:heads], bank[4][0:heads, 0:TILES]))
                land(v.memset(opened[0:heads, 0:1], 0.0))
                signal(v.tensor_tensor_scan(opened[0:heads, 1:TILES + 1], row_a[0:heads], row_f[0:heads], 0.0,
                                     ALU.mult, ALU.add), p2["dopened"])
                dve.wait_ge(p2["dcarried"], run + 1)
                land(v.tensor_copy(carry_l[:, 0:K], bank[5][0:LINES, 0:K]))
                for k in range(K):
                    h, f = k // 2, k % 2
                    last = v.tensor_tensor_scan(DL[:, k, :], AL[:, k, :], PL[:, k, :],
                                                carry_l[:, f * heads + h:f * heads + h + 1], ALU.mult, ALU.add)
                land(last)
                if run == 0:
                    land(v.tensor_tensor(C1[:], ML[:], C2, ALU.max))
                    land(v.tensor_tensor(C2, C2, C1[:], ALU.subtract))
                    signal(v.tensor_tensor(C1[:], ML[:], C1[:], ALU.subtract), p2["args2"])
                    dve.wait_ge(p2["exp2"], 1)
                    land(v.tensor_tensor(DL[:], DL[:], C1[:], ALU.mult))
                    land(v.tensor_tensor(DL[:], DL[:], C2, ALU.add))
                    land(v.tensor_scalar(DL[:], DL[:], 1e-16, None, ALU.add))
                    land(v.reciprocal(DL[:], DL[:]))
                    land(v.tensor_tensor(C1[:], C1[:], DL[:], ALU.mult))
                    signal(v.tensor_tensor(C2, C2, DL[:], ALU.mult), p2["coef"])
                else:
                    land(v.reciprocal(DL[:, 0:K], DL[:, 0:K]))
                    signal(v.tensor_tensor(by_head(C1), by_head(DL), lines_bc(last_l), ALU.mult), p2["coef"])
                dve.wait_ge(p2["back"], run + 1)
                parts = 4 if run == 0 else 3
                for q in range(parts):
                    for k in range(K):
                        h, f = k // 2, k % 2
                        b, at = 2 * q + k // 4, (k % 4) * P
                        last = v.tensor_copy(coef[:, f * LINES:(f + 1) * LINES, q * heads + h],
                                             bank[b][:, at:at + LINES])
                signal(last, p2["done"])
                settle()
            softmax(0, HEADS)

            def g_sum(n, slot, use, first=False):
                dve.wait_ge(g_bc, n + 1)
                dve.wait_ge(g_in[slot], 32 * (use + 1))
                land(v.tensor_tensor(pv[:], bank[2][:, :], V[:, bass.ts(n, CHUNK)], ALU.mult))
                start = 0.0 if first else run_sum[1 - slot][:, CHUNK - 1:CHUNK]
                land(v.tensor_tensor_scan(run_sum[slot][:], bank[1][:, :], pv[:], start, ALU.mult, ALU.add))
                land(v.tensor_tensor(t_sb[:], bank[4][:, :], hd_out[slot][:], ALU.mult))
                land(v.tensor_tensor(o_sb[slot][:], bank[3][:, :], run_sum[slot][:], ALU.mult))
                signal(v.tensor_tensor(o_sb[slot][:], o_sb[slot][:], t_sb[:], ALU.add), g_o)

            def g_y_of(n):
                dve.wait_ge(g_u, n + 1)
                after_projection(rows_of(5), g_y)

            def g_next(n, slot, use):
                dve.wait_ge(g_gelu, n + 1)
                dve.wait_ge(x1_stored[slot], 16 * (use + 1))
                land(v.tensor_tensor(x1_sb[slot][:], y_sb[:], ring_b[slot][:], ALU.add))
                dve.sem_inc(g_x1, 1)
                normalize([(hn_sb[:, t, :], x1_sb[slot][:, t, :]) for t in range(TILE_GROUP)],
                          keep=last_t[:, bass.ts(n, TILE_GROUP)], done=g_n)

            def g_turn(n, slot, use):
                g_sum(n, slot, use)
                g_next(n - 1, *prev(slot, use))
                g_y_of(n)
                settle()
            g_sum(0, 0, 0, first=True)
            g_y_of(0)
            settle()
            visits(dve, 1, CHUNKS, 2, g_turn)
            g_next(CHUNKS - 1, 1, CHUNKS // 2 - 1)
            settle()

            for hop in range(HOPS):
                base, uses = hop * CHUNKS, hop * CHUNKS // 2

                def h_query(n, slot, first=False):
                    dve.wait_ge(h_T, base + n + 1)
                    dve.sem_inc(vector_seen, 1)
                    start = 0.0 if first else run_sum[1 - slot][:, 0:1]
                    signal(v.tensor_tensor_scan(run_sum[slot][:, ::-1], bank[2][:, ::-1],
                                         V[:, bass.ts(CHUNKS - 1 - n, CHUNK)], start,
                                         ALU.mult, ALU.add), h_q)

                def h_leaky(n, slot):
                    dve.wait_ge(h_vs, base + n + 1)
                    dve.sem_inc(vector_seen, 1)
                    land(v.scalar_tensor_tensor(out=t_sb[:], in0=run_sum[slot][:], scalar=bq_sb[:, hop:hop + 1],
                                                in1=V[:, bass.ts(CHUNKS - 1 - n, CHUNK)], op0=ALU.add, op1=ALU.add))
                    signal(v.scalar_tensor_tensor(out=z_sb[:], in0=t_sb[:], scalar=SLOPE, in1=t_sb[:],
                                           op0=ALU.mult, op1=ALU.max), h_z)

                def h_turn(n, slot, use):
                    h_query(n, slot)
                    h_leaky(n - 1, 1 - slot)
                    settle()
                h_query(0, 0, first=True)
                settle()
                visits(dve, 1, CHUNKS, 2, h_turn)
                dve.wait_ge(h_sc, base + CHUNKS - 1)
                h_leaky(CHUNKS - 1, 1)
                settle()
                softmax(hop + 1, 1)

                def k_sum(n, slot, first=False):
                    dve.wait_ge(k_bc, base + n + 1)
                    land(v.tensor_tensor(pv[:], bank[1][:, :], V[:, bass.ts(n, CHUNK)], ALU.mult))
                    start = 0.0 if first else run_sum[1 - slot][:, CHUNK - 1:CHUNK]
                    land(v.tensor_tensor_scan(run_sum[slot][:], bank[0][:, :], pv[:], start, ALU.mult, ALU.add))
                    signal(v.scalar_tensor_tensor(out=o_sb[slot][:], in0=run_sum[slot][:], scalar=0.0, in1=bank[2][:, :],
                                           op0=ALU.max, op1=ALU.mult), k_h)

                def k_final(n, slot, use):
                    dve.wait_ge(k_T, base + n + 1)
                    dve.wait_ge(x1_in[slot], 16 * (use + 1))
                    signal(v.tensor_tensor(h_sb[slot][:], rows_of(3), x1_sb[slot][:], ALU.add), k_done)

                def k_turn(n, slot, use):
                    k_sum(n, slot)
                    if hop == HOPS - 1:
                        s, u = prev(slot, use)
                        dve.wait_ge(put_done[s], 64 * u)
                        k_final(n - 1, s, u)
                    settle()
                k_sum(0, 0, first=True)
                settle()
                if hop < HOPS - 1:
                    visits(dve, 1, CHUNKS, 2, k_turn)
                    continue
                for n in (1, 2):
                    k_sum(n, n % 2)
                    k_final(n - 1, (n - 1) % 2, 0)
                    settle()
                visits(dve, 3, CHUNKS, 2, k_turn)
                dve.wait_ge(put_done[1], 64 * (CHUNKS // 2 - 1))
                k_final(CHUNKS - 1, 1, CHUNKS // 2 - 1)

        @block.tensor
        def _(pe):
            def mm(dst, lhsT, rhs, start=True, stop=True):
                return nc.tensor.matmul(dst, lhsT, rhs, start=start, stop=stop)

            def tr(dst, src):
                k = src.shape[0]
                return nc.tensor.transpose(dst, src, ident[0:k, 0:k])

            pe.wait_ge(loaded, 16 * LOADS - 16)
            pe.wait_ge(att_loaded, 16 * 2 * HEADS)
            tr(tile_of(0, 0), w_sb[:]).then_inc(wT_done, 1)
            pe.wait_ge(wT_copied, 1)
            mm(bank[1][:, 0:2 * HEADS], wT[:], att_sb[:]).then_inc(watt_done, 1)
            pe.wait_ge(weights_ready, 1)

            def node(n, slot, use):
                pe.wait_ge(nn_norm, n + 1)
                for t in range(ROWS):
                    last = tr(tile_of(0, t), xn[:, t, :])
                last.then_inc(nn_T, 1)
                pe.wait_ge(nn_relu, n + 1)
                for t in range(ROWS):
                    last = mm(tile_of(1, t), aT[:, t * P:(t + 1) * P], w_sb[:])
                last.then_inc(nn_h, 1)
            visits(pe, 0, BLOCKS, 2, node)

            def l_visit(n, slot, use, first=False):
                pe.wait_ge(l_norm, n + 1)
                for t in range(2 * TILE_GROUP):
                    last = tr(tile_of(t // TILE_GROUP, t % TILE_GROUP), xn[:, t, :])
                last.then_inc(l_T, 1)
                pe.wait_ge(l_relu, n + 1)
                if not first:
                    pe.wait_ge(l_hd, n)
                K = 2 * HEADS
                for t in range(TILE_GROUP):
                    a, b = aT[:, t * P:(t + 1) * P], bT[:, t * P:(t + 1) * P]
                    mm(tile_of(5, t), a, w_sb[:])
                    mm(bank[4][:, t * K:(t + 1) * K], a, w_att[:, 0:K], True, False)
                    mm(bank[4][:, t * K:(t + 1) * K], b, w_att[:, K:2 * K], False, True)
                mm(bank[2][:, :], w_sb[:], aT[:])
                mm(bank[3][:, :], w_sb[:], bT[:]).then_inc(l_h, 1)
            l_visit(0, 0, 0, first=True)
            visits(pe, 1, CHUNKS, 2, l_visit)

            def softmax(run, heads):
                K = heads * HALVES
                SK = 2 * K if run == 0 else K
                for k in range(SK):
                    f = k % 2
                    last = tr(bank[k // 4][0:LINES, (k % 4) * P:(k % 4 + 1) * P],
                              scores[:, f * LINES:(f + 1) * LINES, k // 2])
                last.then_inc(p2["lines"], 1)
                pe.wait_ge(p2["local"], run + 1)
                for f in range(HALVES):
                    tr(bank[4][0:heads, f * LINES:(f + 1) * LINES], ML[:, f:K:HALVES, P - 1])
                    last = tr(bank[4][0:heads, TILES + f * LINES:TILES + (f + 1) * LINES],
                              whole_l[:, f:f + 1].to_broadcast([LINES, heads]))
                last.then_inc(p2["rows"], 1)
                pe.wait_ge(p2["opened"], run + 1)
                for f in range(HALVES):
                    last = tr(bank[5][0:LINES, f * heads:(f + 1) * heads],
                              opened[0:heads, f * LINES:(f + 1) * LINES])
                last.then_inc(p2["carried"], 1)
                pe.wait_ge(p2["den"], run + 1)
                for f in range(HALVES):
                    last = tr(bank[4][0:heads, f * LINES:(f + 1) * LINES], DL[:, f:K:HALVES, P - 1])
                last.then_inc(p2["drows"], 1)
                pe.wait_ge(p2["dopened"], run + 1)
                for f in range(HALVES):
                    last = tr(bank[5][0:LINES, f * heads:(f + 1) * heads],
                              opened[0:heads, f * LINES:(f + 1) * LINES])
                last.then_inc(p2["dcarried"], 1)
                pe.wait_ge(p2["coef"], run + 1)
                for q, src in enumerate((AL, PL, C1, C2)[:4 if run == 0 else 3]):
                    for k in range(K):
                        last = tr(bank[2 * q + k // 4][:, (k % 4) * P:(k % 4) * P + LINES], src[:, k, :])
                last.then_inc(p2["back"], 1)
                pe.wait_ge(p2["done"], run + 1)
            pe.wait_ge(l_hd, CHUNKS)
            pe.wait_ge(l_n, CHUNKS)
            softmax(0, HEADS)

            def g_bcast(n, slot, first=False):
                pe.wait_ge(g_staged, n + 1)
                for t in range(TILE_GROUP):
                    last = tr(bank[0][0:4 * HEADS, t * P:(t + 1) * P], coef_st[slot][:, t, :])
                last.then_inc(g_cT, 1)
                pe.wait_ge(g_cTs, n + 1)
                if not first:
                    pe.wait_ge(g_o, n)
                for q in range(4):
                    last = mm(bank[1 + q][:, :], sel[:, q, :], coefT[:])
                last.then_inc(g_bc, 1)
                pe.wait_ge(g_o, n + 1)
                for t in range(TILE_GROUP):
                    last = tr(tile_of(5, t), o_sb[slot][:, t * P:(t + 1) * P])
                last.then_inc(g_u, 1)

            def g_query(n, slot):
                pe.wait_ge(g_h, n + 1)
                for t in range(TILE_GROUP):
                    last = tr(tile_of(6, t), h_sb[slot][:, t, :])
                last.then_inc(g_hT, 1)
                pe.wait_ge(g_hTs, n + 1)
                mm(bank[7][:, :], wq_sb[:, 0, :], aT[:]).then_inc(g_q, 1)

            def g_turn(n, slot, use):
                g_bcast(n, slot)
                g_query(n - 1, 1 - slot)
            g_bcast(0, 0, first=True)
            visits(pe, 1, CHUNKS, 2, g_turn)
            g_query(CHUNKS - 1, 1)

            for hop in range(HOPS):
                base, uses = hop * CHUNKS, hop * CHUNKS // 2
                if hop:
                    pe.wait_ge(k_done, base)
                else:
                    pe.wait_ge(g_done, CHUNKS)

                def h_values(n, slot, use, first=False):
                    pe.wait_ge(hs_in[slot], 64 * (uses + use + 1))
                    pe.wait_ge(ea_in[slot], 32 * (uses + use + 1))
                    pe.wait_ge(h_staged, base + n + 1)
                    if not first:
                        pe.wait_ge(h_q, base + n)
                    for t in range(TILE_GROUP):
                        tr(tile_of(0, t), ring_a[slot][:, t, :])
                        tr(tile_of(1, t), ring_b[slot][:, t, :])
                        last = tr(tile_of(2, t), coef_st[slot][:, t, 0:1].to_broadcast([P, P]))
                    last.then_inc(h_T, 1)
                    pe.wait_ge(h_Ts, base + n + 1)
                    mm(bank[3][:, :], wn_sb[:, hop, :], aT[:], True, False)
                    mm(bank[3][:, :], we_sb[:, hop, :], bT[:], False, True).then_inc(h_v, 1)

                def h_score(n):
                    pe.wait_ge(h_z, base + n + 1)
                    for t in range(TILE_GROUP):
                        last = mm(bank[4][:, t:t + 1], z_sb[:, t * P:(t + 1) * P], attn_sb[:, hop:hop + 1])
                    last.then_inc(h_sc, 1)

                def h_turn(n, slot, use):
                    h_values(n, slot, use)
                    h_score(n - 1)
                h_values(0, 0, 0, first=True)
                visits(pe, 1, CHUNKS, 2, h_turn)
                pe.wait_ge(h_scs, base + CHUNKS - 1)
                h_score(CHUNKS - 1)
                pe.wait_ge(h_scs, base + CHUNKS)
                softmax(hop + 1, 1)

                def k_bcast(n, slot, first=False):
                    pe.wait_ge(k_staged, base + n + 1)
                    if not first:
                        pe.wait_ge(k_h, base + n)
                    for q in range(3):
                        for t in range(TILE_GROUP):
                            last = tr(tile_of(q, t), coef_st[slot][:, t, q:q + 1].to_broadcast([P, P]))
                    last.then_inc(k_bc, 1)

                def k_rows(n, slot, first=False):
                    pe.wait_ge(k_h, base + n + 1)
                    if not first:
                        pe.wait_ge(k_done, base + n)
                    for t in range(TILE_GROUP):
                        last = tr(tile_of(3, t), o_sb[slot][:, t * P:(t + 1) * P])
                    if hop < HOPS - 1:
                        last = mm(bank[4][:, :], wq_sb[:, hop + 1, :], o_sb[slot][:])
                    last.then_inc(k_T, 1)

                def k_turn(n, slot, use):
                    k_bcast(n, slot)
                    k_rows(n - 1, 1 - slot)
                k_bcast(0, 0, first=True)
                k_bcast(1, 1)
                k_rows(0, 0, first=True)
                visits(pe, 2, CHUNKS, 2, k_turn)
                k_rows(CHUNKS - 1, 1)


_SHAPES = ["x", "src_tiles", "dst_tiles", "next_tiles", "edge_ids", "dst_lines", "prev_lines", "next_lines",
           "edge_attr", "W", "att", "bias", "gamma", "beta", "Wq", "Wn", "We", "bq", "bn", "be", "attn",
           "ident", "sel"]


def kernel(**inputs):
    import numpy as _np
    import concourse.bacc as _bacc
    from concourse import mybir as _mybir
    from concourse.bass_utils import run_bass_kernel_spmd as _run

    given = {k: _np.asarray(v) for k, v in inputs.items()}

    def pad(a, value):
        return _np.concatenate([a, _np.full(E_PAD - a.shape[0], value, a.dtype)])

    def tiles(a):
        return a.reshape(TILES, P).T

    def lines(a):
        return a.reshape(HALVES, LINES, P).transpose(1, 0, 2)

    dst = pad(given["dst"], N)
    ends = _np.full(1, -1, dst.dtype)
    after, before = _np.concatenate([dst[1:], ends]), _np.concatenate([ends, dst[:-1]])
    sel = _np.zeros((4 * HEADS, 4, D), _np.float32)
    for q in range(4):
        for h in range(HEADS):
            sel[q * HEADS + h, q, h * D // HEADS:(h + 1) * D // HEADS] = 1
    data = {
        "x": given["x"], "src_tiles": tiles(pad(given["src"], 0)), "dst_tiles": tiles(dst),
        "next_tiles": tiles(after), "edge_ids": tiles(_np.arange(E_PAD, dtype=_np.int32)),
        "dst_lines": lines(dst), "prev_lines": lines(before), "next_lines": lines(after),
        "edge_attr": given["edge_attr_128"], "W": given["L0_gnn_W"],
        "att": _np.stack([given["L0_gnn_att_src"], given["L0_gnn_att_dst"]]),
        "bias": given["L0_gnn_bias"][None], "gamma": given["L0_gnn_gamma"][None], "beta": given["L0_gnn_beta"][None],
        "Wq": given["L1_gnn_Wq"], "Wn": given["L1_gnn_Wn"], "We": given["L1_gnn_We"],
        "bq": given["L1_gnn_bq"].T, "bn": given["L1_gnn_bn"].T, "be": given["L1_gnn_be"].T,
        "attn": given["L1_gnn_attn"].T, "ident": _np.eye(P, dtype=_np.float32), "sel": sel,
    }
    nc = _bacc.Bacc("TRN2", target_bir_lowering=False, num_devices=1)
    arrays, args = {}, []
    for name in _SHAPES:
        a = _np.ascontiguousarray(data[name])
        arrays[f"in_{name}"] = a
        args.append(nc.dram_tensor(f"in_{name}", a.shape, _mybir.dt.from_np(a.dtype), kind="ExternalInput").ap())
    out = nc.dram_tensor("out_0", (N, D), _mybir.dt.float32, kind="ExternalOutput").ap()
    build(nc, *args, out)
    return _run(nc, [arrays], core_ids=[0]).results[0]["out_0"]
```

```python
from contextlib import ExitStack

import numpy as np
import concourse.bass as bass
from concourse import mybir

P = 128
D = 128
N = 100000
E = 25000
HEADS = 4
HOPS = 3
TILE_GROUP = 4
CHUNK = TILE_GROUP * P
CHUNKS = 2 * -(-E // (2 * CHUNK))
E_PAD = CHUNKS * CHUNK
TILES = E_PAD // P
HALVES = 2
LINES = TILES // HALVES
ROWS = 8
BLOCK = P * ROWS
BLOCKS = -(-N // BLOCK)
LAST_BLOCK_PARTS = (N - (BLOCKS - 1) * BLOCK) // ROWS
NODE_RING = 6
X_RING = 6
EPS = 1e-5
NONE = -1e30
SKIP = 1 << 20
SLOPE = 0.2
PARTS = 3
RSQRT_SEED = float(0x5F3759DF)
assert (N - (BLOCKS - 1) * BLOCK) % ROWS == 0


def visits(eng, first, total, ring, visit):
    turns = (total - first) // ring
    with eng.Fori(0, turns) as j:
        for u in range(first, first + ring):
            visit(j * ring + u, u % ring, j + u // ring)
    for n in range(first + turns * ring, total):
        visit(n, n % ring, n // ring)


def of_two(slot, use):
    return slot % 2, use * (X_RING // 2) + slot // 2


def of_three(slot, use):
    return slot % 3, use * (X_RING // 3) + slot // 3


def build(nc, x, src_tiles, dst_tiles, next_tiles, edge_ids, dst_lines, prev_lines, next_lines, edge_attr,
          W, att, bias, gamma, beta, Wq, Wn, We, bq, bn, be, attn, ident_in, sel_in, out):
    f32 = mybir.dt.float32
    bf16 = mybir.dt.bfloat16
    i32 = mybir.dt.int32
    ALU = mybir.AluOpType
    ACT = mybir.ActivationFunctionType
    AX = mybir.AxisListType
    ctx = ExitStack()
    with ctx:
        def sb(name, shape, dt=f32):
            return ctx.enter_context(nc.sbuf_tensor(name, shape, dt))

        def sem(name):
            return ctx.enter_context(nc.semaphore(name))

        def sems(name, n):
            return [sem(f"{name}{i}") for i in range(n)]

        pos_table = nc.dram_tensor("pos_table", (N, 1), i32).ap()
        xd_rows = nc.dram_tensor("xd_rows", (E_PAD, D), f32).ap()
        hd_feat = nc.dram_tensor("hd_feat", (P, E_PAD), f32).ap()
        x1_rows = nc.dram_tensor("x1_rows", (E_PAD, D), f32).ap()
        h_tables = [nc.dram_tensor("h1_table", (2 * E_PAD, D), f32).ap(),
                    nc.dram_tensor("h2_table", (E_PAD + P, D), f32).ap(),
                    nc.dram_tensor("h3_table", (E_PAD + P, D), f32).ap()]

        def chunked(rows):
            return rows.rearrange("(c t p) d -> c p t d", t=TILE_GROUP, p=P)

        xd_chunks, x1_chunks = chunked(xd_rows), chunked(x1_rows)
        h_chunks = [chunked(h_tables[0][0:E_PAD, :])] + [chunked(t[0:E_PAD, :]) for t in h_tables[1:]]
        own_chunks = chunked(h_tables[0][E_PAD:2 * E_PAD, :])
        hd_chunks = hd_feat.rearrange("f (c e) -> c f e", e=CHUNK)

        ident = sb("ident", [P, P])
        sel = sb("sel", [PARTS * 4 * HEADS, 4, P])
        sel_bf = sb("sel_bf", [PARTS * 4 * HEADS, 4, P], bf16)
        ident_bf = sb("ident_bf", [P, P], bf16)
        w_sb = sb("w_sb", [P, D])
        wT = sb("wT", [P, D])
        att_sb = sb("att_sb", [P, 2 * HEADS])
        w_att = sb("w_att", [P, 4 * HEADS])
        wq_sb = sb("wq_sb", [P, HOPS, D])
        wn_sb = sb("wn_sb", [P, HOPS, D])
        we_sb = sb("we_sb", [P, HOPS, D])
        bq_sb = sb("bq_sb", [P, HOPS])
        bn_sb = sb("bn_sb", [P, HOPS])
        be_sb = sb("be_sb", [P, HOPS])
        v_bias = sb("v_bias", [P, HOPS])
        attn_sb = sb("attn_sb", [P, HOPS])
        bias_bc = sb("bias_bc", [P, D])
        w_mid = sb("w_mid", [P, D])
        middle = sb("middle", [P, D])
        row_mean = sb("row_mean", [P, 2])
        BIAS_K = 65
        bias_rows = sb("bias_rows", [BIAS_K, TILE_GROUP, D], bf16)
        bias_wide = sb("bias_wide", [BIAS_K, 2, D + 2 * HEADS], bf16)
        w_wide = sb("w_wide", [P, D + 2 * HEADS])
        bias_ones = sb("bias_ones", [BIAS_K, P], bf16)
        z_bf = sb("z_bf", [BIAS_K, D], bf16)
        gamma_bc = sb("gamma_bc", [P, D])
        beta_bc = sb("beta_bc", [P, D])
        src_i = sb("src_i", [P, TILES], i32)
        dst_i = sb("dst_i", [P, TILES], i32)
        next_i = sb("next_i", [P, TILES], i32)
        edge_i = sb("edge_i", [P, TILES], i32)
        recv_i = sb("recv_i", [P, TILES], i32)
        put_i = sb("put_i", [P, TILES], i32)
        pos_i = sb("pos_i", [P, TILES], i32)
        hop1_i = next_i
        last_t = sb("last_t", [P, TILES])
        inner_t = sb("inner_t", [P, TILES])
        same_l = sb("same_l", [LINES, HALVES, P])
        pen_l = sb("pen_l", [LINES, HALVES, P])
        last_l = sb("last_l", [LINES, HALVES, P])
        whole_l = sb("whole_l", [LINES, HALVES])
        V = sb("V", [P, E_PAD])
        scores = sb("scores", [P, TILES, 2 * HEADS])
        coef = sb("coef", [P, TILES, 4 * HEADS])
        dst_l, prev_l, next_l = (
            coef[:].rearrange("p t k -> p (t k)")[0:LINES, i * HALVES * P:(i + 1) * HALVES * P].bitcast(i32)
            .rearrange("l (f e) -> l f e", f=HALVES) for i in range(3))
        ring_all = sb("ring_all", [P, X_RING, TILE_GROUP, D])
        ring_a = [ring_all[:, r] for r in range(X_RING)]
        ring_b = [sb(f"ring_b{r}", [P, TILE_GROUP, D]) for r in range(3)]
        idx_a = [sb(f"idx_a{r}", [P, TILE_GROUP], i32) for r in range(3)]
        idx_b = [sb(f"idx_b{r}", [P, TILE_GROUP], i32) for r in range(3)]
        pos_in = [sb(f"pos_in{r}", [P, TILE_GROUP], i32) for r in range(2)]
        xn = sb("xn", [P, 2 * TILE_GROUP, D])
        aT = sb("aT", [P, CHUNK])
        bT = sb("bT", [P, CHUNK])
        hd_pair = sb("hd_pair", [P, 2, CHUNK])
        hd_out = [hd_pair[:, r, :] for r in range(2)]
        y_sb = [sb(f"y_sb{r}", [P, TILE_GROUP, D]) for r in range(2)]
        x1_sb = [sb(f"x1_sb{r}", [P, TILE_GROUP, D]) for r in range(2)]
        h_sb = [sb(f"h_sb{r}", [P, TILE_GROUP, D]) for r in range(2)]
        coef_st = [sb(f"coef_st{r}", [P, TILE_GROUP, 4 * HEADS]) for r in range(2)]
        coef_parts = [sb(f"coef_parts{r}", [P, TILE_GROUP, PARTS * 4 * HEADS], bf16) for r in range(2)]
        coef_wide = sb("coef_wide", [P, TILE_GROUP, 4 * HEADS])
        coefT = sb("coefT", [4 * HEADS, CHUNK])
        coefT_bf = sb("coefT_bf", [PARTS * 4 * HEADS, CHUNK], bf16)
        pv = sb("pv", [P, CHUNK])
        run_pair = sb("run_pair", [P, 2, CHUNK])
        run_sum = [run_pair[:, r, :] for r in range(2)]
        relus = [(aT, bT), (run_pair[:, 0, :], run_pair[:, 1, :])]
        turned = [(aT, bT), tuple(y[:].rearrange("p t d -> p (t d)") for y in y_sb)]
        o_pair = sb("o_pair", [P, 2, CHUNK])
        o_sb = [o_pair[:, r, :] for r in range(2)]
        tz_pair = sb("tz_pair", [P, 2, CHUNK])
        t_sb = tz_pair[:, 0, :]
        own_sb = [tz_pair[:, r, :] for r in range(2)]
        STATS = 3 * TILE_GROUP
        stats = sb("stats", [P, STATS, 6])
        mean = sb("mean", [P, STATS])
        gap = sb("gap", [P, STATS])
        var_e = sb("var_e", [P, 16])
        rstd = sb("rstd", [P, 16])
        nwt = sb("nwt", [P, 16])
        h_scale = sb("h_scale", [P, 2, TILE_GROUP])
        h_shift = sb("h_shift", [P, 2, TILE_GROUP])
        squares = sb("squares", [P, 2, ROWS])
        KH = HEADS * HALVES
        SL = ring_all[:, 0:4].rearrange("p r t d -> p (r t) d")[0:LINES]
        def lines_in(pair):
            return pair.rearrange("p a b -> p (a b)")[0:LINES, :].rearrange("l (k e) -> l k e", e=P)
        ML = lines_in(xn[:, :, :])
        AL = lines_in(tz_pair[:, :, :])
        PL = lines_in(o_pair[:, :, :])
        DL = lines_in(hd_pair[:, :, :])
        C1 = lines_in(run_pair[:, :, :])
        C2 = SL[:, KH:2 * KH, :]
        carry_l = sb("carry_l", [LINES, HALVES * HEADS])
        row_f, row_w = pv[0:HEADS, 0:TILES], pv[0:HEADS, TILES:2 * TILES]
        row_a, row_pen = coefT[0:HEADS, 0:TILES], coefT[0:HEADS, TILES:2 * TILES]
        opened = aT[0:HEADS, 0:TILES + 1]
        pos_none = V[0:125, E_PAD - N // 125:E_PAD]
        BW = ROWS * D
        node_x = [V[:, r * BW:(r + 1) * BW].rearrange("p (t d) -> p t d", d=D) for r in range(NODE_RING)]
        node_y = [V[:, r * BW:(r + 1) * BW].rearrange("p (t d) -> p t d", d=D)
                  for r in range(NODE_RING, 2 * NODE_RING)]
        node_junk = V[:, 2 * NODE_RING * BW:(2 * NODE_RING + 1) * BW].rearrange("p (t d) -> p t d", d=D)

        bank = [ctx.enter_context(nc.psum_tensor(f"bank{i}", [P, 512], f32)) for i in range(8)]

        def tile_of(b, t):
            return bank[b][:, t * P:(t + 1) * P]

        def wide_tile(par, t):
            b, at = 4 + 2 * par + t // 2, (t % 2) * (D + 2 * HEADS)
            return bank[b][:, at:at + D + 2 * HEADS]

        def rows_of(b):
            return bank[b][:, :].rearrange("p (t d) -> p t d", t=TILE_GROUP)

        def node_tiles(par):
            return [tile_of(2 + 2 * par + t // TILE_GROUP, t % TILE_GROUP) for t in range(ROWS)]

        loaded = sem("loaded")
        att_zero, att_loaded = sem("att_zero"), sem("att_loaded")
        wT_done, wT_copied, watt_done = sem("wT_done"), sem("wT_copied"), sem("watt_done")
        weights_ready, index_ready = sem("weights_ready"), sem("index_ready")
        pos_fill, pos_clear = sem("pos_fill"), sem("pos_clear")
        zero_rows, zeroed = sem("zero_rows"), sem("zeroed")
        staged = sem("staged")
        pool_seen, sync_seen, vector_seen = sem("pool_seen"), sem("sync_seen"), sem("vector_seen")
        pos_put, pos_got = sems("pos_put", 2), sems("pos_got", 2)
        pos_copied, pos_ready, hop1_ready = sem("pos_copied"), sem("pos_ready"), sem("hop1_ready")
        step = sem("step")
        nx_in = sems("nx_in", NODE_RING)
        nn_norm, nn_T, nn_relu, nn_h = sem("nn_norm"), sem("nn_T"), sem("nn_relu"), sem("nn_h")
        nn_sq, nn_read = sem("nn_sq"), sem("nn_read")
        nn_y, nn_gelu, nn_out = sem("nn_y"), sem("nn_gelu"), sem("nn_out")
        nn_stored = sems("nn_stored", NODE_RING)
        xs_in, xd_in = sems("xs_in", X_RING), sems("xd_in", 3)
        l_sq, l_read, l_p = sem("l_sq"), sem("l_read"), sem("l_p")
        l_norm, l_T, l_relu, l_h = sem("l_norm"), sem("l_T"), sem("l_relu"), sem("l_h")
        l_hd, l_y, l_gelu, l_n, l_own = sem("l_hd"), sem("l_y"), sem("l_gelu"), sem("l_n"), sem("l_own")
        xd_stored, hd_stored, own_stored = sems("xd_stored", 3), sems("hd_stored", 2), sems("own_stored", 2)
        gx_in, gh_in = sems("gx_in", X_RING), sems("gh_in", 2)
        g_sq, g_read = sem("g_sq"), sem("g_read")
        g_staged, g_cT, g_cTs, g_bc, g_o = sem("g_staged"), sem("g_cT"), sem("g_cTs"), sem("g_bc"), sem("g_o")
        g_u, g_y, g_gelu, g_x1, g_n = sem("g_u"), sem("g_y"), sem("g_gelu"), sem("g_x1"), sem("g_n")
        g_h, g_hT, g_hTs, g_q, g_done = sem("g_h"), sem("g_hT"), sem("g_hTs"), sem("g_q"), sem("g_done")
        x1_stored, h1_stored = sems("x1_stored", 2), sems("h1_stored", 2)
        hs_in, ea_in = sems("hs_in", 2), sems("ea_in", 2)
        h_staged, h_T, h_Ts, h_v, h_q = sem("h_staged"), sem("h_T"), sem("h_Ts"), sem("h_v"), sem("h_q")
        h_vs, h_z, h_sc, h_scs = sem("h_vs"), sem("h_z"), sem("h_sc"), sem("h_scs")
        k_staged, k_bc, k_h, k_T, k_done = sem("k_staged"), sem("k_bc"), sem("k_h"), sem("k_T"), sem("k_done")
        k_stored, x1_in, put_done = sems("k_stored", 2), sems("x1_in", 2), sems("put_done", 2)
        p2 = {n: sem(f"p2_{n}") for n in ("lines", "local", "rows", "opened", "carried", "args", "exp", "den",
                                          "drows", "dopened", "dcarried", "args2", "exp2", "coef", "back", "done")}
        LOADS = 21
        K_BANKS = (0, 4)
        HOP_BANKS = (0, 5)

        def prev(slot, use):
            return 1 - slot, use - (1 if slot == 0 else 0)

        block = ctx.enter_context(nc.Block())

        @block.sync
        def _(sp):
            for dst, src in ((ident, ident_in), (sel, sel_in), (w_sb, W), (bq_sb, bq), (bn_sb, bn), (be_sb, be),
                             (attn_sb, attn), (src_i, src_tiles), (dst_i, dst_tiles), (next_i, next_tiles),
                             (edge_i, edge_ids), (dst_l, dst_lines), (prev_l, prev_lines), (next_l, next_lines)):
                sp.dma_start(dst[:], src).then_inc(loaded, 16)
            for dst, src in ((bias_bc, bias), (gamma_bc, gamma), (beta_bc, beta)):
                sp.dma_start(dst[:], src.to_broadcast([P, D])).then_inc(loaded, 16)
            for dst, src in ((wq_sb, Wq), (wn_sb, Wn), (we_sb, We)):
                sp.dma_start(dst[:], src.rearrange("i k f -> k i f")).then_inc(loaded, 16)
            sp.wait_ge(att_zero, 1)
            part = D // HEADS
            for s in range(2):
                for h in range(HEADS):
                    sp.dma_start(att_sb[part * h:part * (h + 1), s * HEADS + h:s * HEADS + h + 1],
                                 att[s, h, :].unsqueeze(1)).then_inc(att_loaded, 16)
            sp.wait_ge(pos_fill, 1)
            sp.dma_start(pos_table.rearrange("(p c) o -> p (c o)", p=125),
                         pos_none.bitcast(i32)).then_inc(pos_clear, 16)
            sp.wait_ge(zero_rows, 1)
            for t in h_tables[1:]:
                sp.dma_start(t[E_PAD:E_PAD + P, :], y_sb[0][:, 0, :]).then_inc(zeroed, 16)
            for s in (*nn_stored, *hd_stored, *own_stored, *x1_stored, *h1_stored):
                sp.sem_inc(s, 16)

            whole = (BLOCKS - 1) * BLOCK
            x_blocks = x[0:whole, :].rearrange("(b p r) d -> b p r d", p=P, r=ROWS)
            out_blocks = out[0:whole, :].rearrange("(b p r) d -> b p r d", p=P, r=ROWS)

            def node_store(n, slot):
                sp.wait_ge(nn_out, n + 1)
                sp.dma_start(out_blocks[n], node_y[slot]).then_inc(nn_stored[slot], 16)

            def node_turn(n, slot, use):
                sp.wait_ge(nn_out, n - NODE_RING + 1)
                sp.dma_start(node_x[slot], x_blocks[n]).then_inc(nx_in[slot], 16)
                node_store(n - NODE_RING, slot)
            for n in range(NODE_RING):
                sp.dma_start(node_x[n], x_blocks[n]).then_inc(nx_in[n], 16)
            visits(sp, NODE_RING, BLOCKS - 1, NODE_RING, node_turn)
            n = BLOCKS - 1
            sp.wait_ge(nn_out, n - NODE_RING + 1)
            sp.dma_start(node_x[n % NODE_RING][0:LAST_BLOCK_PARTS],
                         x[whole:N, :].rearrange("(p r) d -> p r d", r=ROWS)).then_inc(nx_in[n % NODE_RING], 16)
            for m in range(n - NODE_RING, n):
                node_store(m, m % NODE_RING)
            sp.wait_ge(nn_out, n + 1)
            sp.dma_start(out[whole:N, :].rearrange("(p r) d -> p r d", r=ROWS),
                         node_y[n % NODE_RING][0:LAST_BLOCK_PARTS]).then_inc(nn_stored[n % NODE_RING], 16)

            def store_own(n, slot):
                sp.wait_ge(l_own, n + 1)
                sp.dma_start(own_chunks[n], h_sb[slot][:]).then_inc(own_stored[slot], 16)

            def store_x(n, slot, use):
                trio, trio_use = of_three(slot, use)
                sp.wait_ge(xd_in[trio], 64 * (trio_use + 1))
                sp.dma_start(xd_chunks[n], ring_b[trio][:]).then_inc(xd_stored[trio], 16)

            def store_hd(n, slot):
                sp.wait_ge(l_hd, n + 1)
                sp.dma_start(hd_chunks[n], hd_out[slot][:]).then_inc(hd_stored[slot], 16)

            def keep_turn(n, slot, use):
                store_x(n, slot, use)
                store_hd(n - 2, slot % 2)
                store_own(n - 4, slot % 2)
            for n in range(4):
                store_x(n, n, 0)
                if n >= 2:
                    store_hd(n - 2, n % 2)
            visits(sp, 4, CHUNKS, X_RING, keep_turn)
            for n in (CHUNKS - 2, CHUNKS - 1):
                store_hd(n, n % 2)
                store_own(n - 2, n % 2)
            store_own(CHUNKS - 2, 0)
            store_own(CHUNKS - 1, 1)

            for r in range(3):
                sp.wait_ge(xd_stored[r], 16 * len(range(r, CHUNKS, 3)))
            for r in range(2):
                sp.wait_ge(hd_stored[r], 16 * (CHUNKS // 2 + 1))
            sp.wait_ge(p2["done"], 1)

            def sums_load(n, slot, pair_slot):
                sp.dma_start(ring_a[slot], xd_chunks[n]).then_inc(gx_in[slot], 16)
                sp.dma_start(hd_out[pair_slot], hd_chunks[n]).then_inc(gh_in[pair_slot], 16)

            def sums_store(n, slot):
                sp.wait_ge(g_x1, n + 1)
                sp.dma_start(x1_chunks[n], x1_sb[slot][:]).then_inc(x1_stored[slot], 16)
                sp.wait_ge(g_h, n + 1)
                sp.dma_start(h_chunks[0][n], h_sb[slot][:]).then_inc(h1_stored[slot], 16)

            def sums_turn(n, slot, use):
                sp.wait_ge(g_o, n - 1)
                sp.sem_inc(sync_seen, 1)
                sp.wait_ge(g_x1, n - X_RING + 1)
                sp.sem_inc(sync_seen, 1)
                sums_load(n, slot, slot % 2)
                sums_store(n - 4, slot % 2)
            for n in range(X_RING):
                if n >= 2:
                    sp.wait_ge(g_o, n - 1)
                sums_load(n, n, n % 2)
                if n >= 4:
                    sums_store(n - 4, n % 2)
            visits(sp, X_RING, CHUNKS, X_RING, sums_turn)
            for n in range(CHUNKS - 4, CHUNKS):
                sums_store(n, n % 2)

            chunk_full = E // CHUNK
            at = chunk_full * CHUNK
            tiles_full, rest = (E - at) // P, (E - at) % P
            edge_chunks = edge_attr[0:at, :].rearrange("(c t p) d -> c p t d", t=TILE_GROUP, p=P)
            for hop in range(HOPS):
                base, uses = hop * CHUNKS, hop * CHUNKS // 2
                if hop:
                    sp.wait_ge(h_T, base)
                for n in range(CHUNKS - chunk_full):
                    if CHUNKS - 1 - n > chunk_full:
                        sp.sem_inc(ea_in[n % 2], 32)
                        continue
                    sp.dma_start(ring_b[n % 2][:, 0:tiles_full, :],
                                 edge_attr[at:at + tiles_full * P, :].rearrange("(t p) d -> p t d", p=P)
                                 ).then_inc(ea_in[n % 2], 16)
                    sp.dma_start(ring_b[n % 2][0:rest, tiles_full, :],
                                 edge_attr[at + tiles_full * P:E, :]).then_inc(ea_in[n % 2], 16)

                def edge_load(n, slot, use):
                    sp.wait_ge(h_T, base + n - 1)
                    sp.sem_inc(sync_seen, 1)
                    sp.dma_start(ring_b[slot][:], edge_chunks[CHUNKS - 1 - n]).then_inc(ea_in[slot], 32)
                visits(sp, CHUNKS - chunk_full, CHUNKS, 2, edge_load)

                if hop < HOPS - 1:
                    def store(n, slot, use):
                        sp.wait_ge(k_done, base + n + 1)
                        sp.dma_start(h_chunks[hop + 1][n], h_sb[slot][:]).then_inc(k_stored[slot], 16)
                    visits(sp, 0, CHUNKS, 2, store)
                else:
                    for r in range(2):
                        sp.wait_ge(x1_stored[r], 16 * (CHUNKS // 2 + 1))
                        sp.dma_start(x1_sb[r][:], x1_chunks[r]).then_inc(x1_in[r], 16)

                    def x1_load(n, slot, use):
                        sp.wait_ge(k_done, base + n - 1)
                        sp.dma_start(x1_sb[slot][:], x1_chunks[n]).then_inc(x1_in[slot], 16)
                    visits(sp, 2, CHUNKS, 2, x1_load)
            for r in range(NODE_RING):
                sp.wait_ge(nn_stored[r], 16 * (len(range(r, BLOCKS, NODE_RING)) + 1))
            for r in range(2):
                sp.wait_ge(own_stored[r], 16 * (CHUNKS // 2 + 1))
                sp.wait_ge(h1_stored[r], 16 * (CHUNKS // 2 + 1))
                sp.wait_ge(k_stored[r], 16 * (HOPS - 1) * CHUNKS // 2)
                sp.wait_ge(pos_put[r], 64 * (CHUNKS // 2))
                sp.wait_ge(put_done[r], 64 * (CHUNKS // 2))
            sp.wait_ge(pos_clear, 16)
            sp.wait_ge(zeroed, 32)

        @block.gpsimd
        def _(pool):
            def wait_count(s, value):
                pool.wait_ge(s, value)
                pool.sem_inc(pool_seen, 1)

            def stage(dst, cols_of):
                nc.gpsimd.tensor_copy(dst[:], cols_of).then_inc(staged, 1)

            def gather(dst_of_tile, table, index, done):
                for t in range(TILE_GROUP):
                    pool.indirect_dma_start(out=dst_of_tile(t), out_offset=None, in_=table,
                                            in_offset=bass.IndirectOffsetOnAxis(ap=index[:, t:t + 1], axis=0)
                                            ).then_inc(done, 16)

            def scatter(table, index, src_of_tile, done):
                for t in range(TILE_GROUP):
                    pool.indirect_dma_start(out=table, in_=src_of_tile(t), in_offset=None, bounds_check=N - 1,
                                            out_offset=bass.IndirectOffsetOnAxis(ap=index[:, t:t + 1], axis=0),
                                            oob_is_err=False).then_inc(done, 16)

            def cols(array, n):
                return array[:, bass.ts(n, TILE_GROUP)]

            pool.wait_ge(index_ready, 1)
            pool.wait_ge(pos_clear, 16)

            def put_pos(n, slot, use):
                stage(pos_in[slot], cols(edge_i, n))
                stage(idx_a[slot], cols(put_i, n))
                pool.wait_ge(staged, 2)
                scatter(pos_table, idx_a[slot], lambda t: pos_in[slot][:, t:t + 1], pos_put[slot])
                pool.sem_clear(staged)

            def put_pos_again(n, slot, use):
                wait_count(pos_put[slot], 64 * use)
                put_pos(n, slot, use)
            put_pos(0, 0, 0)
            put_pos(1, 1, 0)
            visits(pool, 2, CHUNKS, 2, put_pos_again)
            for r in range(2):
                pool.wait_ge(pos_put[r], 64 * (CHUNKS // 2))

            def get_pos(n, slot, use):
                stage(idx_a[slot], cols(src_i, n))
                pool.wait_ge(staged, 1)
                gather(lambda t: pos_in[slot][:, t:t + 1], pos_table, idx_a[slot], pos_got[slot])
                pool.sem_clear(staged)

            def copy_pos(n, slot, use):
                wait_count(pos_got[slot], 64 * (use + 1))
                nc.gpsimd.tensor_copy(cols(pos_i, n), pos_in[slot][:]).then_inc(pos_copied, 1)
                wait_count(pos_copied, n + 1)

            def pos_turn(n, slot, use):
                get_pos(n, slot, use)
                copy_pos(n - 1, *prev(slot, use))
            get_pos(0, 0, 0)
            visits(pool, 1, CHUNKS, 2, pos_turn)
            copy_pos(CHUNKS - 1, 1, CHUNKS // 2 - 1)
            pool.sem_inc(pos_ready, 1)

            def get_x(n, slot, use):
                trio = slot % 3
                stage(idx_a[trio], cols(src_i, n))
                stage(idx_b[trio], cols(recv_i, n))
                pool.wait_ge(staged, 2)
                gather(lambda t: ring_a[slot][:, t, :], x, idx_a[trio], xs_in[slot])
                gather(lambda t: ring_b[trio][:, t, :], x, idx_b[trio], xd_in[trio])
                pool.sem_clear(staged)

            def get_x_again(n, slot, use):
                trio, trio_use = of_three(slot, use)
                wait_count(l_norm, n - 2)
                wait_count(xd_stored[trio], 16 * trio_use)
                wait_count(l_n, n - X_RING + 1)
                get_x(n, slot, use)
            for n in range(X_RING):
                if n >= 3:
                    pool.wait_ge(l_norm, n - 2)
                    pool.wait_ge(xd_stored[n % 3], 16 * (n // 3))
                get_x(n, n, 0)
            visits(pool, X_RING, CHUNKS, X_RING, get_x_again)

            pool.wait_ge(p2["done"], 1)

            def stage_coef(n, slot):
                rest, K = coef_st[slot], 4 * HEADS
                stage(rest, coef[:, bass.ts(n, TILE_GROUP), :])
                pool.wait_ge(staged, 1)
                for i in range(PARTS):
                    part = coef_parts[slot][:, :, i * K:(i + 1) * K]
                    if i == PARTS - 1:
                        nc.gpsimd.tensor_copy(part, rest[:]).then_inc(g_staged, 1)
                        break
                    nc.gpsimd.tensor_copy(part, rest[:]).then_inc(staged, 1)
                    pool.wait_ge(staged, 3 * i + 2)
                    nc.gpsimd.tensor_copy(coef_wide[:], part).then_inc(staged, 1)
                    pool.wait_ge(staged, 3 * i + 3)
                    nc.gpsimd.tensor_tensor(rest[:], rest[:], coef_wide[:], ALU.subtract).then_inc(staged, 1)
                    pool.wait_ge(staged, 3 * i + 4)
                pool.sem_clear(staged)

            def stage_coef_again(n, slot, use):
                wait_count(g_cT, n - 1)
                stage_coef(n, slot)
            stage_coef(0, 0)
            stage_coef(1, 1)
            visits(pool, 2, CHUNKS, 2, stage_coef_again)

            for hop in range(HOPS):
                base, uses = hop * CHUNKS, hop * CHUNKS // 2
                if hop == 0:
                    pool.wait_ge(hop1_ready, 1)
                    pool.wait_ge(zeroed, 32)
                for r in range(2):
                    if hop == 0:
                        pool.wait_ge(h1_stored[r], 16 * (CHUNKS // 2 + 1))
                        pool.wait_ge(own_stored[r], 16 * (CHUNKS // 2 + 1))
                    else:
                        pool.wait_ge(k_stored[r], 16 * uses)
                index = hop1_i if hop == 0 else pos_i

                def get_h(n, slot, use):
                    c = CHUNKS - 1 - n
                    nc.gpsimd.tensor_copy(coef_st[slot][:, :, 0], cols(inner_t, c)).then_inc(h_staged, 1)
                    stage(idx_a[slot], cols(index, c))
                    pool.wait_ge(staged, 1)
                    gather(lambda t: ring_a[slot][:, t, :], h_tables[hop], idx_a[slot], hs_in[slot])
                    pool.sem_clear(staged)

                def get_h_again(n, slot, use):
                    wait_count(h_T, base + n - 1)
                    get_h(n, slot, use)
                get_h(0, 0, 0)
                get_h(1, 1, 0)
                visits(pool, 2, CHUNKS, 2, get_h_again)

                pool.wait_ge(p2["done"], hop + 2)

                def stage_hop_coef(n, slot):
                    nc.gpsimd.tensor_copy(coef_st[slot][:, :, 0:3],
                                          coef[:, bass.ts(n, TILE_GROUP), 0:3]).then_inc(k_staged, 1)

                def stage_hop_coef_again(n, slot, use):
                    wait_count(k_bc, base + n - 1)
                    stage_hop_coef(n, slot)

                if hop < HOPS - 1:
                    stage_hop_coef(0, 0)
                    stage_hop_coef(1, 1)
                    visits(pool, 2, CHUNKS, 2, stage_hop_coef_again)
                    continue
                for r in range(NODE_RING):
                    pool.wait_ge(nn_stored[r], 16 * (len(range(r, BLOCKS, NODE_RING)) + 1))

                def put_out(n, slot):
                    stage(idx_a[slot], cols(put_i, n))
                    pool.wait_ge(staged, 1)
                    wait_count(k_done, base + n + 1)
                    scatter(out, idx_a[slot], lambda t: h_sb[slot][:, t, :], put_done[slot])
                    pool.sem_clear(staged)

                stage_hop_coef(0, 0)
                stage_hop_coef(1, 1)
                for n in (2, 3):
                    stage_hop_coef_again(n, n % 2, 1)
                    put_out(n - 2, n % 2)

                def last_turns(n, slot, use):
                    stage_hop_coef_again(n, slot, use)
                    wait_count(put_done[slot], 64 * (use - 1))
                    put_out(n - 2, slot)
                visits(pool, 4, CHUNKS, 2, last_turns)
                for n in (CHUNKS - 2, CHUNKS - 1):
                    pool.wait_ge(put_done[n % 2], 64 * (CHUNKS // 2 - 1))
                    put_out(n, n % 2)

        @block.scalar
        def _(act):
            def copy(dst, src):
                return nc.scalar.activation(dst, src, ACT.Copy)

            def h_of(pair):
                for t in range(TILE_GROUP):
                    last = nc.scalar.activation(h_sb[pair][:, t, :], x1_sb[pair][:, t, :], ACT.Relu,
                                                bias=h_shift[:, pair, t:t + 1], scale=h_scale[:, pair, t:t + 1])
                return last

            def squares_of(tiles, junk, par):
                for t, src in enumerate(tiles):
                    last = nc.scalar.activation(junk[:, t, :], src, ACT.Square, accum_out=squares[:, par, t:t + 1])
                return last

            def node_relu(n):
                act.wait_ge(nn_T, n + 1)
                nc.scalar.activation(aT[:], bank[0][:, :], ACT.Relu).then_inc(nn_relu, 1)
                nc.scalar.activation(bT[:], bank[1][:, :], ACT.Relu).then_inc(nn_relu, 1)

            def node_squares(n, par):
                act.wait_ge(nn_h, n + 1)
                squares_of(node_tiles(par), node_junk, par).then_inc(nn_sq, 1)

            def node_gelu(n, slot):
                act.wait_ge(nn_y, n + 1)
                nc.scalar.activation(node_y[slot], node_y[slot], ACT.Gelu).then_inc(nn_gelu, 1)

            def node_turn(n, slot, use):
                node_relu(n)
                node_gelu(n - 2, (slot - 2) % NODE_RING)
                node_squares(n, slot % 2)
            for n in range(2):
                node_relu(n)
                node_squares(n, n)
            visits(act, 2, BLOCKS, NODE_RING, node_turn)
            for n in (BLOCKS - 2, BLOCKS - 1):
                node_gelu(n, n % NODE_RING)

            act.wait_ge(pos_clear, 16)
            for r in range(NODE_RING):
                act.wait_ge(nn_stored[r], 16 * (len(range(r, BLOCKS, NODE_RING)) + 1))
            pv_tiles = pv[:].rearrange("p (t d) -> p t d", d=D)

            def l_relu_x(n, par):
                act.wait_ge(l_T, n + 1)
                nc.scalar.activation(relus[par][0][:], bank[0][:, :], ACT.Relu)
                nc.scalar.activation(relus[par][1][:], bank[1][:, :], ACT.Relu).then_inc(l_relu, 1)

            def l_values(n, pair, pair_use):
                act.wait_ge(l_h, n + 1)
                act.wait_ge(hd_stored[pair], 16 * (pair_use + 1))
                copy(V[:, bass.ts(n, CHUNK)], bank[2][:, :])
                copy(hd_out[pair], bank[3][:, :]).then_inc(l_hd, 1)

            def l_squares(n, par):
                act.wait_ge(l_p, n + 1)
                squares_of([wide_tile(par, t)[:, 0:D] for t in range(TILE_GROUP)], pv_tiles, par)
                for g in range(2):
                    wide = bank[4 + 2 * par + g][:, 0:2 * (D + 2 * HEADS)].rearrange("p (t k) -> p t k", t=2)
                    last = copy(scores[:, bass.ts(n * 2 + g, 2), :], wide[:, :, D:D + 2 * HEADS])
                last.then_inc(l_sq, 1)

            def l_gelu_of(n, pair):
                act.wait_ge(l_y, n + 1)
                nc.scalar.activation(y_sb[pair][:], y_sb[pair][:], ACT.Gelu).then_inc(l_gelu, 1)

            def l_relu_of(n, pair):
                act.wait_ge(l_n, n + 1)
                h_of(pair).then_inc(l_own, 1)

            def l_turn(n, slot, use, earlier=3):
                pair, pair_use = of_two(slot, use)
                if earlier >= 2:
                    l_gelu_of(n - 2, pair)
                l_relu_x(n, pair)
                if earlier >= 1:
                    l_values(n - 1, *prev(pair, pair_use))
                l_squares(n, pair)
                if earlier >= 3:
                    l_relu_of(n - 3, 1 - pair)
            for n in range(3):
                l_turn(n, n, 0, n)
            visits(act, 3, CHUNKS, X_RING, l_turn)
            l_values(CHUNKS - 1, 1, CHUNKS // 2 - 1)
            l_gelu_of(CHUNKS - 2, 0)
            l_relu_of(CHUNKS - 3, 1)
            l_gelu_of(CHUNKS - 1, 1)
            l_relu_of(CHUNKS - 2, 0)
            l_relu_of(CHUNKS - 1, 1)

            def softmax_exps(run, heads):
                K = heads * HALVES
                act.wait_ge(p2["args"], run + 1)
                nc.scalar.activation(AL[:, 0:K], AL[:, 0:K], ACT.Exp)
                nc.scalar.activation(row_a[0:heads], row_a[0:heads], ACT.Exp)
                nc.scalar.activation(PL[:, 0:K], PL[:, 0:K], ACT.Exp).then_inc(p2["exp"], 1)
                if run == 0:
                    act.wait_ge(p2["args2"], 1)
                    nc.scalar.activation(C1[:, 0:K], C1[:, 0:K], ACT.Exp)
                    nc.scalar.activation(C2[:, 0:K], C2[:, 0:K], ACT.Exp).then_inc(p2["exp2"], 1)
            softmax_exps(0, HEADS)

            def g_coef(n):
                act.wait_ge(g_cT, n + 1)
                copy(coefT_bf[:], bank[0][0:PARTS * 4 * HEADS, :]).then_inc(g_cTs, 1)

            def g_squares(n, par):
                act.wait_ge(g_u, n + 1)
                squares_of([tile_of(5, t) for t in range(TILE_GROUP)], xn[:, 0:TILE_GROUP, :],
                           par).then_inc(g_sq, 1)

            def g_gelu_of(n, pair):
                act.wait_ge(g_y, n + 1)
                nc.scalar.activation(y_sb[pair][:], y_sb[pair][:], ACT.Gelu).then_inc(g_gelu, 1)

            def g_rows(n, pair):
                act.wait_ge(g_n, n + 1)
                h_of(pair).then_inc(g_h, 1)
                act.wait_ge(g_hT, n + 1)
                copy(aT[:], bank[6][:, :]).then_inc(g_hTs, 1)

            def g_queries(n):
                act.wait_ge(g_q, n + 1)
                copy(V[:, bass.ts(n, CHUNK)], bank[7][:, ::-1]).then_inc(g_done, 1)

            def g_turn(n, slot, use, earlier=3):
                g_coef(n + 1)
                if earlier >= 1:
                    g_gelu_of(n - 1, 1 - slot)
                if earlier >= 3:
                    g_queries(n - 3)
                g_squares(n, slot)
                if earlier >= 2:
                    g_rows(n - 2, slot)
            g_coef(0)
            for n in range(3):
                g_turn(n, n % 2, 0, n)
            visits(act, 3, CHUNKS - 1, 2, g_turn)
            g_gelu_of(CHUNKS - 2, 0)
            g_squares(CHUNKS - 1, 1)
            g_queries(CHUNKS - 4)
            g_rows(CHUNKS - 3, 1)
            g_gelu_of(CHUNKS - 1, 1)
            g_queries(CHUNKS - 3)
            g_rows(CHUNKS - 2, 0)
            g_queries(CHUNKS - 2)
            g_rows(CHUNKS - 1, 1)
            g_queries(CHUNKS - 1)

            for hop in range(HOPS):
                base, uses = hop * CHUNKS, hop * CHUNKS // 2

                def h_copies(n, slot):
                    act.wait_ge(h_T, base + n + 1)
                    for i in range(2):
                        last = copy(turned[slot][i][:], bank[HOP_BANKS[slot] + i][:, :])
                    last.then_inc(h_Ts, 1)

                def h_values(n):
                    act.wait_ge(h_v, base + n + 1)
                    act.wait_ge(h_q, base + n + 1)
                    nc.scalar.activation(V[:, bass.ts(CHUNKS - 1 - n, CHUNK)], bank[3][:, :], ACT.Identity,
                                         bias=v_bias[:, hop:hop + 1]).then_inc(h_vs, 1)

                def h_scores(n):
                    act.wait_ge(h_sc, base + n + 1)
                    copy(scores[:, bass.ts(CHUNKS - 1 - n, TILE_GROUP), 0], bank[4][:, 0:TILE_GROUP]).then_inc(h_scs, 1)

                def h_turn(n, slot, use):
                    h_copies(n, slot)
                    h_values(n - 1)
                    h_scores(n - 2)
                h_copies(0, 0)
                h_copies(1, 1)
                h_values(0)
                visits(act, 2, CHUNKS, 2, h_turn)
                h_values(CHUNKS - 1)
                h_scores(CHUNKS - 2)
                h_scores(CHUNKS - 1)
                softmax_exps(hop + 1, 1)

                if hop < HOPS - 1:
                    def k_out(n, slot):
                        act.wait_ge(k_T, base + n + 1)
                        copy(h_sb[slot][:], rows_of(3))
                        copy(V[:, bass.ts(n, CHUNK)], bank[7][:, ::-1]).then_inc(k_done, 1)

                    def k_out_again(n, slot, use):
                        act.wait_ge(k_stored[slot], 16 * (uses + use))
                        k_out(n, slot)
                    k_out(0, 0)
                    k_out(1, 1)
                    visits(act, 2, CHUNKS, 2, k_out_again)

        @block.vector
        def _(dve):
            steps = [0]

            def land(ins, meanwhile=None):
                steps[0] += 1
                at = steps[0]
                ins.then_inc(step, 1)
                if meanwhile is not None:
                    meanwhile()
                dve.wait_ge(step, at)

            def signal(ins, s):
                land(ins)
                dve.sem_inc(s, 1)

            def settle():
                steps[0] = 0
                dve.sem_clear(step)

            v = nc.vector

            def inverse_std(norms, sums=None, between=lambda i: None):
                w = norms + (0 if sums is None else sums.shape[1])
                va, r, t = var_e[:, 0:w], rstd[:, 0:w], nwt[:, 0:w]
                at = [0]

                def chain(ins):
                    land(ins, lambda: between(at[0]))
                    at[0] += 1
                if norms:
                    st = stats[:, 0:norms]
                    v.tensor_tensor(mean[:, 0:norms], st[:, :, 1], st[:, :, 4], ALU.add)
                    v.tensor_tensor(var_e[:, 0:norms], st[:, :, 2], st[:, :, 5], ALU.add)
                    chain(v.tensor_tensor(gap[:, 0:norms], st[:, :, 1], st[:, :, 4], ALU.subtract))
                    chain(v.tensor_tensor(gap[:, 0:norms], gap[:, 0:norms], gap[:, 0:norms], ALU.mult))
                    chain(v.scalar_tensor_tensor(out=var_e[:, 0:norms], in0=gap[:, 0:norms], scalar=D / 4.0,
                                                 in1=var_e[:, 0:norms], op0=ALU.mult, op1=ALU.add))
                    v.tensor_scalar(mean[:, 0:norms], mean[:, 0:norms], 0.5, None, ALU.mult)
                if sums is not None:
                    if norms:
                        v.tensor_scalar(var_e[:, 0:norms], var_e[:, 0:norms], 1.0 / D, EPS, ALU.mult, ALU.add)
                    chain(v.tensor_scalar(var_e[:, norms:w], sums, 1.0 / D, EPS, ALU.mult, ALU.add))
                else:
                    chain(v.tensor_scalar(va, va, 1.0 / D, EPS, ALU.mult, ALU.add))
                chain(v.tensor_scalar(r.bitcast(i32), va.bitcast(i32), 1, None, ALU.arith_shift_right))
                chain(v.tensor_scalar(r.bitcast(i32), r.bitcast(i32), -1.0, RSQRT_SEED, ALU.mult, ALU.add))
                for _ in range(3):
                    chain(v.scalar_tensor_tensor(out=t, in0=r, scalar=-0.5, in1=r, op0=ALU.mult, op1=ALU.mult))
                    chain(v.tensor_tensor(t, t, va, ALU.mult))
                    chain(v.scalar_tensor_tensor(out=r, in0=t, scalar=1.5, in1=r, op0=ALU.add, op1=ALU.mult))

            def h_norm(first, pair, done, keep=None):
                scale = h_scale[:, pair, :]
                if keep is None:
                    land(v.tensor_copy(scale, rstd[:, first:first + TILE_GROUP]))
                else:
                    land(v.tensor_tensor(scale, rstd[:, first:first + TILE_GROUP], keep, ALU.mult))
                v.scalar_tensor_tensor(out=h_shift[:, pair, :], in0=mean[:, first:first + TILE_GROUP], scalar=-1.0,
                                       in1=scale, op0=ALU.mult, op1=ALU.mult).then_inc(done, 1)

            def measure(first, tiles):
                for i, src in enumerate(tiles):
                    last = v.bn_stats(stats[:, first + i, :], src)
                land(last)

            def normalize(first, tiles, done):
                for i, (dst, src) in enumerate(tiles):
                    k = first + i
                    last = v.tensor_scalar(dst, src, mean[:, k:k + 1], rstd[:, k:k + 1], ALU.subtract, ALU.mult)
                signal(last, done)

            def scale_shift(y, tiles, first_r, read, done):
                for t, src in enumerate(tiles):
                    last = v.scalar_tensor_tensor(out=y[:, t, :], in0=src,
                                                  scalar=rstd[:, first_r + t:first_r + t + 1], in1=gamma_bc[:],
                                                  op0=ALU.mult, op1=ALU.mult)
                signal(last, read)
                signal(v.tensor_tensor(y, y, beta_bc[:].unsqueeze(1).to_broadcast([P, len(tiles), D]), ALU.add), done)

            signal(v.memset(att_sb[:], 0.0), att_zero)
            land(v.memset(w_att[:], 0.0))
            signal(v.memset(pos_none.bitcast(i32), E_PAD), pos_fill)
            signal(v.memset(y_sb[0][:], 0.0), zero_rows)
            land(v.memset(bias_rows[:], 0.0))
            land(v.memset(bias_ones[:], 0.0))
            for row in (0, 32, 64):
                land(v.memset(bias_ones[row:row + 1, :], 1.0))
            dve.wait_ge(loaded, 16 * LOADS - 16)
            land(v.tensor_copy(sel_bf[:], sel[:]))
            land(v.tensor_copy(ident_bf[:], ident[:]))
            land(v.tensor_scalar(middle[:], ident[:], -1.0 / D, None, ALU.add))
            land(v.tensor_reduce(row_mean[:, 0:1], w_sb[:], AX.X, ALU.add))
            land(v.tensor_reduce(row_mean[:, 1:2], bias_bc[:], AX.X, ALU.add))
            land(v.tensor_scalar(row_mean[:], row_mean[:], 1.0 / D, None, ALU.mult))
            land(v.tensor_scalar(w_mid[:], w_sb[:], row_mean[:, 0:1], None, ALU.subtract))
            land(v.tensor_scalar(bias_bc[:], bias_bc[:], row_mean[:, 1:2], None, ALU.subtract))
            for row in (0, 32, 64):
                part = bias_rows[row:row + 1, :, :]
                land(v.tensor_copy(part, bias_bc[row:row + 1, :].unsqueeze(1).to_broadcast([1, TILE_GROUP, D])))
                for below in range(row + 32, 65, 32):
                    land(v.tensor_copy(t_sb[below:below + 1, 0:D], bias_bc[below:below + 1, :]))
                    land(v.tensor_copy(z_bf[below:below + 1, :], bias_bc[below:below + 1, :]))
                    land(v.tensor_tensor(bias_bc[below:below + 1, :], t_sb[below:below + 1, 0:D],
                                         z_bf[below:below + 1, :], ALU.subtract))
            land(v.memset(bias_wide[:], 0.0))
            land(v.tensor_copy(bias_wide[:, :, 0:D], bias_rows[:, 0:2, :]))
            land(v.tensor_tensor(v_bias[:], bn_sb[:], be_sb[:], ALU.add))
            land(v.tensor_tensor(inner_t[:], next_i[:], dst_i[:], ALU.is_equal))
            land(v.tensor_scalar(last_t[:], inner_t[:], -1.0, 1.0, ALU.mult, ALU.add))
            land(v.scalar_tensor_tensor(out=put_i[:], in0=inner_t[:], scalar=float(SKIP), in1=dst_i[:],
                                        op0=ALU.mult, op1=ALU.add))
            signal(v.tensor_scalar(recv_i[:], dst_i[:], float(N - 1), None, ALU.min), index_ready)
            land(v.tensor_tensor(same_l[:], prev_l[:], dst_l[:], ALU.is_equal))
            land(v.tensor_scalar(pen_l[:], same_l[:], -1.0, -NONE, ALU.add, ALU.mult))
            land(v.tensor_tensor(last_l[:], next_l[:], dst_l[:], ALU.not_equal))
            land(v.tensor_reduce(whole_l[:], same_l[:], AX.X, ALU.min))
            dve.wait_ge(wT_done, 1)
            signal(v.tensor_copy(wT[:], tile_of(0, 0)), wT_copied)
            dve.wait_ge(watt_done, 1)
            H = HEADS
            land(v.tensor_copy(w_att[:, 0:H], bank[1][:, 0:H]))
            land(v.tensor_copy(w_att[:, 2 * H:4 * H], bank[1][:, 0:2 * H]))
            land(v.tensor_copy(w_att[:, 2 * H:3 * H], bank[1][:, H:2 * H]))
            land(v.tensor_tensor(w_att[:, 3 * H:4 * H], w_att[:, 0:H], w_att[:, 2 * H:3 * H], ALU.add))
            land(v.tensor_copy(w_wide[:, 0:D], w_mid[:]))
            land(v.tensor_copy(w_wide[:, D:D + 2 * H], w_att[:, 0:2 * H]))
            dve.sem_inc(weights_ready, 1)
            dve.wait_ge(zeroed, 32)
            settle()

            def node_sum(n, slot):
                dve.wait_ge(nn_gelu, n + 1)
                signal(v.tensor_tensor(node_y[slot], node_y[slot], node_x[slot], ALU.add), nn_out)

            def node_scale(n, slot, use, first_r):
                dve.wait_ge(nn_stored[slot], 16 * (use + 1))
                scale_shift(node_y[slot], node_tiles(slot % 2), first_r, nn_read, nn_y)

            def node_turn(n, slot, use, earlier=3, later=True):
                back3, back2, ahead = ((slot + k) % NODE_RING for k in (-3, -2, 1))

                def between(i):
                    if i >= 11 and earlier >= 3:
                        if i == 11:
                            dve.wait_ge(nn_gelu, n - 2)
                        two = slice(2 * (i - 11), 2 * (i - 11) + 2)
                        last = v.tensor_tensor(node_y[back3][:, two, :], node_y[back3][:, two, :],
                                               node_x[back3][:, two, :], ALU.add)
                        if i == 14:
                            last.then_inc(nn_out, 1)
                    if 4 <= i < 4 + ROWS and later:
                        v.bn_stats(stats[:, i - 4, :], node_x[ahead][:, i - 4, :])
                if later:
                    dve.wait_ge(nx_in[ahead], 16 * (use + (2 if slot == NODE_RING - 1 else 1)))
                if earlier >= 2:
                    dve.wait_ge(nn_sq, n - 1)
                inverse_std(ROWS, squares[:, slot % 2, :] if earlier >= 2 else None, between=between)
                if earlier >= 1:
                    dve.wait_ge(nn_T, n)
                normalize(0, [(xn[:, t, :], node_x[slot][:, t, :]) for t in range(ROWS)], nn_norm)
                if earlier >= 2:
                    node_scale(n - 2, back2, use - (1 if slot < 2 else 0), ROWS)
                settle()
            dve.wait_ge(nx_in[0], 16)
            measure(0, [node_x[0][:, t, :] for t in range(ROWS)])
            settle()
            for n in range(3):
                node_turn(n, n, 0, n)
            visits(dve, 3, BLOCKS - 1, NODE_RING, node_turn)
            n = BLOCKS - 1
            node_turn(n, n % NODE_RING, n // NODE_RING, later=False)
            for m in (n - 1, n):
                node_sum(m - 1, (m - 1) % NODE_RING)
                dve.wait_ge(nn_sq, m + 1)
                inverse_std(0, squares[:, m % 2, :])
                node_scale(m, m % NODE_RING, m // NODE_RING, 0)
                settle()
            node_sum(n, n % NODE_RING)
            settle()

            G = TILE_GROUP

            def tiles_of(a):
                return [a[:, t, :] for t in range(G)]

            def l_x1(n, slot, first=False):
                pair = slot % 2
                dve.wait_ge(l_gelu, n + 1)
                if not first:
                    dve.wait_ge(l_own, n - 1)
                land(v.tensor_tensor(x1_sb[pair][:], y_sb[pair][:], ring_a[slot], ALU.add))
                measure(2 * G, tiles_of(x1_sb[pair]))

            def l_scale(n, pair, first_r):
                scale_shift(y_sb[pair][:], [wide_tile(pair, t)[:, 0:D] for t in range(G)], first_r, l_read, l_y)

            def l_apply_x1(n, pair, pair_use):
                dve.wait_ge(own_stored[pair], 16 * (pair_use + 1))
                h_norm(2 * G, pair, l_n)

            def l_turn(n, slot, use, earlier=5, later=True):
                pair, pair_use = of_two(slot, use)
                ahead = (slot + 1) % X_RING
                if earlier >= 3:
                    l_x1(n - 3, (slot - 3) % X_RING, first=earlier < 5)

                def between(i):
                    if later and 4 <= i < 4 + 2 * G:
                        t = i - 4
                        v.bn_stats(stats[:, t, :], (tiles_of(ring_a[ahead]) + tiles_of(ring_b[ahead % 3]))[t])
                if later:
                    ahead_use = use + (1 if slot == X_RING - 1 else 0)
                    dve.wait_ge(xs_in[ahead], 64 * (ahead_use + 1))
                    dve.wait_ge(xd_in[ahead % 3], 64 * (of_three(ahead, ahead_use)[1] + 1))
                if earlier >= 2:
                    dve.wait_ge(l_sq, n - 1)
                norms = 3 * G if earlier >= 3 else 2 * G
                inverse_std(norms, squares[:, pair, 0:G] if earlier >= 2 else None, between=between)
                if earlier >= 1:
                    dve.wait_ge(l_T, n)
                sources = tiles_of(ring_a[slot]) + tiles_of(ring_b[slot % 3])
                normalize(0, [(xn[:, t, :], src) for t, src in enumerate(sources)], l_norm)
                if earlier >= 2:
                    l_scale(n - 2, pair, norms)
                if earlier >= 3:
                    l_apply_x1(n - 3, 1 - pair, pair_use - (2 if pair == 0 else 1))
                settle()
            dve.wait_ge(xs_in[0], 64)
            dve.wait_ge(xd_in[0], 64)
            measure(0, tiles_of(ring_a[0]) + tiles_of(ring_b[0]))
            settle()
            for n in range(5):
                l_turn(n, n, 0, n)
            visits(dve, 5, CHUNKS - 1, X_RING, l_turn)
            n = CHUNKS - 1
            l_turn(n, n % X_RING, n // X_RING, later=False)
            for m in range(CHUNKS, CHUNKS + 3):
                l_x1(m - 3, (m - 3) % X_RING)
                if m < CHUNKS + 2:
                    dve.wait_ge(l_sq, m - 1)
                    inverse_std(3 * G, squares[:, m % 2, 0:G])
                    l_scale(m - 2, m % 2, 3 * G)
                else:
                    inverse_std(3 * G)
                l_apply_x1(m - 3, (m - 3) % 2, (m - 3) // 2)
                settle()

            dve.wait_ge(pos_ready, 1)
            none = coef[:, :, 0]
            land(v.tensor_scalar(none, pos_i[:], float(E_PAD), None, ALU.is_ge))
            land(v.tensor_tensor(none, none, edge_i[:], ALU.mult))
            land(v.tensor_tensor(hop1_i[:], none, pos_i[:], ALU.add))
            dve.sem_inc(hop1_ready, 1)

            def softmax(run, heads):
                K = heads * HALVES
                SK = 2 * K if run == 0 else K

                def lines_bc(a):
                    return a[:].unsqueeze(1).to_broadcast([LINES, heads, HALVES, P])

                def by_head(a):
                    return a[:, 0:K].rearrange("l (h f) e -> l h f e", f=HALVES)

                dve.wait_ge(p2["lines"], run + 1)
                for b in range(-(-SK // 4)):
                    w = min(4, SK - 4 * b)
                    land(v.tensor_copy(SL[:, 4 * b:4 * b + w, :],
                                       bank[b][0:LINES, 0:w * P].rearrange("l (k e) -> l k e", e=P)))
                if run == 0:
                    land(v.scalar_tensor_tensor(out=SL[:], in0=SL[:], scalar=SLOPE, in1=SL[:],
                                                op0=ALU.mult, op1=ALU.max))
                for k in range(K):
                    last = v.tensor_tensor_scan(ML[:, k, :], pen_l[:, k % 2, :], SL[:, k, :], NONE, ALU.add, ALU.max)
                signal(last, p2["local"])
                dve.wait_ge(p2["rows"], run + 1)
                land(v.tensor_copy(row_f[0:heads], bank[4][0:heads, 0:TILES]))
                land(v.tensor_copy(row_w[0:heads], bank[4][0:heads, TILES:2 * TILES]))
                land(v.tensor_scalar(row_pen[0:heads], row_w[0:heads], -1.0, -NONE, ALU.add, ALU.mult))
                land(v.memset(opened[0:heads, 0:1], NONE))
                land(v.tensor_tensor_scan(opened[0:heads, 1:TILES + 1], row_pen[0:heads], row_f[0:heads], NONE,
                                          ALU.add, ALU.max))
                land(v.tensor_tensor(row_a[0:heads], opened[0:heads, 0:TILES], opened[0:heads, 1:TILES + 1],
                                     ALU.subtract))
                land(v.tensor_scalar(row_a[0:heads], row_a[0:heads], 0.0, None, ALU.min))
                dve.sem_inc(p2["opened"], 1)
                dve.wait_ge(p2["carried"], run + 1)
                land(v.tensor_copy(carry_l[:, 0:K], bank[5][0:LINES, 0:K]))
                for k in range(K):
                    h, f = k // 2, k % 2
                    last = v.tensor_tensor_scan(ML[:, k, :], pen_l[:, f, :], SL[:, k, :],
                                                carry_l[:, f * heads + h:f * heads + h + 1], ALU.add, ALU.max)
                land(last)
                for k in range(K):
                    h, f = k // 2, k % 2
                    last = v.tensor_copy(AL[:, k, 0:1], carry_l[:, f * heads + h:f * heads + h + 1])
                land(last)
                land(v.tensor_copy(AL[:, 0:K, 1:P], ML[:, 0:K, 0:P - 1]))
                land(v.tensor_tensor(AL[:, 0:K], AL[:, 0:K], ML[:, 0:K], ALU.subtract))
                land(v.tensor_scalar(AL[:, 0:K], AL[:, 0:K], 0.0, None, ALU.min))
                signal(v.tensor_tensor(PL[:, 0:K], SL[:, 0:K], ML[:, 0:K], ALU.subtract), p2["args"])
                dve.wait_ge(p2["exp"], run + 1)
                land(v.tensor_tensor(by_head(AL), by_head(AL), lines_bc(same_l), ALU.mult))
                land(v.tensor_tensor(row_a[0:heads], row_a[0:heads], row_w[0:heads], ALU.mult))
                for k in range(K):
                    last = v.tensor_tensor_scan(DL[:, k, :], AL[:, k, :], PL[:, k, :], 0.0, ALU.mult, ALU.add)
                signal(last, p2["den"])
                dve.wait_ge(p2["drows"], run + 1)
                land(v.tensor_copy(row_f[0:heads], bank[4][0:heads, 0:TILES]))
                land(v.memset(opened[0:heads, 0:1], 0.0))
                signal(v.tensor_tensor_scan(opened[0:heads, 1:TILES + 1], row_a[0:heads], row_f[0:heads], 0.0,
                                     ALU.mult, ALU.add), p2["dopened"])
                dve.wait_ge(p2["dcarried"], run + 1)
                land(v.tensor_copy(carry_l[:, 0:K], bank[5][0:LINES, 0:K]))
                for k in range(K):
                    h, f = k // 2, k % 2
                    last = v.tensor_tensor_scan(DL[:, k, :], AL[:, k, :], PL[:, k, :],
                                                carry_l[:, f * heads + h:f * heads + h + 1], ALU.mult, ALU.add)
                land(last)
                if run == 0:
                    land(v.tensor_tensor(C1[:], ML[:], C2, ALU.max))
                    land(v.tensor_tensor(C2, C2, C1[:], ALU.subtract))
                    signal(v.tensor_tensor(C1[:], ML[:], C1[:], ALU.subtract), p2["args2"])
                    dve.wait_ge(p2["exp2"], 1)
                    land(v.tensor_tensor(DL[:], DL[:], C1[:], ALU.mult))
                    land(v.tensor_tensor(DL[:], DL[:], C2, ALU.add))
                    land(v.tensor_scalar(DL[:], DL[:], 1e-16, None, ALU.add))
                    land(v.reciprocal(DL[:], DL[:]))
                    land(v.tensor_tensor(C1[:], C1[:], DL[:], ALU.mult))
                    signal(v.tensor_tensor(C2, C2, DL[:], ALU.mult), p2["coef"])
                else:
                    land(v.reciprocal(DL[:, 0:K], DL[:, 0:K]))
                    signal(v.tensor_tensor(by_head(C1), by_head(DL), lines_bc(last_l), ALU.mult), p2["coef"])
                dve.wait_ge(p2["back"], run + 1)
                parts = 4 if run == 0 else 3
                for q in range(parts):
                    for k in range(K):
                        h, f = k // 2, k % 2
                        b, at = 2 * q + k // 4, (k % 4) * P
                        last = v.tensor_copy(coef[:, f * LINES:(f + 1) * LINES, q * heads + h],
                                             bank[b][:, at:at + LINES])
                signal(last, p2["done"])
                settle()
            softmax(0, HEADS)

            def g_sum_part(i, n, pair, first=False):
                if i == 0:
                    v.tensor_tensor(pv[:], bank[2][:, :], V[:, bass.ts(n, CHUNK)], ALU.mult)
                elif i == 1:
                    v.tensor_tensor(own_sb[pair], bank[4][:, :], hd_out[pair], ALU.mult)
                elif i == 2:
                    start = 0.0 if first else run_sum[1 - pair][:, CHUNK - 1:CHUNK]
                    v.tensor_tensor_scan(run_sum[pair][:], bank[1][:, :], pv[:], start, ALU.mult, ALU.add)
                elif i == 4:
                    v.tensor_tensor(o_sb[pair], bank[3][:, :], run_sum[pair][:], ALU.mult)
                elif i == 6:
                    v.tensor_tensor(o_sb[pair], o_sb[pair], own_sb[pair], ALU.add).then_inc(g_o, 1)

            def g_sum_waits(n, pair, pair_use):
                dve.wait_ge(g_bc, n + 1)
                dve.wait_ge(gh_in[pair], 16 * (pair_use + 1))
                dve.sem_inc(vector_seen, 1)

            def g_x1_of(n, slot, use, first=False):
                pair, pair_use = of_two(slot, use)
                dve.wait_ge(g_gelu, n + 1)
                dve.wait_ge(gx_in[slot], 16 * (use + 1))
                dve.wait_ge(x1_stored[pair], 16 * (pair_use + 1))
                if not first:
                    dve.wait_ge(g_h, n - 1)
                signal(v.tensor_tensor(x1_sb[pair][:], y_sb[pair][:], ring_a[slot], ALU.add), g_x1)
                measure(0, tiles_of(x1_sb[pair]))

            def g_scale(n, pair, first_r):
                scale_shift(y_sb[pair][:], [tile_of(5, t) for t in range(G)], first_r, g_read, g_y)

            def g_apply_x1(n, pair, pair_use):
                dve.wait_ge(h1_stored[pair], 16 * (pair_use + 1))
                h_norm(0, pair, g_n, keep=last_t[:, bass.ts(n, TILE_GROUP)])

            def g_turn(n, slot, use, first=False):
                pair, pair_use = of_two(slot, use)
                g_x1_of(n - 2, (slot - 2) % X_RING, use - (1 if slot < 2 else 0), first)
                dve.wait_ge(g_sq, n)
                g_sum_waits(n, pair, pair_use)
                inverse_std(G, squares[:, 1 - pair, 0:G], between=lambda i: g_sum_part(i, n, pair))
                g_scale(n - 1, 1 - pair, G)
                g_apply_x1(n - 2, pair, pair_use - 1)
                settle()
            g_sum_waits(0, 0, 0)
            for i in range(7):
                g_sum_part(i, 0, 0, first=True)
                land(v.memset(var_e[:, 0:1], 0.0))
            dve.wait_ge(g_sq, 1)
            g_sum_waits(1, 1, 0)
            inverse_std(0, squares[:, 0, 0:G], between=lambda i: g_sum_part(i, 1, 1))
            g_scale(0, 0, 0)
            settle()
            for n in (2, 3):
                g_turn(n, n, 0, first=True)
            visits(dve, 4, CHUNKS, X_RING, g_turn)
            n = CHUNKS
            g_x1_of(n - 2, (n - 2) % X_RING, (n - 2) // X_RING)
            dve.wait_ge(g_sq, n)
            inverse_std(G, squares[:, 1, 0:G])
            g_scale(n - 1, 1, G)
            g_apply_x1(n - 2, 0, CHUNKS // 2 - 1)
            g_x1_of(n - 1, (n - 1) % X_RING, (n - 1) // X_RING)
            inverse_std(G)
            g_apply_x1(n - 1, 1, CHUNKS // 2 - 1)
            settle()

            for hop in range(HOPS):
                base, uses = hop * CHUNKS, hop * CHUNKS // 2

                def h_query(n, slot, first=False):
                    dve.wait_ge(h_T, base + n + 1)
                    dve.sem_inc(vector_seen, 1)
                    start = 0.0 if first else run_sum[1 - slot][:, 0:1]
                    signal(v.tensor_tensor_scan(run_sum[slot][:, ::-1], bank[HOP_BANKS[slot] + 2][:, ::-1],
                                         V[:, bass.ts(CHUNKS - 1 - n, CHUNK)], start,
                                         ALU.mult, ALU.add), h_q)

                def h_leaky(n, slot, first=False):
                    if not first:
                        dve.wait_ge(h_sc, base + n - 1)
                        dve.sem_inc(vector_seen, 1)
                    dve.wait_ge(h_vs, base + n + 1)
                    dve.sem_inc(vector_seen, 1)
                    land(v.scalar_tensor_tensor(out=t_sb[:], in0=run_sum[slot][:], scalar=bq_sb[:, hop:hop + 1],
                                                in1=V[:, bass.ts(CHUNKS - 1 - n, CHUNK)], op0=ALU.add, op1=ALU.add))
                    signal(v.scalar_tensor_tensor(out=o_sb[slot], in0=t_sb[:], scalar=SLOPE, in1=t_sb[:],
                                                  op0=ALU.mult, op1=ALU.max), h_z)

                def h_turn(n, slot, use):
                    h_query(n, slot)
                    h_leaky(n - 1, 1 - slot)
                    settle()
                h_query(0, 0, first=True)
                for n in (1, 2):
                    h_query(n, n % 2)
                    h_leaky(n - 1, 1 - n % 2, first=True)
                settle()
                visits(dve, 3, CHUNKS, 2, h_turn)
                h_leaky(CHUNKS - 1, 1)
                settle()
                softmax(hop + 1, 1)

                def k_sum(n, slot, first=False):
                    b = K_BANKS[slot]
                    dve.wait_ge(k_bc, base + n + 1)
                    land(v.tensor_tensor(pv[:], bank[b + 1][:, :], V[:, bass.ts(n, CHUNK)], ALU.mult))
                    start = 0.0 if first else run_sum[1 - slot][:, CHUNK - 1:CHUNK]
                    land(v.tensor_tensor_scan(run_sum[slot][:], bank[b][:, :], pv[:], start, ALU.mult, ALU.add))
                    v.scalar_tensor_tensor(out=o_sb[slot][:], in0=run_sum[slot][:], scalar=0.0,
                                           in1=bank[b + 2][:, :], op0=ALU.max, op1=ALU.mult).then_inc(k_h, 1)

                def k_final(n, slot, use):
                    dve.wait_ge(k_T, base + n + 1)
                    dve.wait_ge(x1_in[slot], 16 * (use + 1))
                    signal(v.tensor_tensor(h_sb[slot][:], rows_of(3), x1_sb[slot][:], ALU.add), k_done)

                def k_turn(n, slot, use):
                    k_sum(n, slot)
                    if hop == HOPS - 1:
                        s, u = prev(slot, use)
                        dve.wait_ge(put_done[s], 64 * u)
                        k_final(n - 1, s, u)
                    settle()
                k_sum(0, 0, first=True)
                settle()
                if hop < HOPS - 1:
                    visits(dve, 1, CHUNKS, 2, k_turn)
                    continue
                for n in (1, 2):
                    k_sum(n, n % 2)
                    k_final(n - 1, (n - 1) % 2, 0)
                    settle()
                visits(dve, 3, CHUNKS, 2, k_turn)
                dve.wait_ge(put_done[1], 64 * (CHUNKS // 2 - 1))
                k_final(CHUNKS - 1, 1, CHUNKS // 2 - 1)

        @block.tensor
        def _(pe):
            def mm(dst, lhsT, rhs, start=True, stop=True):
                return nc.tensor.matmul(dst, lhsT, rhs, start=start, stop=stop)

            def tr(dst, src):
                k = src.shape[0]
                return nc.tensor.transpose(dst, src, ident[0:k, 0:k])

            pe.wait_ge(loaded, 16 * LOADS - 16)
            pe.wait_ge(att_loaded, 16 * 2 * HEADS)
            tr(tile_of(0, 0), w_sb[:]).then_inc(wT_done, 1)
            pe.wait_ge(wT_copied, 1)
            mm(bank[1][:, 0:2 * HEADS], wT[:], att_sb[:]).then_inc(watt_done, 1)
            pe.wait_ge(weights_ready, 1)

            def add_bias(b):
                mm(bank[b][:, :], bias_ones[:], bias_rows[:].rearrange("k t d -> k (t d)"), True, False)

            def node(n, slot, use, earlier=2):
                pe.wait_ge(nn_norm, n + 1)
                for t in range(ROWS):
                    last = tr(tile_of(t // TILE_GROUP, t % TILE_GROUP), xn[:, t, :])
                last.then_inc(nn_T, 1)
                if earlier >= 2:
                    pe.wait_ge(nn_read, n - 1)
                b = 2 + 2 * (slot % 2)
                for g in range(2):
                    add_bias(b + g)
                for g, relu in enumerate((aT, bT)):
                    pe.wait_ge(nn_relu, 2 * n + 1 + g)
                    for t in range(TILE_GROUP):
                        last = mm(tile_of(b + g, t), relu[:, t * P:(t + 1) * P], w_mid[:], False,
                                  t == TILE_GROUP - 1)
                last.then_inc(nn_h, 1)
            node(0, 0, 0, 0)
            node(1, 1, 0, 1)
            visits(pe, 2, BLOCKS, 2, node)

            def l_values(n, par):
                mm(bank[2][:, :], w_sb[:], relus[par][0][:])
                mm(bank[3][:, :], w_sb[:], relus[par][1][:]).then_inc(l_h, 1)

            def l_visit(n, slot, use, earlier=2):
                pe.wait_ge(l_norm, n + 1)
                for t in range(2 * TILE_GROUP):
                    last = tr(tile_of(t // TILE_GROUP, t % TILE_GROUP), xn[:, t, :])
                last.then_inc(l_T, 1)
                if earlier >= 2:
                    pe.wait_ge(l_hd, n - 1)
                if earlier >= 1:
                    l_values(n - 1, 1 - slot)
                if earlier >= 2:
                    pe.wait_ge(l_read, n - 1)
                K = 2 * HEADS
                for g in range(2):
                    mm(bank[4 + 2 * slot + g][:, 0:2 * (D + K)], bias_ones[:],
                       bias_wide[:].rearrange("k t d -> k (t d)"), True, False)
                pe.wait_ge(l_relu, n + 1)
                for t in range(TILE_GROUP):
                    a, b = (r[:, t * P:(t + 1) * P] for r in relus[slot])
                    mm(wide_tile(slot, t), a, w_wide[:], False, False)
                    last = mm(wide_tile(slot, t)[:, D:D + K], b, w_att[:, K:2 * K], False, t % 2 == 1)
                last.then_inc(l_p, 1)
            l_visit(0, 0, 0, 0)
            l_visit(1, 1, 0, 1)
            visits(pe, 2, CHUNKS, 2, l_visit)
            pe.wait_ge(l_hd, CHUNKS - 1)
            l_values(CHUNKS - 1, 1)

            def softmax(run, heads):
                K = heads * HALVES
                SK = 2 * K if run == 0 else K
                for k in range(SK):
                    f = k % 2
                    last = tr(bank[k // 4][0:LINES, (k % 4) * P:(k % 4 + 1) * P],
                              scores[:, f * LINES:(f + 1) * LINES, k // 2])
                last.then_inc(p2["lines"], 1)
                pe.wait_ge(p2["local"], run + 1)
                for f in range(HALVES):
                    tr(bank[4][0:heads, f * LINES:(f + 1) * LINES], ML[:, f:K:HALVES, P - 1])
                    last = tr(bank[4][0:heads, TILES + f * LINES:TILES + (f + 1) * LINES],
                              whole_l[:, f:f + 1].to_broadcast([LINES, heads]))
                last.then_inc(p2["rows"], 1)
                pe.wait_ge(p2["opened"], run + 1)
                for f in range(HALVES):
                    last = tr(bank[5][0:LINES, f * heads:(f + 1) * heads],
                              opened[0:heads, f * LINES:(f + 1) * LINES])
                last.then_inc(p2["carried"], 1)
                pe.wait_ge(p2["den"], run + 1)
                for f in range(HALVES):
                    last = tr(bank[4][0:heads, f * LINES:(f + 1) * LINES], DL[:, f:K:HALVES, P - 1])
                last.then_inc(p2["drows"], 1)
                pe.wait_ge(p2["dopened"], run + 1)
                for f in range(HALVES):
                    last = tr(bank[5][0:LINES, f * heads:(f + 1) * heads],
                              opened[0:heads, f * LINES:(f + 1) * LINES])
                last.then_inc(p2["dcarried"], 1)
                pe.wait_ge(p2["coef"], run + 1)
                for q, src in enumerate((AL, PL, C1, C2)[:4 if run == 0 else 3]):
                    for k in range(K):
                        last = tr(bank[2 * q + k // 4][:, (k % 4) * P:(k % 4) * P + LINES], src[:, k, :])
                last.then_inc(p2["back"], 1)
                pe.wait_ge(p2["done"], run + 1)
            pe.wait_ge(l_hd, CHUNKS)
            pe.wait_ge(l_n, CHUNKS)
            softmax(0, HEADS)

            def g_bcast(n, slot, first=False):
                pe.wait_ge(g_staged, n + 1)
                for t in range(TILE_GROUP):
                    last = mm(bank[0][0:PARTS * 4 * HEADS, t * P:(t + 1) * P], coef_parts[slot][:, t, :], ident_bf[:])
                last.then_inc(g_cT, 1)
                pe.wait_ge(g_cTs, n + 1)
                if not first:
                    pe.wait_ge(g_o, n)
                for q in range(4):
                    last = mm(bank[1 + q][:, :], sel_bf[:, q, :], coefT_bf[:])
                last.then_inc(g_bc, 1)

            def g_project(n, slot, first=False):
                if not first:
                    pe.wait_ge(g_read, n)
                add_bias(5)
                pe.wait_ge(g_o, n + 1)
                for t in range(TILE_GROUP):
                    last = mm(tile_of(5, t), o_sb[slot][:, t * P:(t + 1) * P], middle[:], False,
                              t == TILE_GROUP - 1)
                last.then_inc(g_u, 1)

            def g_turned(n, slot):
                pe.wait_ge(g_h, n + 1)
                for t in range(TILE_GROUP):
                    last = tr(tile_of(6, t), h_sb[slot][:, t, :])
                last.then_inc(g_hT, 1)

            def g_query(n):
                pe.wait_ge(g_hTs, n + 1)
                mm(bank[7][:, :], wq_sb[:, 0, :], aT[:]).then_inc(g_q, 1)

            def g_turn(n, slot, use, earlier=3):
                g_bcast(n + 1, 1 - slot)
                if earlier >= 4:
                    pe.wait_ge(g_done, n - 3)
                if earlier >= 3:
                    g_query(n - 3)
                g_project(n, slot, first=earlier == 0)
                if earlier >= 2:
                    g_turned(n - 2, slot)
            g_bcast(0, 0, first=True)
            for n in range(4):
                g_turn(n, n % 2, 0, n)
            visits(pe, 4, CHUNKS - 1, 2, lambda n, slot, use: g_turn(n, slot, use, 4))
            n = CHUNKS - 1
            pe.wait_ge(g_done, n - 3)
            g_query(n - 3)
            g_project(n, 1)
            for m in (n - 2, n - 1, n):
                g_turned(m, m % 2)
                pe.wait_ge(g_done, m)
                g_query(m)

            for hop in range(HOPS):
                base, uses = hop * CHUNKS, hop * CHUNKS // 2
                if hop:
                    pe.wait_ge(k_done, base)
                else:
                    pe.wait_ge(g_done, CHUNKS)

                def h_turned(n, slot, use, first=False):
                    pe.wait_ge(hs_in[slot], 64 * (uses + use + 1))
                    pe.wait_ge(ea_in[slot], 32 * (uses + use + 1))
                    pe.wait_ge(h_staged, base + n + 1)
                    if not first:
                        pe.wait_ge(h_q, base + n - 1)
                    b = HOP_BANKS[slot]
                    for t in range(TILE_GROUP):
                        tr(tile_of(b, t), ring_a[slot][:, t, :])
                        tr(tile_of(b + 1, t), ring_b[slot][:, t, :])
                        last = tr(tile_of(b + 2, t), coef_st[slot][:, t, 0:1].to_broadcast([P, P]))
                    last.then_inc(h_T, 1)

                def h_values(n, slot, first=False):
                    pe.wait_ge(h_Ts, base + n + 1)
                    if not first:
                        pe.wait_ge(h_vs, base + n)
                    mm(bank[3][:, :], wn_sb[:, hop, :], turned[slot][0][:], True, False)
                    mm(bank[3][:, :], we_sb[:, hop, :], turned[slot][1][:], False, True).then_inc(h_v, 1)

                def h_score(n, slot, first=False):
                    if not first:
                        pe.wait_ge(h_scs, base + n)
                    pe.wait_ge(h_z, base + n + 1)
                    for t in range(TILE_GROUP):
                        last = mm(bank[4][:, t:t + 1], o_sb[slot][:, t * P:(t + 1) * P], attn_sb[:, hop:hop + 1])
                    last.then_inc(h_sc, 1)

                def h_turn(n, slot, use, first=False):
                    h_turned(n, slot, use)
                    h_values(n - 1, 1 - slot)
                    h_score(n - 2, slot, first)
                h_turned(0, 0, 0, first=True)
                h_turned(1, 1, 0, first=True)
                h_values(0, 0, first=True)
                h_turn(2, 0, 1, first=True)
                visits(pe, 3, CHUNKS, 2, h_turn)
                h_values(CHUNKS - 1, 1)
                h_score(CHUNKS - 2, 0)
                h_score(CHUNKS - 1, 1)
                pe.wait_ge(h_scs, base + CHUNKS)
                softmax(hop + 1, 1)

                def k_bcast(n, slot, first=False):
                    pe.wait_ge(k_staged, base + n + 1)
                    if not first:
                        pe.wait_ge(k_h, base + n - 1)
                    for q in range(3):
                        for t in range(TILE_GROUP):
                            last = tr(tile_of(K_BANKS[slot] + q, t), coef_st[slot][:, t, q:q + 1].to_broadcast([P, P]))
                    last.then_inc(k_bc, 1)

                def k_rows(n, slot, first=False):
                    pe.wait_ge(k_h, base + n + 1)
                    if not first:
                        pe.wait_ge(k_done, base + n)
                    for t in range(TILE_GROUP):
                        last = tr(tile_of(3, t), o_sb[slot][:, t * P:(t + 1) * P])
                    if hop < HOPS - 1:
                        last = mm(bank[7][:, :], wq_sb[:, hop + 1, :], o_sb[slot][:])
                    last.then_inc(k_T, 1)

                def k_turn(n, slot, use):
                    k_bcast(n, slot)
                    k_rows(n - 1, 1 - slot)
                k_bcast(0, 0, first=True)
                k_bcast(1, 1, first=True)
                k_rows(0, 0, first=True)
                visits(pe, 2, CHUNKS, 2, k_turn)
                k_rows(CHUNKS - 1, 1)


_SHAPES = ["x", "src_tiles", "dst_tiles", "next_tiles", "edge_ids", "dst_lines", "prev_lines", "next_lines",
           "edge_attr", "W", "att", "bias", "gamma", "beta", "Wq", "Wn", "We", "bq", "bn", "be", "attn",
           "ident", "sel"]


def kernel(**inputs):
    import numpy as _np
    import concourse.bacc as _bacc
    from concourse import mybir as _mybir
    from concourse.bass_utils import run_bass_kernel_spmd as _run

    given = {k: _np.asarray(v) for k, v in inputs.items()}

    def pad(a, value):
        return _np.concatenate([a, _np.full(E_PAD - a.shape[0], value, a.dtype)])

    def tiles(a):
        return a.reshape(TILES, P).T

    def lines(a):
        return a.reshape(HALVES, LINES, P).transpose(1, 0, 2)

    dst = pad(given["dst"], N)
    ends = _np.full(1, -1, dst.dtype)
    after, before = _np.concatenate([dst[1:], ends]), _np.concatenate([ends, dst[:-1]])
    sel = _np.zeros((PARTS, 4 * HEADS, 4, D), _np.float32)
    for q in range(4):
        for h in range(HEADS):
            sel[:, q * HEADS + h, q, h * D // HEADS:(h + 1) * D // HEADS] = 1
    data = {
        "x": given["x"], "src_tiles": tiles(pad(given["src"], 0)), "dst_tiles": tiles(dst),
        "next_tiles": tiles(after), "edge_ids": tiles(_np.arange(E_PAD, dtype=_np.int32)),
        "dst_lines": lines(dst), "prev_lines": lines(before), "next_lines": lines(after),
        "edge_attr": given["edge_attr_128"], "W": given["L0_gnn_W"],
        "att": _np.stack([given["L0_gnn_att_src"], given["L0_gnn_att_dst"]]),
        "bias": given["L0_gnn_bias"][None], "gamma": given["L0_gnn_gamma"][None], "beta": given["L0_gnn_beta"][None],
        "Wq": given["L1_gnn_Wq"], "Wn": given["L1_gnn_Wn"], "We": given["L1_gnn_We"],
        "bq": given["L1_gnn_bq"].T, "bn": given["L1_gnn_bn"].T, "be": given["L1_gnn_be"].T,
        "attn": given["L1_gnn_attn"].T, "ident": _np.eye(P, dtype=_np.float32),
        "sel": sel.reshape(PARTS * 4 * HEADS, 4, D),
    }
    nc = _bacc.Bacc("TRN2", target_bir_lowering=False, num_devices=1)
    arrays, args = {}, []
    for name in _SHAPES:
        a = _np.ascontiguousarray(data[name])
        arrays[f"in_{name}"] = a
        args.append(nc.dram_tensor(f"in_{name}", a.shape, _mybir.dt.from_np(a.dtype), kind="ExternalInput").ap())
    out = nc.dram_tensor("out_0", (N, D), _mybir.dt.float32, kind="ExternalOutput").ap()
    build(nc, *args, out)
    return _run(nc, [arrays], core_ids=[0]).results[0]["out_0"]
```

```python
from contextlib import ExitStack

import numpy as np
import concourse.bass as bass
from concourse import mybir

P = 128
D = 128
N = 100000
E = 25000
HEADS = 4
HOPS = 3
TILE_GROUP = 4
CHUNK = TILE_GROUP * P
CHUNKS = 2 * -(-E // (2 * CHUNK))
E_PAD = CHUNKS * CHUNK
TILES = E_PAD // P
HALVES = 2
LINES = TILES // HALVES
ROWS = 8
BLOCK = P * ROWS
BLOCKS = -(-N // BLOCK)
LAST_BLOCK_PARTS = (N - (BLOCKS - 1) * BLOCK) // ROWS
NODE_RING = 6
X_RING = 6
EPS = 1e-5
NONE = -1e30
SKIP = 1 << 20
SLOPE = 0.2
PARTS = 3
RSQRT_SEED = float(0x5F3759DF)
assert (N - (BLOCKS - 1) * BLOCK) % ROWS == 0


def visits(eng, first, total, ring, visit):
    turns = (total - first) // ring
    with eng.Fori(0, turns) as j:
        for u in range(first, first + ring):
            visit(j * ring + u, u % ring, j + u // ring)
    for n in range(first + turns * ring, total):
        visit(n, n % ring, n // ring)


def of_two(slot, use):
    return slot % 2, use * (X_RING // 2) + slot // 2


def of_three(slot, use):
    return slot % 3, use * (X_RING // 3) + slot // 3


def build(nc, x, src_tiles, dst_tiles, next_tiles, edge_ids, dst_lines, prev_lines, next_lines, edge_attr,
          W, att, bias, gamma, beta, Wq, Wn, We, bq, bn, be, attn, ident_in, sel_in, out):
    f32 = mybir.dt.float32
    bf16 = mybir.dt.bfloat16
    i32 = mybir.dt.int32
    ALU = mybir.AluOpType
    ACT = mybir.ActivationFunctionType
    AX = mybir.AxisListType
    ctx = ExitStack()
    with ctx:
        def sb(name, shape, dt=f32):
            return ctx.enter_context(nc.sbuf_tensor(name, shape, dt))

        def sem(name):
            return ctx.enter_context(nc.semaphore(name))

        def sems(name, n):
            return [sem(f"{name}{i}") for i in range(n)]

        pos_table = nc.dram_tensor("pos_table", (N, 1), i32).ap()
        xd_rows = nc.dram_tensor("xd_rows", (E_PAD, D), f32).ap()
        hd_feat = nc.dram_tensor("hd_feat", (P, E_PAD), f32).ap()
        x1_rows = nc.dram_tensor("x1_rows", (E_PAD, D), f32).ap()
        h_tables = [nc.dram_tensor("h1_table", (2 * E_PAD, D), f32).ap(),
                    nc.dram_tensor("h2_table", (E_PAD + P, D), f32).ap(),
                    nc.dram_tensor("h3_table", (E_PAD + P, D), f32).ap()]

        def chunked(rows):
            return rows.rearrange("(c t p) d -> c p t d", t=TILE_GROUP, p=P)

        xd_chunks, x1_chunks = chunked(xd_rows), chunked(x1_rows)
        h_chunks = [chunked(h_tables[0][0:E_PAD, :])] + [chunked(t[0:E_PAD, :]) for t in h_tables[1:]]
        own_chunks = chunked(h_tables[0][E_PAD:2 * E_PAD, :])
        hd_chunks = hd_feat.rearrange("f (c e) -> c f e", e=CHUNK)

        ident = sb("ident", [P, P])
        sel = sb("sel", [PARTS * 4 * HEADS, 4, P])
        sel_bf = sb("sel_bf", [PARTS * 4 * HEADS, 4, P], bf16)
        ident_bf = sb("ident_bf", [P, P], bf16)
        w_sb = sb("w_sb", [P, D])
        wT = sb("wT", [P, D])
        att_sb = sb("att_sb", [P, 2 * HEADS])
        w_att = sb("w_att", [P, 4 * HEADS])
        wq_sb = sb("wq_sb", [P, HOPS, D])
        wn_sb = sb("wn_sb", [P, HOPS, D])
        we_sb = sb("we_sb", [P, HOPS, D])
        bq_sb = sb("bq_sb", [P, HOPS])
        bn_sb = sb("bn_sb", [P, HOPS])
        be_sb = sb("be_sb", [P, HOPS])
        v_bias = sb("v_bias", [P, HOPS])
        attn_sb = sb("attn_sb", [P, HOPS])
        bias_bc = sb("bias_bc", [P, D])
        w_mid = sb("w_mid", [P, D])
        middle = sb("middle", [P, D])
        row_mean = sb("row_mean", [P, 2])
        BIAS_K = 65
        bias_rows = sb("bias_rows", [BIAS_K, TILE_GROUP, D], bf16)
        bias_wide = sb("bias_wide", [BIAS_K, 2, D + 2 * HEADS], bf16)
        w_wide = sb("w_wide", [P, D + 2 * HEADS])
        bias_ones = sb("bias_ones", [BIAS_K, P], bf16)
        z_bf = sb("z_bf", [BIAS_K, D], bf16)
        gamma_bc = sb("gamma_bc", [P, D])
        beta_bc = sb("beta_bc", [P, D])
        src_i = sb("src_i", [P, TILES], i32)
        dst_i = sb("dst_i", [P, TILES], i32)
        next_i = sb("next_i", [P, TILES], i32)
        edge_i = sb("edge_i", [P, TILES], i32)
        recv_i = sb("recv_i", [P, TILES], i32)
        put_i = sb("put_i", [P, TILES], i32)
        pos_i = sb("pos_i", [P, TILES], i32)
        hop1_i = next_i
        last_t = sb("last_t", [P, TILES])
        inner_t = sb("inner_t", [P, TILES])
        same_l = sb("same_l", [LINES, HALVES, P])
        pen_l = sb("pen_l", [LINES, HALVES, P])
        last_l = sb("last_l", [LINES, HALVES, P])
        whole_l = sb("whole_l", [LINES, HALVES])
        V = sb("V", [P, E_PAD])
        scores = sb("scores", [P, TILES, 2 * HEADS])
        coef = sb("coef", [P, TILES, 4 * HEADS])
        dst_l, prev_l, next_l = (
            coef[:].rearrange("p t k -> p (t k)")[0:LINES, i * HALVES * P:(i + 1) * HALVES * P].bitcast(i32)
            .rearrange("l (f e) -> l f e", f=HALVES) for i in range(3))
        ring_all = sb("ring_all", [P, X_RING, TILE_GROUP, D])
        ring_a = [ring_all[:, r] for r in range(X_RING)]
        ring_b = [sb(f"ring_b{r}", [P, TILE_GROUP, D]) for r in range(3)]
        idx_a = [sb(f"idx_a{r}", [P, TILE_GROUP], i32) for r in range(3)]
        pos_idx = [sb(f"pos_idx{r}", [P, TILE_GROUP], i32) for r in range(2)]
        idx_b = [sb(f"idx_b{r}", [P, TILE_GROUP], i32) for r in range(3)]
        pos_in = [sb(f"pos_in{r}", [P, TILE_GROUP], i32) for r in range(2)]
        xn = sb("xn", [P, 2 * TILE_GROUP, D])
        aT = sb("aT", [P, CHUNK])
        bT = sb("bT", [P, CHUNK])
        hd_pair = sb("hd_pair", [P, 2, CHUNK])
        hd_out = [hd_pair[:, r, :] for r in range(2)]
        y_sb = [sb(f"y_sb{r}", [P, TILE_GROUP, D]) for r in range(2)]
        x1_sb = [sb(f"x1_sb{r}", [P, TILE_GROUP, D]) for r in range(2)]
        h_sb = [sb(f"h_sb{r}", [P, TILE_GROUP, D]) for r in range(2)]
        coef_st = [sb(f"coef_st{r}", [P, TILE_GROUP, 4 * HEADS]) for r in range(2)]
        coef_parts = [sb(f"coef_parts{r}", [P, TILE_GROUP, PARTS * 4 * HEADS], bf16) for r in range(2)]
        coef_wide = sb("coef_wide", [P, TILE_GROUP, 4 * HEADS])
        coefT = sb("coefT", [4 * HEADS, CHUNK])
        coefT_bf = sb("coefT_bf", [PARTS * 4 * HEADS, CHUNK], bf16)
        pv = sb("pv", [P, CHUNK])
        run_pair = sb("run_pair", [P, 2, CHUNK])
        run_sum = [run_pair[:, r, :] for r in range(2)]
        relus = [(aT, bT), (run_pair[:, 0, :], run_pair[:, 1, :])]
        turned = [(aT, bT), tuple(y[:].rearrange("p t d -> p (t d)") for y in y_sb)]
        o_pair = sb("o_pair", [P, 2, CHUNK])
        o_sb = [o_pair[:, r, :] for r in range(2)]
        tz_pair = sb("tz_pair", [P, 2, CHUNK])
        t_sb = tz_pair[:, 0, :]
        own_sb = [tz_pair[:, r, :] for r in range(2)]
        STATS = 3 * TILE_GROUP
        stats = sb("stats", [P, STATS, 6])
        mean = sb("mean", [P, STATS])
        gap = sb("gap", [P, STATS])
        var_e = sb("var_e", [P, 16])
        rstd = sb("rstd", [P, 16])
        nwt = sb("nwt", [P, 16])
        x_shift = sb("x_shift", [P, TILE_GROUP])
        h_junk = sb("h_junk", [P, 1])
        h_scale = sb("h_scale", [P, 2, TILE_GROUP])
        h_shift = sb("h_shift", [P, 2, TILE_GROUP])
        squares = sb("squares", [P, 2, ROWS])
        KH = HEADS * HALVES
        SL = ring_all[:, 0:4].rearrange("p r t d -> p (r t) d")[0:LINES]
        def lines_in(pair):
            return pair.rearrange("p a b -> p (a b)")[0:LINES, :].rearrange("l (k e) -> l k e", e=P)
        ML = lines_in(xn[:, :, :])
        AL = lines_in(tz_pair[:, :, :])
        PL = lines_in(o_pair[:, :, :])
        DL = lines_in(hd_pair[:, :, :])
        C1 = lines_in(run_pair[:, :, :])
        C2 = SL[:, KH:2 * KH, :]
        carry_l = sb("carry_l", [LINES, HALVES * HEADS])
        row_f, row_w = pv[0:HEADS, 0:TILES], pv[0:HEADS, TILES:2 * TILES]
        row_a, row_pen = coefT[0:HEADS, 0:TILES], coefT[0:HEADS, TILES:2 * TILES]
        opened = aT[0:HEADS, 0:TILES + 1]
        pos_none = V[0:125, E_PAD - N // 125:E_PAD]
        BW = ROWS * D
        node_x = [V[:, r * BW:(r + 1) * BW].rearrange("p (t d) -> p t d", d=D) for r in range(NODE_RING)]
        node_y = [V[:, r * BW:(r + 1) * BW].rearrange("p (t d) -> p t d", d=D)
                  for r in range(NODE_RING, 2 * NODE_RING)]
        node_junk = V[:, 2 * NODE_RING * BW:(2 * NODE_RING + 1) * BW].rearrange("p (t d) -> p t d", d=D)

        bank = [ctx.enter_context(nc.psum_tensor(f"bank{i}", [P, 512], f32)) for i in range(8)]

        def tile_of(b, t):
            return bank[b][:, t * P:(t + 1) * P]

        def wide_tile(par, t):
            b, at = 4 + 2 * par + t // 2, (t % 2) * (D + 2 * HEADS)
            return bank[b][:, at:at + D + 2 * HEADS]

        def rows_of(b):
            return bank[b][:, :].rearrange("p (t d) -> p t d", t=TILE_GROUP)

        def node_tiles(par):
            return [tile_of(2 + 2 * par + t // TILE_GROUP, t % TILE_GROUP) for t in range(ROWS)]

        loaded = sem("loaded")
        att_zero, att_loaded = sem("att_zero"), sem("att_loaded")
        wT_done, wT_copied, watt_done = sem("wT_done"), sem("wT_copied"), sem("watt_done")
        weights_ready, index_ready = sem("weights_ready"), sem("index_ready")
        pos_fill, pos_clear = sem("pos_fill"), sem("pos_clear")
        zero_rows, zeroed = sem("zero_rows"), sem("zeroed")
        staged = sem("staged")
        pool_seen, sync_seen, vector_seen = sem("pool_seen"), sem("sync_seen"), sem("vector_seen")
        pos_put, pos_got = sems("pos_put", 2), sems("pos_got", 2)
        pos_copied, pos_ready, hop1_ready = sem("pos_copied"), sem("pos_ready"), sem("hop1_ready")
        step = sem("step")
        nx_in = sems("nx_in", NODE_RING)
        nn_norm, nn_T, nn_relu, nn_h = sem("nn_norm"), sem("nn_T"), sem("nn_relu"), sem("nn_h")
        nn_sq, nn_read = sem("nn_sq"), sem("nn_read")
        nn_std, nn_norm_act = sem("nn_std"), sem("nn_norm_act")
        l_x1_done = sem("l_x1_done")
        l_std, l_norm_act = sem("l_std"), sem("l_norm_act")
        nn_y, nn_gelu, nn_out = sem("nn_y"), sem("nn_gelu"), sem("nn_out")
        nn_stored = sems("nn_stored", NODE_RING)
        xs_in, xd_in = sems("xs_in", X_RING), sems("xd_in", 3)
        l_sq, l_read, l_p = sem("l_sq"), sem("l_read"), sem("l_p")
        l_norm, l_T, l_relu, l_h = sem("l_norm"), sem("l_T"), sem("l_relu"), sem("l_h")
        l_hd, l_y, l_gelu, l_n, l_own = sem("l_hd"), sem("l_y"), sem("l_gelu"), sem("l_n"), sem("l_own")
        xd_stored, hd_stored, own_stored = sems("xd_stored", 3), sems("hd_stored", 2), sems("own_stored", 2)
        gx_in, gh_in = sems("gx_in", X_RING), sems("gh_in", 2)
        g_sq, g_read = sem("g_sq"), sem("g_read")
        g_staged, g_cT, g_cTs, g_bc, g_o = sem("g_staged"), sem("g_cT"), sem("g_cTs"), sem("g_bc"), sem("g_o")
        g_u, g_y, g_gelu, g_x1, g_n = sem("g_u"), sem("g_y"), sem("g_gelu"), sem("g_x1"), sem("g_n")
        g_h, g_hT, g_hTs, g_q, g_done = sem("g_h"), sem("g_hT"), sem("g_hTs"), sem("g_q"), sem("g_done")
        x1_stored, h1_stored = sems("x1_stored", 2), sems("h1_stored", 2)
        hs_in, ea_in = sems("hs_in", 2), sems("ea_in", 2)
        h_staged, h_T, h_Ts, h_v, h_q = sem("h_staged"), sem("h_T"), sem("h_Ts"), sem("h_v"), sem("h_q")
        h_vs, h_z, h_sc, h_scs = sem("h_vs"), sem("h_z"), sem("h_sc"), sem("h_scs")
        k_staged, k_bc, k_h, k_T, k_done = sem("k_staged"), sem("k_bc"), sem("k_h"), sem("k_T"), sem("k_done")
        k_stored, x1_in, put_done = sems("k_stored", 2), sems("x1_in", 2), sems("put_done", 2)
        p2 = {n: sem(f"p2_{n}") for n in ("lines", "local", "rows", "opened", "carried", "args", "exp", "den",
                                          "drows", "dopened", "dcarried", "args2", "exp2", "coef", "back", "done")}
        LOADS = 21
        SUM_BANKS = (5, 7)
        ROW_BANKS = (3, 7)
        K_BANKS = (0, 4)
        HOP_BANKS = (0, 5)

        def prev(slot, use):
            return 1 - slot, use - (1 if slot == 0 else 0)

        block = ctx.enter_context(nc.Block())

        @block.sync
        def _(sp):
            for dst, src in ((ident, ident_in), (sel, sel_in), (w_sb, W), (bq_sb, bq), (bn_sb, bn), (be_sb, be),
                             (attn_sb, attn), (src_i, src_tiles), (dst_i, dst_tiles), (next_i, next_tiles),
                             (edge_i, edge_ids), (dst_l, dst_lines), (prev_l, prev_lines), (next_l, next_lines)):
                sp.dma_start(dst[:], src).then_inc(loaded, 16)
            for dst, src in ((bias_bc, bias), (gamma_bc, gamma), (beta_bc, beta)):
                sp.dma_start(dst[:], src.to_broadcast([P, D])).then_inc(loaded, 16)
            for dst, src in ((wq_sb, Wq), (wn_sb, Wn), (we_sb, We)):
                sp.dma_start(dst[:], src.rearrange("i k f -> k i f")).then_inc(loaded, 16)
            sp.wait_ge(att_zero, 1)
            part = D // HEADS
            for s in range(2):
                for h in range(HEADS):
                    sp.dma_start(att_sb[part * h:part * (h + 1), s * HEADS + h:s * HEADS + h + 1],
                                 att[s, h, :].unsqueeze(1)).then_inc(att_loaded, 16)
            sp.wait_ge(pos_fill, 1)
            sp.dma_start(pos_table.rearrange("(p c) o -> p (c o)", p=125),
                         pos_none.bitcast(i32)).then_inc(pos_clear, 16)
            sp.wait_ge(zero_rows, 1)
            for t in h_tables[1:]:
                sp.dma_start(t[E_PAD:E_PAD + P, :], y_sb[0][:, 0, :]).then_inc(zeroed, 16)
            for s in (*nn_stored, *hd_stored, *own_stored, *x1_stored, *h1_stored):
                sp.sem_inc(s, 16)

            whole = (BLOCKS - 1) * BLOCK
            x_blocks = x[0:whole, :].rearrange("(b p r) d -> b p r d", p=P, r=ROWS)
            out_blocks = out[0:whole, :].rearrange("(b p r) d -> b p r d", p=P, r=ROWS)

            def node_store(n, slot):
                sp.wait_ge(nn_out, n + 1)
                sp.dma_start(out_blocks[n], node_y[slot]).then_inc(nn_stored[slot], 16)

            def node_turn(n, slot, use):
                sp.wait_ge(nn_out, n - NODE_RING + 1)
                sp.dma_start(node_x[slot], x_blocks[n]).then_inc(nx_in[slot], 16)
                node_store(n - NODE_RING, slot)
            for n in range(NODE_RING):
                sp.dma_start(node_x[n], x_blocks[n]).then_inc(nx_in[n], 16)
            visits(sp, NODE_RING, BLOCKS - 1, NODE_RING, node_turn)
            n = BLOCKS - 1
            sp.wait_ge(nn_out, n - NODE_RING + 1)
            sp.dma_start(node_x[n % NODE_RING][0:LAST_BLOCK_PARTS],
                         x[whole:N, :].rearrange("(p r) d -> p r d", r=ROWS)).then_inc(nx_in[n % NODE_RING], 16)
            for m in range(n - NODE_RING, n):
                node_store(m, m % NODE_RING)
            sp.wait_ge(nn_out, n + 1)
            sp.dma_start(out[whole:N, :].rearrange("(p r) d -> p r d", r=ROWS),
                         node_y[n % NODE_RING][0:LAST_BLOCK_PARTS]).then_inc(nn_stored[n % NODE_RING], 16)

            def store_own(n, slot):
                sp.wait_ge(l_own, n + 1)
                sp.dma_start(own_chunks[n], h_sb[slot][:]).then_inc(own_stored[slot], 16)

            def store_x(n, slot, use):
                trio, trio_use = of_three(slot, use)
                sp.wait_ge(xd_in[trio], 64 * (trio_use + 1))
                sp.dma_start(xd_chunks[n], ring_b[trio][:]).then_inc(xd_stored[trio], 16)

            def store_hd(n, slot):
                sp.wait_ge(l_hd, n + 1)
                sp.dma_start(hd_chunks[n], hd_out[slot][:]).then_inc(hd_stored[slot], 16)

            def keep_turn(n, slot, use):
                store_x(n, slot, use)
                store_hd(n - 2, slot % 2)
                store_own(n - 4, slot % 2)
            for n in range(4):
                store_x(n, n, 0)
                if n >= 2:
                    store_hd(n - 2, n % 2)
            visits(sp, 4, CHUNKS, X_RING, keep_turn)
            for n in (CHUNKS - 2, CHUNKS - 1):
                store_hd(n, n % 2)
                store_own(n - 2, n % 2)
            store_own(CHUNKS - 2, 0)
            store_own(CHUNKS - 1, 1)

            for r in range(3):
                sp.wait_ge(xd_stored[r], 16 * len(range(r, CHUNKS, 3)))
            for r in range(2):
                sp.wait_ge(hd_stored[r], 16 * (CHUNKS // 2 + 1))
            sp.wait_ge(p2["done"], 1)

            def sums_load(n, slot, pair_slot):
                sp.dma_start(ring_a[slot], xd_chunks[n]).then_inc(gx_in[slot], 16)
                sp.dma_start(hd_out[pair_slot], hd_chunks[n]).then_inc(gh_in[pair_slot], 16)

            def sums_store(n, slot):
                sp.wait_ge(g_x1, n + 1)
                sp.dma_start(x1_chunks[n], x1_sb[slot][:]).then_inc(x1_stored[slot], 16)
                sp.wait_ge(g_h, n + 1)
                sp.dma_start(h_chunks[0][n], h_sb[slot][:]).then_inc(h1_stored[slot], 16)

            def sums_turn(n, slot, use):
                sp.wait_ge(g_o, n - 1)
                sp.sem_inc(sync_seen, 1)
                sp.wait_ge(g_x1, n - X_RING + 1)
                sp.sem_inc(sync_seen, 1)
                sums_load(n, slot, slot % 2)
                sums_store(n - 4, slot % 2)
            for n in range(X_RING):
                if n >= 2:
                    sp.wait_ge(g_o, n - 1)
                sums_load(n, n, n % 2)
                if n >= 4:
                    sums_store(n - 4, n % 2)
            visits(sp, X_RING, CHUNKS, X_RING, sums_turn)
            for n in range(CHUNKS - 4, CHUNKS):
                sums_store(n, n % 2)

            chunk_full = E // CHUNK
            at = chunk_full * CHUNK
            tiles_full, rest = (E - at) // P, (E - at) % P
            edge_chunks = edge_attr[0:at, :].rearrange("(c t p) d -> c p t d", t=TILE_GROUP, p=P)
            for hop in range(HOPS):
                base, uses = hop * CHUNKS, hop * CHUNKS // 2
                if hop:
                    sp.wait_ge(h_T, base)
                for n in range(CHUNKS - chunk_full):
                    if CHUNKS - 1 - n > chunk_full:
                        sp.sem_inc(ea_in[n % 2], 32)
                        continue
                    sp.dma_start(ring_b[n % 2][:, 0:tiles_full, :],
                                 edge_attr[at:at + tiles_full * P, :].rearrange("(t p) d -> p t d", p=P)
                                 ).then_inc(ea_in[n % 2], 16)
                    sp.dma_start(ring_b[n % 2][0:rest, tiles_full, :],
                                 edge_attr[at + tiles_full * P:E, :]).then_inc(ea_in[n % 2], 16)

                def edge_load(n, slot, use):
                    sp.wait_ge(h_T, base + n - 1)
                    sp.sem_inc(sync_seen, 1)
                    sp.dma_start(ring_b[slot][:], edge_chunks[CHUNKS - 1 - n]).then_inc(ea_in[slot], 32)
                visits(sp, CHUNKS - chunk_full, CHUNKS, 2, edge_load)

                if hop < HOPS - 1:
                    def store(n, slot, use):
                        sp.wait_ge(k_done, base + n + 1)
                        sp.dma_start(h_chunks[hop + 1][n], h_sb[slot][:]).then_inc(k_stored[slot], 16)
                    visits(sp, 0, CHUNKS, 2, store)
                else:
                    for r in range(2):
                        sp.wait_ge(x1_stored[r], 16 * (CHUNKS // 2 + 1))
                        sp.dma_start(x1_sb[r][:], x1_chunks[r]).then_inc(x1_in[r], 16)

                    def x1_load(n, slot, use):
                        sp.wait_ge(k_done, base + n - 1)
                        sp.dma_start(x1_sb[slot][:], x1_chunks[n]).then_inc(x1_in[slot], 16)
                    visits(sp, 2, CHUNKS, 2, x1_load)
            for r in range(NODE_RING):
                sp.wait_ge(nn_stored[r], 16 * (len(range(r, BLOCKS, NODE_RING)) + 1))
            for r in range(2):
                sp.wait_ge(own_stored[r], 16 * (CHUNKS // 2 + 1))
                sp.wait_ge(h1_stored[r], 16 * (CHUNKS // 2 + 1))
                sp.wait_ge(k_stored[r], 16 * (HOPS - 1) * CHUNKS // 2)
                sp.wait_ge(pos_put[r], 64 * (CHUNKS // 2))
                sp.wait_ge(put_done[r], 64 * (CHUNKS // 2))
            sp.wait_ge(pos_clear, 16)
            sp.wait_ge(zeroed, 32)

        @block.gpsimd
        def _(pool):
            def wait_count(s, value):
                pool.wait_ge(s, value)
                pool.sem_inc(pool_seen, 1)

            def stage(dst, cols_of):
                nc.gpsimd.tensor_copy(dst[:], cols_of).then_inc(staged, 1)

            def gather(dst_of_tile, table, index, done):
                for t in range(TILE_GROUP):
                    pool.indirect_dma_start(out=dst_of_tile(t), out_offset=None, in_=table,
                                            in_offset=bass.IndirectOffsetOnAxis(ap=index[:, t:t + 1], axis=0)
                                            ).then_inc(done, 16)

            def scatter(table, index, src_of_tile, done):
                for t in range(TILE_GROUP):
                    pool.indirect_dma_start(out=table, in_=src_of_tile(t), in_offset=None, bounds_check=N - 1,
                                            out_offset=bass.IndirectOffsetOnAxis(ap=index[:, t:t + 1], axis=0),
                                            oob_is_err=False).then_inc(done, 16)

            def cols(array, n):
                return array[:, bass.ts(n, TILE_GROUP)]

            pool.wait_ge(index_ready, 1)
            pool.wait_ge(pos_clear, 16)

            def put_pos(n, slot, use):
                stage(pos_in[slot], cols(edge_i, n))
                stage(pos_idx[slot], cols(put_i, n))
                pool.wait_ge(staged, 2)
                scatter(pos_table, pos_idx[slot], lambda t: pos_in[slot][:, t:t + 1], pos_put[slot])
                pool.sem_clear(staged)

            def put_pos_again(n, slot, use):
                wait_count(pos_put[slot], 64 * use)
                put_pos(n, slot, use)

            def node_sum(n, slot):
                wait_count(nn_gelu, n + 1)
                nc.gpsimd.tensor_tensor(node_y[slot], node_y[slot], node_x[slot], ALU.add).then_inc(nn_out, 1)

            def of_node_pair(slot, use):
                return slot % 2, use * (NODE_RING // 2) + slot // 2

            def put_turn(n, slot, use):
                pair, pair_use = of_node_pair(slot, use)
                put_pos_again(n + 2, pair, pair_use + 1)
                node_sum(n, slot)
            for n in (0, 1):
                put_pos(n, n, 0)
            AHEAD = 2
            visits(pool, 0, CHUNKS - AHEAD, NODE_RING, put_turn)
            for r in range(2):
                pool.wait_ge(pos_put[r], 64 * (CHUNKS // 2))

            def get_x(n, slot, use):
                trio = slot % 3
                stage(idx_a[trio], cols(src_i, n))
                stage(idx_b[trio], cols(recv_i, n))
                pool.wait_ge(staged, 2)
                gather(lambda t: ring_a[slot][:, t, :], x, idx_a[trio], xs_in[slot])
                gather(lambda t: ring_b[trio][:, t, :], x, idx_b[trio], xd_in[trio])
                pool.sem_clear(staged)

            def get_pos(n, slot, use):
                stage(pos_idx[slot], cols(src_i, n))
                pool.wait_ge(staged, 1)
                gather(lambda t: pos_in[slot][:, t:t + 1], pos_table, pos_idx[slot], pos_got[slot])
                pool.sem_clear(staged)

            def copy_pos(n, slot, use):
                wait_count(pos_got[slot], 64 * (use + 1))
                nc.gpsimd.tensor_copy(cols(pos_i, n), pos_in[slot][:]).then_inc(pos_copied, 1)
                wait_count(pos_copied, n + 1)

            def pos_turn(n, slot, use):
                get_pos(n, slot, use)
                copy_pos(n - 1, *prev(slot, use))
            def get_turn(n, slot, use):
                pair, pair_use = of_node_pair(slot, use)
                pos_turn(n - CHUNKS + AHEAD, pair, pair_use - (CHUNKS - AHEAD) // 2)
                node_sum(n, slot)
            assert BLOCKS == 2 * CHUNKS - AHEAD
            n = CHUNKS - AHEAD
            get_pos(0, 0, 0)
            node_sum(n, n % NODE_RING)
            visits(pool, n + 1, BLOCKS - 5, NODE_RING, get_turn)
            for m in range(BLOCKS - 5, BLOCKS - 1):
                get_turn(m, m % NODE_RING, m // NODE_RING)
                if m < BLOCKS - 3:
                    n = m - (BLOCKS - 5)
                    get_x(n, n, 0)
            pos_turn(CHUNKS - 1, 1, CHUNKS // 2 - 1)
            copy_pos(CHUNKS - 1, 1, CHUNKS // 2 - 1)
            pool.sem_inc(pos_ready, 1)
            node_sum(BLOCKS - 1, (BLOCKS - 1) % NODE_RING)

            def get_x_again(n, slot, use):
                trio, trio_use = of_three(slot, use)
                wait_count(l_norm, n - 2)
                wait_count(xd_stored[trio], 16 * trio_use)
                wait_count(l_x1_done, n - X_RING + 1)
                get_x(n, slot, use)
            for n in range(2, X_RING):
                if n >= 3:
                    pool.wait_ge(l_norm, n - 2)
                    pool.wait_ge(xd_stored[n % 3], 16 * (n // 3))
                get_x(n, n, 0)
            visits(pool, X_RING, CHUNKS, X_RING, get_x_again)

            pool.wait_ge(p2["done"], 1)

            def stage_coef(n, slot):
                rest, K = coef_st[slot], 4 * HEADS
                stage(rest, coef[:, bass.ts(n, TILE_GROUP), :])
                pool.wait_ge(staged, 1)
                for i in range(PARTS):
                    part = coef_parts[slot][:, :, i * K:(i + 1) * K]
                    if i == PARTS - 1:
                        nc.gpsimd.tensor_copy(part, rest[:]).then_inc(g_staged, 1)
                        break
                    nc.gpsimd.tensor_copy(part, rest[:]).then_inc(staged, 1)
                    pool.wait_ge(staged, 3 * i + 2)
                    nc.gpsimd.tensor_copy(coef_wide[:], part).then_inc(staged, 1)
                    pool.wait_ge(staged, 3 * i + 3)
                    nc.gpsimd.tensor_tensor(rest[:], rest[:], coef_wide[:], ALU.subtract).then_inc(staged, 1)
                    pool.wait_ge(staged, 3 * i + 4)
                pool.sem_clear(staged)

            def stage_coef_again(n, slot, use):
                wait_count(g_cT, n - 1)
                stage_coef(n, slot)
            stage_coef(0, 0)
            stage_coef(1, 1)
            visits(pool, 2, CHUNKS, 2, stage_coef_again)

            for hop in range(HOPS):
                base, uses = hop * CHUNKS, hop * CHUNKS // 2
                if hop == 0:
                    pool.wait_ge(hop1_ready, 1)
                    pool.wait_ge(zeroed, 32)
                for r in range(2):
                    if hop == 0:
                        pool.wait_ge(h1_stored[r], 16 * (CHUNKS // 2 + 1))
                        pool.wait_ge(own_stored[r], 16 * (CHUNKS // 2 + 1))
                    else:
                        pool.wait_ge(k_stored[r], 16 * uses)
                index = hop1_i if hop == 0 else pos_i

                def get_h(n, slot, use):
                    c = CHUNKS - 1 - n
                    nc.gpsimd.tensor_copy(coef_st[slot][:, :, 0], cols(inner_t, c)).then_inc(h_staged, 1)
                    stage(idx_a[slot], cols(index, c))
                    pool.wait_ge(staged, 1)
                    gather(lambda t: ring_a[slot][:, t, :], h_tables[hop], idx_a[slot], hs_in[slot])
                    pool.sem_clear(staged)

                def get_h_again(n, slot, use):
                    wait_count(h_T, base + n - 1)
                    get_h(n, slot, use)
                get_h(0, 0, 0)
                get_h(1, 1, 0)
                visits(pool, 2, CHUNKS, 2, get_h_again)

                pool.wait_ge(p2["done"], hop + 2)

                def stage_hop_coef(n, slot):
                    nc.gpsimd.tensor_copy(coef_st[slot][:, :, 0:3],
                                          coef[:, bass.ts(n, TILE_GROUP), 0:3]).then_inc(k_staged, 1)

                def stage_hop_coef_again(n, slot, use):
                    wait_count(k_bc, base + n - 1)
                    stage_hop_coef(n, slot)

                if hop < HOPS - 1:
                    stage_hop_coef(0, 0)
                    stage_hop_coef(1, 1)
                    visits(pool, 2, CHUNKS, 2, stage_hop_coef_again)
                    continue
                for r in range(NODE_RING):
                    pool.wait_ge(nn_stored[r], 16 * (len(range(r, BLOCKS, NODE_RING)) + 1))

                def put_out(n, slot):
                    stage(idx_a[slot], cols(put_i, n))
                    pool.wait_ge(staged, 1)
                    wait_count(k_done, base + n + 1)
                    scatter(out, idx_a[slot], lambda t: h_sb[slot][:, t, :], put_done[slot])
                    pool.sem_clear(staged)

                stage_hop_coef(0, 0)
                stage_hop_coef(1, 1)
                for n in (2, 3):
                    stage_hop_coef_again(n, n % 2, 1)
                    put_out(n - 2, n % 2)

                def last_turns(n, slot, use):
                    stage_hop_coef_again(n, slot, use)
                    wait_count(put_done[slot], 64 * (use - 1))
                    put_out(n - 2, slot)
                visits(pool, 4, CHUNKS, 2, last_turns)
                for n in (CHUNKS - 2, CHUNKS - 1):
                    pool.wait_ge(put_done[n % 2], 64 * (CHUNKS // 2 - 1))
                    put_out(n, n % 2)

        @block.scalar
        def _(act):
            def copy(dst, src):
                return nc.scalar.activation(dst, src, ACT.Copy)

            def h_of(pair):
                for t in range(TILE_GROUP):
                    last = nc.scalar.activation(h_sb[pair][:, t, :], x1_sb[pair][:, t, :], ACT.Relu,
                                                bias=h_shift[:, pair, t:t + 1], scale=h_scale[:, pair, t:t + 1])
                return last

            def squares_of(tiles, junk, par):
                for t, src in enumerate(tiles):
                    last = nc.scalar.activation(junk[:, t, :], src, ACT.Square, accum_out=squares[:, par, t:t + 1])
                return last

            def normalize_x(src, done):
                for t in range(TILE_GROUP):
                    last = nc.scalar.activation(xn[:, t, :], src[:, t, :], ACT.Identity,
                                                bias=x_shift[:, t:t + 1], scale=rstd[:, t:t + 1])
                last.then_inc(done, 1)

            def node_norm(n, slot):
                act.wait_ge(nn_std, n + 1)
                normalize_x(node_x[slot], nn_norm_act)

            def node_relu(n):
                act.wait_ge(nn_T, n + 1)
                nc.scalar.activation(aT[:], bank[0][:, :], ACT.Relu).then_inc(nn_relu, 1)
                nc.scalar.activation(bT[:], bank[1][:, :], ACT.Relu).then_inc(nn_relu, 1)

            def node_squares(n, par):
                act.wait_ge(nn_h, n + 1)
                squares_of(node_tiles(par), node_junk, par).then_inc(nn_sq, 1)

            def node_gelu(n, slot):
                act.wait_ge(nn_y, n + 1)
                nc.scalar.activation(node_y[slot], node_y[slot], ACT.Gelu).then_inc(nn_gelu, 1)

            def node_turn(n, slot, use, earlier=2):
                node_norm(n, slot)
                if earlier >= 1:
                    node_squares(n - 1, 1 - slot % 2)
                node_relu(n)
                if earlier >= 2:
                    node_gelu(n - 2, (slot - 2) % NODE_RING)
            for n in range(2):
                node_turn(n, n, 0, n)
            visits(act, 2, BLOCKS, NODE_RING, node_turn)
            node_gelu(BLOCKS - 2, (BLOCKS - 2) % NODE_RING)
            node_squares(BLOCKS - 1, (BLOCKS - 1) % 2)
            node_gelu(BLOCKS - 1, (BLOCKS - 1) % NODE_RING)

            pv_tiles = pv[:].rearrange("p (t d) -> p t d", d=D)

            def l_relu_x(n, par):
                act.wait_ge(l_T, n + 1)
                nc.scalar.activation(relus[par][0][:], bank[0][:, :], ACT.Relu)
                nc.scalar.activation(relus[par][1][:], bank[1][:, :], ACT.Relu).then_inc(l_relu, 1)

            def l_values(n, pair, pair_use):
                act.wait_ge(l_h, n + 1)
                act.wait_ge(hd_stored[pair], 16 * (pair_use + 1))
                copy(V[:, bass.ts(n, CHUNK)], bank[2][:, :])
                copy(hd_out[pair], bank[3][:, :]).then_inc(l_hd, 1)

            def l_squares(n, par):
                act.wait_ge(l_p, n + 1)
                squares_of([wide_tile(par, t)[:, 0:D] for t in range(TILE_GROUP)], pv_tiles, par)
                for g in range(2):
                    wide = bank[4 + 2 * par + g][:, 0:2 * (D + 2 * HEADS)].rearrange("p (t k) -> p t k", t=2)
                    last = copy(scores[:, bass.ts(n * 2 + g, 2), :], wide[:, :, D:D + 2 * HEADS])
                last.then_inc(l_sq, 1)

            def l_gelu_of(n, pair):
                act.wait_ge(l_y, n + 1)
                nc.scalar.activation(y_sb[pair][:], y_sb[pair][:], ACT.Gelu).then_inc(l_gelu, 1)

            def l_relu_of(n, pair):
                act.wait_ge(l_n, n + 1)
                h_of(pair).then_inc(l_own, 1)

            def l_turn(n, slot, use, earlier=4):
                pair, pair_use = of_two(slot, use)
                act.wait_ge(l_std, n + 1)
                normalize_x(ring_a[slot], l_norm_act)
                if earlier >= 1:
                    l_squares(n - 1, 1 - pair)
                if earlier >= 2:
                    l_gelu_of(n - 2, pair)
                l_relu_x(n, pair)
                if earlier >= 4:
                    l_relu_of(n - 4, pair)
                if earlier >= 1:
                    l_values(n - 1, *prev(pair, pair_use))
            l_turn(0, 0, 0, 0)
            act.wait_ge(pos_clear, 16)
            for r in range(NODE_RING):
                act.wait_ge(nn_stored[r], 16 * (len(range(r, BLOCKS, NODE_RING)) + 1))
            for n in (1, 2, 3):
                l_turn(n, n, 0, n)
            visits(act, 4, CHUNKS, X_RING, l_turn)
            l_squares(CHUNKS - 1, 1)
            l_values(CHUNKS - 1, 1, CHUNKS // 2 - 1)
            l_gelu_of(CHUNKS - 2, 0)
            l_relu_of(CHUNKS - 4, 0)
            l_gelu_of(CHUNKS - 1, 1)
            l_relu_of(CHUNKS - 3, 1)
            l_relu_of(CHUNKS - 2, 0)
            l_relu_of(CHUNKS - 1, 1)

            def softmax_exps(run, heads):
                K = heads * HALVES
                act.wait_ge(p2["args"], run + 1)
                nc.scalar.activation(AL[:, 0:K], AL[:, 0:K], ACT.Exp)
                nc.scalar.activation(row_a[0:heads], row_a[0:heads], ACT.Exp)
                nc.scalar.activation(PL[:, 0:K], PL[:, 0:K], ACT.Exp).then_inc(p2["exp"], 1)
                if run == 0:
                    act.wait_ge(p2["args2"], 1)
                    nc.scalar.activation(C1[:, 0:K], C1[:, 0:K], ACT.Exp)
                    nc.scalar.activation(C2[:, 0:K], C2[:, 0:K], ACT.Exp).then_inc(p2["exp2"], 1)
            softmax_exps(0, HEADS)

            def g_coef(n):
                act.wait_ge(g_cT, n + 1)
                copy(coefT_bf[:], bank[0][0:PARTS * 4 * HEADS, :]).then_inc(g_cTs, 1)

            def g_squares(n, par):
                act.wait_ge(g_u, n + 1)
                squares_of([tile_of(SUM_BANKS[par], t) for t in range(TILE_GROUP)], xn[:, 0:TILE_GROUP, :],
                           par).then_inc(g_sq, 1)

            def g_gelu_of(n, pair):
                act.wait_ge(g_y, n + 1)
                nc.scalar.activation(y_sb[pair][:], y_sb[pair][:], ACT.Gelu).then_inc(g_gelu, 1)

            def g_h_of(n, pair):
                act.wait_ge(g_n, n + 1)
                h_of(pair).then_inc(g_h, 1)

            def g_h_turned(n):
                act.wait_ge(g_hT, n + 1)
                copy(aT[:], bank[6][:, :]).then_inc(g_hTs, 1)

            def g_queries(n):
                act.wait_ge(g_q, n + 1)
                copy(V[:, bass.ts(n, CHUNK)], bank[6][:, ::-1]).then_inc(g_done, 1)

            def g_turn(n, slot, use, earlier=5):
                g_coef(n + 1)
                if earlier >= 5:
                    g_queries(n - 5)
                if earlier >= 4:
                    g_h_turned(n - 4)
                g_squares(n, slot)
                if earlier >= 1:
                    g_gelu_of(n - 1, 1 - slot)
                if earlier >= 3:
                    g_h_of(n - 3, 1 - slot)
            g_coef(0)
            for n in range(5):
                g_turn(n, n % 2, 0, n)
            visits(act, 5, CHUNKS - 1, 2, g_turn)
            n = CHUNKS - 1
            g_queries(n - 5)
            g_gelu_of(n - 1, 0)
            g_squares(n, 1)
            g_h_turned(n - 4)
            g_queries(n - 4)
            g_h_of(n - 3, 0)
            g_gelu_of(n, 1)
            for m in range(n - 3, n + 1):
                g_h_turned(m)
                g_queries(m)
                if m < n:
                    g_h_of(m + 1, (m + 1) % 2)

            for hop in range(HOPS):
                base, uses = hop * CHUNKS, hop * CHUNKS // 2

                def h_copies(n, slot):
                    act.wait_ge(h_T, base + n + 1)
                    for i in range(2):
                        last = copy(turned[slot][i][:], bank[HOP_BANKS[slot] + i][:, :])
                    last.then_inc(h_Ts, 1)

                def h_values(n):
                    act.wait_ge(h_v, base + n + 1)
                    act.wait_ge(h_q, base + n + 1)
                    nc.scalar.activation(V[:, bass.ts(CHUNKS - 1 - n, CHUNK)], bank[3][:, :], ACT.Identity,
                                         bias=v_bias[:, hop:hop + 1]).then_inc(h_vs, 1)

                def h_scores(n):
                    act.wait_ge(h_sc, base + n + 1)
                    copy(scores[:, bass.ts(CHUNKS - 1 - n, TILE_GROUP), 0], bank[4][:, 0:TILE_GROUP]).then_inc(h_scs, 1)

                def h_turn(n, slot, use):
                    h_copies(n, slot)
                    h_values(n - 1)
                    h_scores(n - 2)
                h_copies(0, 0)
                h_copies(1, 1)
                h_values(0)
                visits(act, 2, CHUNKS, 2, h_turn)
                h_values(CHUNKS - 1)
                h_scores(CHUNKS - 2)
                h_scores(CHUNKS - 1)
                softmax_exps(hop + 1, 1)

                if hop < HOPS - 1:
                    def k_out(n, slot):
                        act.wait_ge(k_T, base + n + 1)
                        copy(h_sb[slot][:], rows_of(3))
                        copy(V[:, bass.ts(n, CHUNK)], bank[7][:, ::-1]).then_inc(k_done, 1)

                    def k_out_again(n, slot, use):
                        act.wait_ge(k_stored[slot], 16 * (uses + use))
                        k_out(n, slot)
                    k_out(0, 0)
                    k_out(1, 1)
                    visits(act, 2, CHUNKS, 2, k_out_again)

        @block.vector
        def _(dve):
            steps = [0]

            def land(ins, meanwhile=None):
                steps[0] += 1
                at = steps[0]
                ins.then_inc(step, 1)
                if meanwhile is not None:
                    meanwhile()
                dve.wait_ge(step, at)

            def signal(ins, s):
                land(ins)
                dve.sem_inc(s, 1)

            def settle():
                steps[0] = 0
                dve.sem_clear(step)

            v = nc.vector

            def inverse_std(norms, sums=None, between=lambda i: None):
                w = norms + (0 if sums is None else sums.shape[1])
                va, r, t = var_e[:, 0:w], rstd[:, 0:w], nwt[:, 0:w]
                at = [0]

                def chain(ins):
                    land(ins, lambda: between(at[0]))
                    at[0] += 1
                if norms:
                    st = stats[:, 0:norms]
                    v.tensor_tensor(mean[:, 0:norms], st[:, :, 1], st[:, :, 4], ALU.add)
                    v.tensor_tensor(var_e[:, 0:norms], st[:, :, 2], st[:, :, 5], ALU.add)
                    chain(v.tensor_tensor(gap[:, 0:norms], st[:, :, 1], st[:, :, 4], ALU.subtract))
                    chain(v.tensor_tensor(gap[:, 0:norms], gap[:, 0:norms], gap[:, 0:norms], ALU.mult))
                    chain(v.scalar_tensor_tensor(out=var_e[:, 0:norms], in0=gap[:, 0:norms], scalar=D / 4.0,
                                                 in1=var_e[:, 0:norms], op0=ALU.mult, op1=ALU.add))
                    v.tensor_scalar(mean[:, 0:norms], mean[:, 0:norms], 0.5, None, ALU.mult)
                if sums is not None:
                    if norms:
                        v.tensor_scalar(var_e[:, 0:norms], var_e[:, 0:norms], 1.0 / D, EPS, ALU.mult, ALU.add)
                    chain(v.tensor_scalar(var_e[:, norms:w], sums, 1.0 / D, EPS, ALU.mult, ALU.add))
                else:
                    chain(v.tensor_scalar(va, va, 1.0 / D, EPS, ALU.mult, ALU.add))
                chain(v.tensor_scalar(r.bitcast(i32), va.bitcast(i32), 1, None, ALU.arith_shift_right))
                chain(v.tensor_scalar(r.bitcast(i32), r.bitcast(i32), -1.0, RSQRT_SEED, ALU.mult, ALU.add))
                for _ in range(3):
                    chain(v.scalar_tensor_tensor(out=t, in0=r, scalar=-0.5, in1=r, op0=ALU.mult, op1=ALU.mult))
                    chain(v.tensor_tensor(t, t, va, ALU.mult))
                    chain(v.scalar_tensor_tensor(out=r, in0=t, scalar=1.5, in1=r, op0=ALU.add, op1=ALU.mult))

            def h_norm(first, pair, done, keep=None):
                scale = h_scale[:, pair, :]
                if keep is None:
                    land(v.tensor_copy(scale, rstd[:, first:first + TILE_GROUP]))
                else:
                    land(v.tensor_tensor(scale, rstd[:, first:first + TILE_GROUP], keep, ALU.mult))
                signal(v.scalar_tensor_tensor(out=h_shift[:, pair, :], in0=mean[:, first:first + TILE_GROUP],
                                              scalar=-1.0, in1=scale, op0=ALU.mult, op1=ALU.mult), done)

            def measure(first, tiles):
                for i, src in enumerate(tiles):
                    last = v.bn_stats(stats[:, first + i, :], src)
                land(last)

            def normalize(first, tiles, done):
                for i, (dst, src) in enumerate(tiles):
                    k = first + i
                    last = v.tensor_scalar(dst, src, mean[:, k:k + 1], rstd[:, k:k + 1], ALU.subtract, ALU.mult)
                signal(last, done)

            def shift_x(done):
                signal(v.scalar_tensor_tensor(out=x_shift[:], in0=mean[:, 0:TILE_GROUP], scalar=-1.0,
                                              in1=rstd[:, 0:TILE_GROUP], op0=ALU.mult, op1=ALU.mult), done)

            def scale_shift(y, tiles, first_r, read, done):
                for t, src in enumerate(tiles):
                    last = v.scalar_tensor_tensor(out=y[:, t, :], in0=src,
                                                  scalar=rstd[:, first_r + t:first_r + t + 1], in1=gamma_bc[:],
                                                  op0=ALU.mult, op1=ALU.mult)
                signal(last, read)
                signal(v.tensor_tensor(y, y, beta_bc[:].unsqueeze(1).to_broadcast([P, len(tiles), D]), ALU.add), done)

            signal(v.memset(att_sb[:], 0.0), att_zero)
            land(v.memset(w_att[:], 0.0))
            signal(v.memset(pos_none.bitcast(i32), E_PAD), pos_fill)
            signal(v.memset(y_sb[0][:], 0.0), zero_rows)
            land(v.memset(bias_rows[:], 0.0))
            land(v.memset(bias_ones[:], 0.0))
            for row in (0, 32, 64):
                land(v.memset(bias_ones[row:row + 1, :], 1.0))
            dve.wait_ge(loaded, 16 * LOADS - 16)
            land(v.tensor_copy(sel_bf[:], sel[:]))
            land(v.tensor_copy(ident_bf[:], ident[:]))
            land(v.tensor_scalar(middle[:], ident[:], -1.0 / D, None, ALU.add))
            land(v.tensor_reduce(row_mean[:, 0:1], w_sb[:], AX.X, ALU.add))
            land(v.tensor_reduce(row_mean[:, 1:2], bias_bc[:], AX.X, ALU.add))
            land(v.tensor_scalar(row_mean[:], row_mean[:], 1.0 / D, None, ALU.mult))
            land(v.tensor_scalar(w_mid[:], w_sb[:], row_mean[:, 0:1], None, ALU.subtract))
            land(v.tensor_scalar(bias_bc[:], bias_bc[:], row_mean[:, 1:2], None, ALU.subtract))
            for row in (0, 32, 64):
                part = bias_rows[row:row + 1, :, :]
                land(v.tensor_copy(part, bias_bc[row:row + 1, :].unsqueeze(1).to_broadcast([1, TILE_GROUP, D])))
                for below in range(row + 32, 65, 32):
                    land(v.tensor_copy(t_sb[below:below + 1, 0:D], bias_bc[below:below + 1, :]))
                    land(v.tensor_copy(z_bf[below:below + 1, :], bias_bc[below:below + 1, :]))
                    land(v.tensor_tensor(bias_bc[below:below + 1, :], t_sb[below:below + 1, 0:D],
                                         z_bf[below:below + 1, :], ALU.subtract))
            land(v.memset(bias_wide[:], 0.0))
            land(v.tensor_copy(bias_wide[:, :, 0:D], bias_rows[:, 0:2, :]))
            land(v.tensor_tensor(v_bias[:], bn_sb[:], be_sb[:], ALU.add))
            land(v.tensor_tensor(inner_t[:], next_i[:], dst_i[:], ALU.is_equal))
            land(v.tensor_scalar(last_t[:], inner_t[:], -1.0, 1.0, ALU.mult, ALU.add))
            land(v.scalar_tensor_tensor(out=put_i[:], in0=inner_t[:], scalar=float(SKIP), in1=dst_i[:],
                                        op0=ALU.mult, op1=ALU.add))
            signal(v.tensor_scalar(recv_i[:], dst_i[:], float(N - 1), None, ALU.min), index_ready)
            land(v.tensor_tensor(same_l[:], prev_l[:], dst_l[:], ALU.is_equal))
            land(v.tensor_scalar(pen_l[:], same_l[:], -1.0, -NONE, ALU.add, ALU.mult))
            land(v.tensor_tensor(last_l[:], next_l[:], dst_l[:], ALU.not_equal))
            land(v.tensor_reduce(whole_l[:], same_l[:], AX.X, ALU.min))
            dve.wait_ge(wT_done, 1)
            signal(v.tensor_copy(wT[:], tile_of(0, 0)), wT_copied)
            dve.wait_ge(watt_done, 1)
            H = HEADS
            land(v.tensor_copy(w_att[:, 0:H], bank[1][:, 0:H]))
            land(v.tensor_copy(w_att[:, 2 * H:4 * H], bank[1][:, 0:2 * H]))
            land(v.tensor_copy(w_att[:, 2 * H:3 * H], bank[1][:, H:2 * H]))
            land(v.tensor_tensor(w_att[:, 3 * H:4 * H], w_att[:, 0:H], w_att[:, 2 * H:3 * H], ALU.add))
            land(v.tensor_copy(w_wide[:, 0:D], w_mid[:]))
            land(v.tensor_copy(w_wide[:, D:D + 2 * H], w_att[:, 0:2 * H]))
            dve.sem_inc(weights_ready, 1)
            dve.wait_ge(zeroed, 32)
            settle()

            def node_scale(n, slot, use, first_r):
                dve.wait_ge(nn_stored[slot], 16 * (use + 1))
                scale_shift(node_y[slot], node_tiles(slot % 2), first_r, nn_read, nn_y)

            def node_turn(n, slot, use, earlier=3, later=True):
                back2, ahead = (slot - 2) % NODE_RING, (slot + 1) % NODE_RING

                def between(i):
                    if 4 <= i < 4 + ROWS and later:
                        v.bn_stats(stats[:, i - 4, :], node_x[ahead][:, i - 4, :])
                if later:
                    dve.wait_ge(nx_in[ahead], 16 * (use + (2 if slot == NODE_RING - 1 else 1)))
                if earlier >= 1:
                    dve.wait_ge(nn_norm_act, n)
                if earlier >= 2:
                    dve.wait_ge(nn_sq, n - 1)
                inverse_std(ROWS, squares[:, slot % 2, :] if earlier >= 2 else None, between=between)
                shift_x(nn_std)
                if earlier >= 1:
                    dve.wait_ge(nn_T, n)
                normalize(TILE_GROUP, [(xn[:, t, :], node_x[slot][:, t, :]) for t in range(TILE_GROUP, ROWS)],
                          nn_norm)
                if earlier >= 2:
                    node_scale(n - 2, back2, use - (1 if slot < 2 else 0), ROWS)
                settle()
            dve.wait_ge(nx_in[0], 16)
            measure(0, [node_x[0][:, t, :] for t in range(ROWS)])
            settle()
            for n in range(3):
                node_turn(n, n, 0, n)
            visits(dve, 3, BLOCKS - 1, NODE_RING, node_turn)
            n = BLOCKS - 1
            node_turn(n, n % NODE_RING, n // NODE_RING, later=False)
            dve.wait_ge(nn_norm_act, BLOCKS)
            for m in (n - 1, n):
                dve.wait_ge(nn_sq, m + 1)
                inverse_std(0, squares[:, m % 2, :])
                node_scale(m, m % NODE_RING, m // NODE_RING, 0)
                settle()

            G = TILE_GROUP

            def tiles_of(a):
                return [a[:, t, :] for t in range(G)]

            def l_x1_waits(n, first=False):
                dve.wait_ge(l_gelu, n + 1)
                if not first:
                    dve.wait_ge(l_own, n - 1)

            def l_x1_part(i, slot):
                pair = slot % 2
                if i == 0:
                    v.tensor_tensor(x1_sb[pair][:], y_sb[pair][:], ring_a[slot], ALU.add).then_inc(l_x1_done, 1)
                elif 3 <= i < 3 + G:
                    v.bn_stats(stats[:, 2 * G + i - 3, :], x1_sb[pair][:, i - 3, :])

            def l_x1_alone(n, slot):
                l_x1_waits(n)
                for i in range(3 + G):
                    l_x1_part(i, slot)
                    land(v.memset(h_junk[:], 0.0))

            def l_scale(n, pair, first_r):
                scale_shift(y_sb[pair][:], [wide_tile(pair, t)[:, 0:D] for t in range(G)], first_r, l_read, l_y)

            def l_apply_x1(n, pair, pair_use):
                dve.wait_ge(own_stored[pair], 16 * (pair_use + 1))
                h_norm(2 * G, pair, l_n)

            def l_turn(n, slot, use, earlier=5, later=True):
                pair, pair_use = of_two(slot, use)
                ahead, back = (slot + 1) % X_RING, (slot - 3) % X_RING

                def between(i):
                    t = i - 1 if i < 7 else i - 2
                    if later and t in range(2 * G) and i != 7:
                        v.bn_stats(stats[:, t, :], (tiles_of(ring_a[ahead]) + tiles_of(ring_b[ahead % 3]))[t])
                    if earlier >= 3 and i >= 7:
                        if i == 7:
                            l_x1_waits(n - 3, earlier < 5)
                        l_x1_part(i - 7, back)
                if later:
                    ahead_use = use + (1 if slot == X_RING - 1 else 0)
                    dve.wait_ge(xs_in[ahead], 64 * (ahead_use + 1))
                    dve.wait_ge(xd_in[ahead % 3], 64 * (of_three(ahead, ahead_use)[1] + 1))
                if earlier >= 1:
                    dve.wait_ge(l_norm_act, n)
                if earlier >= 2:
                    dve.wait_ge(l_sq, n - 1)
                norms = 3 * G if earlier >= 4 else 2 * G
                inverse_std(norms, squares[:, pair, 0:G] if earlier >= 2 else None, between=between)
                shift_x(l_std)
                if earlier >= 1:
                    dve.wait_ge(l_T, n)
                normalize(G, [(xn[:, G + t, :], src) for t, src in enumerate(tiles_of(ring_b[slot % 3]))], l_norm)
                if earlier >= 2:
                    l_scale(n - 2, pair, norms)
                if earlier >= 4:
                    l_apply_x1(n - 4, pair, pair_use - 2)
                settle()
            dve.wait_ge(xs_in[0], 64)
            dve.wait_ge(xd_in[0], 64)
            measure(0, tiles_of(ring_a[0]) + tiles_of(ring_b[0]))
            settle()
            for n in range(5):
                l_turn(n, n, 0, n)
            visits(dve, 5, CHUNKS - 1, X_RING, l_turn)
            n = CHUNKS - 1
            l_turn(n, n % X_RING, n // X_RING, later=False)
            dve.wait_ge(l_norm_act, CHUNKS)
            for m in range(CHUNKS, CHUNKS + 4):
                if m < CHUNKS + 2:
                    dve.wait_ge(l_sq, m - 1)
                    inverse_std(3 * G, squares[:, m % 2, 0:G])
                    l_scale(m - 2, m % 2, 3 * G)
                else:
                    inverse_std(3 * G)
                l_apply_x1(m - 4, m % 2, (m - 4) // 2)
                if m < CHUNKS + 3:
                    l_x1_alone(m - 3, (m - 3) % X_RING)
                settle()

            dve.wait_ge(pos_ready, 1)
            none = coef[:, :, 0]
            land(v.tensor_scalar(none, pos_i[:], float(E_PAD), None, ALU.is_ge))
            land(v.tensor_tensor(none, none, edge_i[:], ALU.mult))
            land(v.tensor_tensor(hop1_i[:], none, pos_i[:], ALU.add))
            dve.sem_inc(hop1_ready, 1)

            def softmax(run, heads):
                K = heads * HALVES
                SK = 2 * K if run == 0 else K

                def lines_bc(a):
                    return a[:].unsqueeze(1).to_broadcast([LINES, heads, HALVES, P])

                def by_head(a):
                    return a[:, 0:K].rearrange("l (h f) e -> l h f e", f=HALVES)

                dve.wait_ge(p2["lines"], run + 1)
                for b in range(-(-SK // 4)):
                    w = min(4, SK - 4 * b)
                    land(v.tensor_copy(SL[:, 4 * b:4 * b + w, :],
                                       bank[b][0:LINES, 0:w * P].rearrange("l (k e) -> l k e", e=P)))
                if run == 0:
                    land(v.scalar_tensor_tensor(out=SL[:], in0=SL[:], scalar=SLOPE, in1=SL[:],
                                                op0=ALU.mult, op1=ALU.max))
                for k in range(K):
                    last = v.tensor_tensor_scan(ML[:, k, :], pen_l[:, k % 2, :], SL[:, k, :], NONE, ALU.add, ALU.max)
                signal(last, p2["local"])
                dve.wait_ge(p2["rows"], run + 1)
                land(v.tensor_copy(row_f[0:heads], bank[4][0:heads, 0:TILES]))
                land(v.tensor_copy(row_w[0:heads], bank[4][0:heads, TILES:2 * TILES]))
                land(v.tensor_scalar(row_pen[0:heads], row_w[0:heads], -1.0, -NONE, ALU.add, ALU.mult))
                land(v.memset(opened[0:heads, 0:1], NONE))
                land(v.tensor_tensor_scan(opened[0:heads, 1:TILES + 1], row_pen[0:heads], row_f[0:heads], NONE,
                                          ALU.add, ALU.max))
                land(v.tensor_tensor(row_a[0:heads], opened[0:heads, 0:TILES], opened[0:heads, 1:TILES + 1],
                                     ALU.subtract))
                land(v.tensor_scalar(row_a[0:heads], row_a[0:heads], 0.0, None, ALU.min))
                dve.sem_inc(p2["opened"], 1)
                dve.wait_ge(p2["carried"], run + 1)
                land(v.tensor_copy(carry_l[:, 0:K], bank[5][0:LINES, 0:K]))
                for k in range(K):
                    h, f = k // 2, k % 2
                    last = v.tensor_tensor_scan(ML[:, k, :], pen_l[:, f, :], SL[:, k, :],
                                                carry_l[:, f * heads + h:f * heads + h + 1], ALU.add, ALU.max)
                land(last)
                for k in range(K):
                    h, f = k // 2, k % 2
                    last = v.tensor_copy(AL[:, k, 0:1], carry_l[:, f * heads + h:f * heads + h + 1])
                land(last)
                land(v.tensor_copy(AL[:, 0:K, 1:P], ML[:, 0:K, 0:P - 1]))
                land(v.tensor_tensor(AL[:, 0:K], AL[:, 0:K], ML[:, 0:K], ALU.subtract))
                land(v.tensor_scalar(AL[:, 0:K], AL[:, 0:K], 0.0, None, ALU.min))
                signal(v.tensor_tensor(PL[:, 0:K], SL[:, 0:K], ML[:, 0:K], ALU.subtract), p2["args"])
                dve.wait_ge(p2["exp"], run + 1)
                land(v.tensor_tensor(by_head(AL), by_head(AL), lines_bc(same_l), ALU.mult))
                land(v.tensor_tensor(row_a[0:heads], row_a[0:heads], row_w[0:heads], ALU.mult))
                for k in range(K):
                    last = v.tensor_tensor_scan(DL[:, k, :], AL[:, k, :], PL[:, k, :], 0.0, ALU.mult, ALU.add)
                signal(last, p2["den"])
                dve.wait_ge(p2["drows"], run + 1)
                land(v.tensor_copy(row_f[0:heads], bank[4][0:heads, 0:TILES]))
                land(v.memset(opened[0:heads, 0:1], 0.0))
                signal(v.tensor_tensor_scan(opened[0:heads, 1:TILES + 1], row_a[0:heads], row_f[0:heads], 0.0,
                                     ALU.mult, ALU.add), p2["dopened"])
                dve.wait_ge(p2["dcarried"], run + 1)
                land(v.tensor_copy(carry_l[:, 0:K], bank[5][0:LINES, 0:K]))
                for k in range(K):
                    h, f = k // 2, k % 2
                    last = v.tensor_tensor_scan(DL[:, k, :], AL[:, k, :], PL[:, k, :],
                                                carry_l[:, f * heads + h:f * heads + h + 1], ALU.mult, ALU.add)
                land(last)
                if run == 0:
                    land(v.tensor_tensor(C1[:], ML[:], C2, ALU.max))
                    land(v.tensor_tensor(C2, C2, C1[:], ALU.subtract))
                    signal(v.tensor_tensor(C1[:], ML[:], C1[:], ALU.subtract), p2["args2"])
                    dve.wait_ge(p2["exp2"], 1)
                    land(v.tensor_tensor(DL[:], DL[:], C1[:], ALU.mult))
                    land(v.tensor_tensor(DL[:], DL[:], C2, ALU.add))
                    land(v.tensor_scalar(DL[:], DL[:], 1e-16, None, ALU.add))
                    land(v.reciprocal(DL[:], DL[:]))
                    land(v.tensor_tensor(C1[:], C1[:], DL[:], ALU.mult))
                    signal(v.tensor_tensor(C2, C2, DL[:], ALU.mult), p2["coef"])
                else:
                    land(v.reciprocal(DL[:, 0:K], DL[:, 0:K]))
                    signal(v.tensor_tensor(by_head(C1), by_head(DL), lines_bc(last_l), ALU.mult), p2["coef"])
                dve.wait_ge(p2["back"], run + 1)
                parts = 4 if run == 0 else 3
                for q in range(parts):
                    for k in range(K):
                        h, f = k // 2, k % 2
                        b, at = 2 * q + k // 4, (k % 4) * P
                        last = v.tensor_copy(coef[:, f * LINES:(f + 1) * LINES, q * heads + h],
                                             bank[b][:, at:at + LINES])
                signal(last, p2["done"])
                settle()
            softmax(0, HEADS)

            def g_sum_part(i, n, pair, first=False):
                if i == 0:
                    v.tensor_tensor(pv[:], bank[2][:, :], V[:, bass.ts(n, CHUNK)], ALU.mult)
                elif i == 1:
                    v.tensor_tensor(own_sb[pair], bank[4][:, :], hd_out[pair], ALU.mult)
                elif i == 2:
                    start = 0.0 if first else run_sum[1 - pair][:, CHUNK - 1:CHUNK]
                    v.tensor_tensor_scan(run_sum[pair][:], bank[1][:, :], pv[:], start, ALU.mult, ALU.add)
                elif i == 4:
                    v.tensor_tensor(o_sb[pair], bank[3][:, :], run_sum[pair][:], ALU.mult)
                elif i == 6:
                    v.tensor_tensor(o_sb[pair], o_sb[pair], own_sb[pair], ALU.add).then_inc(g_o, 1)

            def g_sum_waits(n, pair, pair_use):
                dve.wait_ge(g_bc, n + 1)
                dve.wait_ge(gh_in[pair], 16 * (pair_use + 1))
                dve.sem_inc(vector_seen, 1)

            def g_x1_waits(n, slot, use, first=False):
                pair, pair_use = of_two(slot, use)
                dve.wait_ge(g_gelu, n + 1)
                dve.wait_ge(gx_in[slot], 16 * (use + 1))
                dve.wait_ge(x1_stored[pair], 16 * (pair_use + 1))
                if not first:
                    dve.wait_ge(g_h, n - 1)

            def g_x1_part(i, slot):
                pair = slot % 2
                if i == 0:
                    v.tensor_tensor(x1_sb[pair][:], y_sb[pair][:], ring_a[slot], ALU.add).then_inc(g_x1, 1)
                elif 2 <= i < 2 + G:
                    v.bn_stats(stats[:, i - 2, :], x1_sb[pair][:, i - 2, :])

            def g_x1_alone(n, slot, use):
                g_x1_waits(n, slot, use)
                for i in range(2 + G):
                    g_x1_part(i, slot)
                    land(v.memset(var_e[:, 0:1], 0.0))

            def g_scale(n, pair, first_r):
                scale_shift(y_sb[pair][:], [tile_of(SUM_BANKS[pair], t) for t in range(G)], first_r, g_read, g_y)

            def g_apply_x1(n, pair, pair_use):
                dve.wait_ge(h1_stored[pair], 16 * (pair_use + 1))
                h_norm(0, pair, g_n, keep=last_t[:, bass.ts(n, TILE_GROUP)])

            def g_turn(n, slot, use, earlier=4):
                pair, pair_use = of_two(slot, use)

                def between(i):
                    g_sum_part(i, n, pair)
                    if i == 7 and earlier >= 2:
                        g_x1_waits(n - 2, (slot - 2) % X_RING, use - (1 if slot < 2 else 0), earlier < 4)
                    if i >= 7 and earlier >= 2:
                        g_x1_part(i - 7, (slot - 2) % X_RING)
                dve.wait_ge(g_sq, n)
                g_sum_waits(n, pair, pair_use)
                inverse_std(G if earlier >= 3 else 0, squares[:, 1 - pair, 0:G], between=between)
                if earlier == 2:
                    g_x1_part(1 + G, (slot - 2) % X_RING)
                g_scale(n - 1, 1 - pair, G if earlier >= 3 else 0)
                if earlier >= 3:
                    g_apply_x1(n - 3, 1 - pair, pair_use - (2 if pair == 0 else 1))
                settle()
            g_sum_waits(0, 0, 0)
            for i in range(7):
                g_sum_part(i, 0, 0, first=True)
                land(v.memset(var_e[:, 0:1], 0.0))
            settle()
            for n in range(1, 4):
                g_turn(n, n, 0, n)
            visits(dve, 4, CHUNKS, X_RING, g_turn)
            n = CHUNKS
            dve.wait_ge(g_sq, n)
            inverse_std(G, squares[:, 1, 0:G])
            g_scale(n - 1, 1, G)
            g_apply_x1(n - 3, 1, CHUNKS // 2 - 2)
            for m in (n - 2, n - 1):
                g_x1_alone(m, m % X_RING, m // X_RING)
                inverse_std(G)
                g_apply_x1(m, m % 2, m // 2)
                settle()

            for hop in range(HOPS):
                base, uses = hop * CHUNKS, hop * CHUNKS // 2

                def h_query(n, slot, first=False):
                    dve.wait_ge(h_T, base + n + 1)
                    dve.sem_inc(vector_seen, 1)
                    start = 0.0 if first else run_sum[1 - slot][:, 0:1]
                    signal(v.tensor_tensor_scan(run_sum[slot][:, ::-1], bank[HOP_BANKS[slot] + 2][:, ::-1],
                                         V[:, bass.ts(CHUNKS - 1 - n, CHUNK)], start,
                                         ALU.mult, ALU.add), h_q)

                def h_leaky(n, slot, first=False):
                    if not first:
                        dve.wait_ge(h_sc, base + n - 1)
                        dve.sem_inc(vector_seen, 1)
                    dve.wait_ge(h_vs, base + n + 1)
                    dve.sem_inc(vector_seen, 1)
                    land(v.scalar_tensor_tensor(out=t_sb[:], in0=run_sum[slot][:], scalar=bq_sb[:, hop:hop + 1],
                                                in1=V[:, bass.ts(CHUNKS - 1 - n, CHUNK)], op0=ALU.add, op1=ALU.add))
                    signal(v.scalar_tensor_tensor(out=o_sb[slot], in0=t_sb[:], scalar=SLOPE, in1=t_sb[:],
                                                  op0=ALU.mult, op1=ALU.max), h_z)

                def h_turn(n, slot, use):
                    h_query(n, slot)
                    h_leaky(n - 1, 1 - slot)
                    settle()
                h_query(0, 0, first=True)
                for n in (1, 2):
                    h_query(n, n % 2)
                    h_leaky(n - 1, 1 - n % 2, first=True)
                settle()
                visits(dve, 3, CHUNKS, 2, h_turn)
                h_leaky(CHUNKS - 1, 1)
                settle()
                softmax(hop + 1, 1)

                def k_sum(n, slot, first=False):
                    b = K_BANKS[slot]
                    dve.wait_ge(k_bc, base + n + 1)
                    land(v.tensor_tensor(pv[:], bank[b + 1][:, :], V[:, bass.ts(n, CHUNK)], ALU.mult))
                    start = 0.0 if first else run_sum[1 - slot][:, CHUNK - 1:CHUNK]
                    land(v.tensor_tensor_scan(run_sum[slot][:], bank[b][:, :], pv[:], start, ALU.mult, ALU.add))
                    v.scalar_tensor_tensor(out=o_sb[slot][:], in0=run_sum[slot][:], scalar=0.0,
                                           in1=bank[b + 2][:, :], op0=ALU.max, op1=ALU.mult).then_inc(k_h, 1)

                def k_final(n, slot, use):
                    dve.wait_ge(k_T, base + n + 1)
                    dve.wait_ge(x1_in[slot], 16 * (use + 1))
                    signal(v.tensor_tensor(h_sb[slot][:], rows_of(ROW_BANKS[slot]), x1_sb[slot][:], ALU.add), k_done)

                def k_turn(n, slot, use):
                    k_sum(n, slot)
                    if hop == HOPS - 1:
                        s, u = prev(slot, use)
                        dve.wait_ge(put_done[s], 64 * u)
                        k_final(n - 1, s, u)
                    settle()
                k_sum(0, 0, first=True)
                settle()
                if hop < HOPS - 1:
                    visits(dve, 1, CHUNKS, 2, k_turn)
                    continue
                for n in (1, 2):
                    k_sum(n, n % 2)
                    k_final(n - 1, (n - 1) % 2, 0)
                    settle()
                visits(dve, 3, CHUNKS, 2, k_turn)
                dve.wait_ge(put_done[1], 64 * (CHUNKS // 2 - 1))
                k_final(CHUNKS - 1, 1, CHUNKS // 2 - 1)

        @block.tensor
        def _(pe):
            def mm(dst, lhsT, rhs, start=True, stop=True):
                return nc.tensor.matmul(dst, lhsT, rhs, start=start, stop=stop)

            def tr(dst, src):
                k = src.shape[0]
                return nc.tensor.transpose(dst, src, ident[0:k, 0:k])

            pe.wait_ge(loaded, 16 * LOADS - 16)
            pe.wait_ge(att_loaded, 16 * 2 * HEADS)
            tr(tile_of(0, 0), w_sb[:]).then_inc(wT_done, 1)
            pe.wait_ge(wT_copied, 1)
            mm(bank[1][:, 0:2 * HEADS], wT[:], att_sb[:]).then_inc(watt_done, 1)
            pe.wait_ge(weights_ready, 1)

            def add_bias(b):
                mm(bank[b][:, :], bias_ones[:], bias_rows[:].rearrange("k t d -> k (t d)"), True, False)

            def node(n, slot, use, earlier=2):
                pe.wait_ge(nn_norm, n + 1)
                pe.wait_ge(nn_norm_act, n + 1)
                for t in range(ROWS):
                    last = tr(tile_of(t // TILE_GROUP, t % TILE_GROUP), xn[:, t, :])
                last.then_inc(nn_T, 1)
                if earlier >= 2:
                    pe.wait_ge(nn_read, n - 1)
                b = 2 + 2 * (slot % 2)
                for g in range(2):
                    add_bias(b + g)
                for g, relu in enumerate((aT, bT)):
                    pe.wait_ge(nn_relu, 2 * n + 1 + g)
                    for t in range(TILE_GROUP):
                        last = mm(tile_of(b + g, t), relu[:, t * P:(t + 1) * P], w_mid[:], False,
                                  t == TILE_GROUP - 1)
                last.then_inc(nn_h, 1)
            node(0, 0, 0, 0)
            node(1, 1, 0, 1)
            visits(pe, 2, BLOCKS, 2, node)

            def l_values(n, par):
                mm(bank[2][:, :], w_sb[:], relus[par][0][:])
                mm(bank[3][:, :], w_sb[:], relus[par][1][:]).then_inc(l_h, 1)

            def l_visit(n, slot, use, earlier=2):
                pe.wait_ge(l_norm, n + 1)
                pe.wait_ge(l_norm_act, n + 1)
                for t in range(2 * TILE_GROUP):
                    last = tr(tile_of(t // TILE_GROUP, t % TILE_GROUP), xn[:, t, :])
                last.then_inc(l_T, 1)
                if earlier >= 2:
                    pe.wait_ge(l_hd, n - 1)
                if earlier >= 1:
                    l_values(n - 1, 1 - slot)
                if earlier >= 2:
                    pe.wait_ge(l_read, n - 1)
                K = 2 * HEADS
                for g in range(2):
                    mm(bank[4 + 2 * slot + g][:, 0:2 * (D + K)], bias_ones[:],
                       bias_wide[:].rearrange("k t d -> k (t d)"), True, False)
                pe.wait_ge(l_relu, n + 1)
                for t in range(TILE_GROUP):
                    a, b = (r[:, t * P:(t + 1) * P] for r in relus[slot])
                    mm(wide_tile(slot, t), a, w_wide[:], False, False)
                    last = mm(wide_tile(slot, t)[:, D:D + K], b, w_att[:, K:2 * K], False, t % 2 == 1)
                last.then_inc(l_p, 1)
            l_visit(0, 0, 0, 0)
            l_visit(1, 1, 0, 1)
            visits(pe, 2, CHUNKS, 2, l_visit)
            pe.wait_ge(l_hd, CHUNKS - 1)
            l_values(CHUNKS - 1, 1)

            def softmax(run, heads):
                K = heads * HALVES
                SK = 2 * K if run == 0 else K
                for k in range(SK):
                    f = k % 2
                    last = tr(bank[k // 4][0:LINES, (k % 4) * P:(k % 4 + 1) * P],
                              scores[:, f * LINES:(f + 1) * LINES, k // 2])
                last.then_inc(p2["lines"], 1)
                pe.wait_ge(p2["local"], run + 1)
                for f in range(HALVES):
                    tr(bank[4][0:heads, f * LINES:(f + 1) * LINES], ML[:, f:K:HALVES, P - 1])
                    last = tr(bank[4][0:heads, TILES + f * LINES:TILES + (f + 1) * LINES],
                              whole_l[:, f:f + 1].to_broadcast([LINES, heads]))
                last.then_inc(p2["rows"], 1)
                pe.wait_ge(p2["opened"], run + 1)
                for f in range(HALVES):
                    last = tr(bank[5][0:LINES, f * heads:(f + 1) * heads],
                              opened[0:heads, f * LINES:(f + 1) * LINES])
                last.then_inc(p2["carried"], 1)
                pe.wait_ge(p2["den"], run + 1)
                for f in range(HALVES):
                    last = tr(bank[4][0:heads, f * LINES:(f + 1) * LINES], DL[:, f:K:HALVES, P - 1])
                last.then_inc(p2["drows"], 1)
                pe.wait_ge(p2["dopened"], run + 1)
                for f in range(HALVES):
                    last = tr(bank[5][0:LINES, f * heads:(f + 1) * heads],
                              opened[0:heads, f * LINES:(f + 1) * LINES])
                last.then_inc(p2["dcarried"], 1)
                pe.wait_ge(p2["coef"], run + 1)
                for q, src in enumerate((AL, PL, C1, C2)[:4 if run == 0 else 3]):
                    for k in range(K):
                        last = tr(bank[2 * q + k // 4][:, (k % 4) * P:(k % 4) * P + LINES], src[:, k, :])
                last.then_inc(p2["back"], 1)
                pe.wait_ge(p2["done"], run + 1)
            pe.wait_ge(l_hd, CHUNKS)
            pe.wait_ge(l_n, CHUNKS)
            softmax(0, HEADS)

            def g_coefs(n, slot):
                pe.wait_ge(g_staged, n + 1)
                for t in range(TILE_GROUP):
                    last = mm(bank[0][0:PARTS * 4 * HEADS, t * P:(t + 1) * P], coef_parts[slot][:, t, :], ident_bf[:])
                last.then_inc(g_cT, 1)

            def g_bcast(n, first=False):
                pe.wait_ge(g_cTs, n + 1)
                if not first:
                    pe.wait_ge(g_o, n)
                for q in range(4):
                    last = mm(bank[1 + q][:, :], sel_bf[:, q, :], coefT_bf[:])
                last.then_inc(g_bc, 1)

            def g_project(n, slot, first=False):
                if not first:
                    pe.wait_ge(g_read, n - 1)
                add_bias(SUM_BANKS[slot])
                pe.wait_ge(g_o, n + 1)
                for t in range(TILE_GROUP):
                    last = mm(tile_of(SUM_BANKS[slot], t), o_sb[slot][:, t * P:(t + 1) * P], middle[:], False,
                              t == TILE_GROUP - 1)
                last.then_inc(g_u, 1)

            def g_turned(n, slot):
                pe.wait_ge(g_h, n + 1)
                for t in range(TILE_GROUP):
                    last = tr(tile_of(6, t), h_sb[slot][:, t, :])
                last.then_inc(g_hT, 1)

            def g_query(n):
                pe.wait_ge(g_hTs, n + 1)
                mm(bank[6][:, :], wq_sb[:, 0, :], aT[:]).then_inc(g_q, 1)

            def g_turn(n, slot, use, earlier=5):
                g_coefs(n + 1, 1 - slot)
                if earlier >= 5:
                    pe.wait_ge(g_done, n - 4)
                if earlier >= 4:
                    g_turned(n - 4, slot)
                g_project(n, slot, first=earlier <= 1)
                g_bcast(n + 1)
                if earlier >= 4:
                    g_query(n - 4)
            g_coefs(0, 0)
            g_bcast(0, first=True)
            for n in range(5):
                g_turn(n, n % 2, 0, n)
            visits(pe, 5, CHUNKS - 1, 2, g_turn)
            n = CHUNKS - 1
            g_project(n, 1)
            for m in range(n - 4, n + 1):
                pe.wait_ge(g_done, m)
                g_turned(m, m % 2)
                g_query(m)

            for hop in range(HOPS):
                base, uses = hop * CHUNKS, hop * CHUNKS // 2
                if hop:
                    pe.wait_ge(k_done, base)
                else:
                    pe.wait_ge(g_done, CHUNKS)

                def h_turned(n, slot, use, first=False):
                    pe.wait_ge(hs_in[slot], 64 * (uses + use + 1))
                    pe.wait_ge(ea_in[slot], 32 * (uses + use + 1))
                    pe.wait_ge(h_staged, base + n + 1)
                    if not first:
                        pe.wait_ge(h_q, base + n - 1)
                    b = HOP_BANKS[slot]
                    for t in range(TILE_GROUP):
                        tr(tile_of(b, t), ring_a[slot][:, t, :])
                        tr(tile_of(b + 1, t), ring_b[slot][:, t, :])
                        last = tr(tile_of(b + 2, t), coef_st[slot][:, t, 0:1].to_broadcast([P, P]))
                    last.then_inc(h_T, 1)

                def h_values(n, slot, first=False):
                    pe.wait_ge(h_Ts, base + n + 1)
                    if not first:
                        pe.wait_ge(h_vs, base + n)
                    mm(bank[3][:, :], wn_sb[:, hop, :], turned[slot][0][:], True, False)
                    mm(bank[3][:, :], we_sb[:, hop, :], turned[slot][1][:], False, True).then_inc(h_v, 1)

                def h_score(n, slot, first=False):
                    if not first:
                        pe.wait_ge(h_scs, base + n)
                    pe.wait_ge(h_z, base + n + 1)
                    for t in range(TILE_GROUP):
                        last = mm(bank[4][:, t:t + 1], o_sb[slot][:, t * P:(t + 1) * P], attn_sb[:, hop:hop + 1])
                    last.then_inc(h_sc, 1)

                def h_turn(n, slot, use, first=False):
                    h_turned(n, slot, use)
                    h_values(n - 1, 1 - slot)
                    h_score(n - 2, slot, first)
                h_turned(0, 0, 0, first=True)
                h_turned(1, 1, 0, first=True)
                h_values(0, 0, first=True)
                h_turn(2, 0, 1, first=True)
                visits(pe, 3, CHUNKS, 2, h_turn)
                h_values(CHUNKS - 1, 1)
                h_score(CHUNKS - 2, 0)
                h_score(CHUNKS - 1, 1)
                pe.wait_ge(h_scs, base + CHUNKS)
                softmax(hop + 1, 1)

                def k_bcast(n, slot, first=False):
                    pe.wait_ge(k_staged, base + n + 1)
                    if not first:
                        pe.wait_ge(k_h, base + n - 1)
                    for q in range(3):
                        for t in range(TILE_GROUP):
                            last = tr(tile_of(K_BANKS[slot] + q, t), coef_st[slot][:, t, q:q + 1].to_broadcast([P, P]))
                    last.then_inc(k_bc, 1)

                def k_rows(n, slot, first=False):
                    pe.wait_ge(k_h, base + n + 1)
                    last_hop = hop == HOPS - 1
                    if not first:
                        pe.wait_ge(k_done, base + n - (1 if last_hop else 0))
                    for t in range(TILE_GROUP):
                        last = tr(tile_of(ROW_BANKS[slot] if last_hop else 3, t), o_sb[slot][:, t * P:(t + 1) * P])
                    if hop < HOPS - 1:
                        last = mm(bank[7][:, :], wq_sb[:, hop + 1, :], o_sb[slot][:])
                    last.then_inc(k_T, 1)

                def k_turn(n, slot, use):
                    k_bcast(n, slot)
                    k_rows(n - 1, 1 - slot)
                k_bcast(0, 0, first=True)
                k_bcast(1, 1, first=True)
                k_rows(0, 0, first=True)
                visits(pe, 2, CHUNKS, 2, k_turn)
                k_rows(CHUNKS - 1, 1)


_SHAPES = ["x", "src_tiles", "dst_tiles", "next_tiles", "edge_ids", "dst_lines", "prev_lines", "next_lines",
           "edge_attr", "W", "att", "bias", "gamma", "beta", "Wq", "Wn", "We", "bq", "bn", "be", "attn",
           "ident", "sel"]


def kernel(**inputs):
    import numpy as _np
    import concourse.bacc as _bacc
    from concourse import mybir as _mybir
    from concourse.bass_utils import run_bass_kernel_spmd as _run

    given = {k: _np.asarray(v) for k, v in inputs.items()}

    def pad(a, value):
        return _np.concatenate([a, _np.full(E_PAD - a.shape[0], value, a.dtype)])

    def tiles(a):
        return a.reshape(TILES, P).T

    def lines(a):
        return a.reshape(HALVES, LINES, P).transpose(1, 0, 2)

    dst = pad(given["dst"], N)
    ends = _np.full(1, -1, dst.dtype)
    after, before = _np.concatenate([dst[1:], ends]), _np.concatenate([ends, dst[:-1]])
    sel = _np.zeros((PARTS, 4 * HEADS, 4, D), _np.float32)
    for q in range(4):
        for h in range(HEADS):
            sel[:, q * HEADS + h, q, h * D // HEADS:(h + 1) * D // HEADS] = 1
    data = {
        "x": given["x"], "src_tiles": tiles(pad(given["src"], 0)), "dst_tiles": tiles(dst),
        "next_tiles": tiles(after), "edge_ids": tiles(_np.arange(E_PAD, dtype=_np.int32)),
        "dst_lines": lines(dst), "prev_lines": lines(before), "next_lines": lines(after),
        "edge_attr": given["edge_attr_128"], "W": given["L0_gnn_W"],
        "att": _np.stack([given["L0_gnn_att_src"], given["L0_gnn_att_dst"]]),
        "bias": given["L0_gnn_bias"][None], "gamma": given["L0_gnn_gamma"][None], "beta": given["L0_gnn_beta"][None],
        "Wq": given["L1_gnn_Wq"], "Wn": given["L1_gnn_Wn"], "We": given["L1_gnn_We"],
        "bq": given["L1_gnn_bq"].T, "bn": given["L1_gnn_bn"].T, "be": given["L1_gnn_be"].T,
        "attn": given["L1_gnn_attn"].T, "ident": _np.eye(P, dtype=_np.float32),
        "sel": sel.reshape(PARTS * 4 * HEADS, 4, D),
    }
    nc = _bacc.Bacc("TRN2", target_bir_lowering=False, num_devices=1)
    arrays, args = {}, []
    for name in _SHAPES:
        a = _np.ascontiguousarray(data[name])
        arrays[f"in_{name}"] = a
        args.append(nc.dram_tensor(f"in_{name}", a.shape, _mybir.dt.from_np(a.dtype), kind="ExternalInput").ap())
    out = nc.dram_tensor("out_0", (N, D), _mybir.dt.float32, kind="ExternalOutput").ap()
    build(nc, *args, out)
    return _run(nc, [arrays], core_ids=[0]).results[0]["out_0"]
```
